# Optimizing a Trainium2 kernel written in Bass

```python
import numpy as np
import jax
import jax.numpy as jnp

def _softmax(x, axis=-1):
    return jax.nn.softmax(x, axis=axis)

def _gelu(x):
    return jax.nn.gelu(x, approximate=True)

def _silu(x):
    return jax.nn.silu(x)

def _sigmoid(x):
    return jax.nn.sigmoid(x)

def _layernorm(x, axis=-1, eps=1e-05):
    m = jnp.mean(x, axis=axis, keepdims=True)
    v = jnp.var(x, axis=axis, keepdims=True)
    return (x - m) / jnp.sqrt(v + eps)

def _scatter_add(tgt, idx, src, axis=0):
    return tgt.at[idx].add(src)

def _segment_sum(src, seg, n):
    return jax.ops.segment_sum(src, seg, n)
kernel_name = 'mk_gnn_preln_d4_gnn_r64_c60fce'

def setup_inputs(seed: int=0):
    np.random.seed(seed)
    _w = jnp.asarray

    def _rec_inputs():
        import jax
        import jax.numpy as jnp
        _gk = jax.random.key(seed)
        x = -0.0001006 + 1 * jax.random.normal(jax.random.fold_in(_gk, 1), (50000, 96), jnp.float32)
        src = jax.random.randint(jax.random.fold_in(_gk, 2), (12500,), 0, 50000, jnp.int32)
        dst = jnp.minimum((50000 * jax.random.uniform(jax.random.fold_in(_gk, 3), (12500,)) ** 2.0).astype(jnp.int32), 49999)
        _o = jnp.argsort(dst, stable=True)
        src = src[_o]
        dst = dst[_o]
        edge_attr_32 = 0.000196303 + 1.00016 * jax.random.normal(jax.random.fold_in(_gk, 12), (12500, 32), jnp.float32)
        edge_weight = jax.random.uniform(jax.random.fold_in(_gk, 14), (12500,), jnp.float32, 0.0, 0.999998)
        return (x, src, dst, edge_attr_32, edge_weight)
    x, src, dst, edge_attr_32, edge_weight = _rec_inputs()

    def _L0_gnn_setup():
        import jax, jax.numpy as jnp
        import numpy as np
        N = 50000
        E = 12500
        D = 96

        def gcn_conv(x, row, col, ew, W, b):
            n = x.shape[0]
            h = x @ W
            deg = jax.ops.segment_sum(ew, col, num_segments=n) + 1.0
            dinv = jnp.where(deg > 0, jax.lax.rsqrt(deg), 0.0)
            norm = dinv[row] * ew * dinv[col]
            agg = jax.ops.segment_sum(h[row] * norm[:, None], col, num_segments=n)
            agg = agg + h * (dinv * dinv)[:, None]
            return agg + b
        key = jax.random.key(seed)
        ks = jax.random.split(key, 8)
        x = jax.random.normal(ks[0], (N, D), dtype=jnp.float32)
        edge_index = jax.random.randint(ks[1], (2, E), 0, N, dtype=jnp.int32)
        edge_weight = jax.random.uniform(ks[2], (E,), dtype=jnp.float32)
        batch = jnp.zeros((N,), dtype=jnp.int32)
        s = 1.0 / np.sqrt(D)
        W1 = jax.random.normal(ks[3], (D, D), dtype=jnp.float32) * s
        b1 = jnp.zeros((D,), dtype=jnp.float32)
        W2 = jax.random.normal(ks[4], (D, D), dtype=jnp.float32) * s
        b2 = jnp.zeros((D,), dtype=jnp.float32)
        return {'x': x, 'edge_index': edge_index, 'edge_weight': edge_weight, 'batch': batch, 'W1': W1, 'b1': b1, 'W2': W2, 'b2': b2}
    _L0_gnn_all = _L0_gnn_setup()
    _L0_gnn_in = {k: v for k, v in _L0_gnn_all.items() if k in ('W1', 'b1', 'W2', 'b2')}
    del _L0_gnn_all

    def _L1_gnn_setup():
        import jax, jax.numpy as jnp
        import numpy as np
        N_NODES = 50000
        N_EDGES = 12500
        D_IN = 96
        D_HID = 96

        def _sage_conv(x, src, dst, Wl, b, Wr, n_nodes):
            msg = x[src]
            agg = jax.ops.segment_sum(msg, dst, num_segments=n_nodes)
            cnt = jax.ops.segment_sum(jnp.ones((src.shape[0],), x.dtype), dst, num_segments=n_nodes)
            agg = agg / jnp.maximum(cnt, 1.0)[:, None]
            return agg @ Wl.T + b + x @ Wr.T
        key = jax.random.key(seed)
        ks = jax.random.split(key, 8)
        x = jax.random.normal(ks[0], (N_NODES, D_IN), dtype=jnp.float32)
        edge_index = jax.random.randint(ks[1], (2, N_EDGES), 0, N_NODES, dtype=jnp.int64)
        s1 = 1.0 / np.sqrt(D_IN)
        s2 = 1.0 / np.sqrt(D_HID)
        W1l = jax.random.uniform(ks[2], (D_HID, D_IN), jnp.float32, -s1, s1)
        b1 = jax.random.uniform(ks[3], (D_HID,), jnp.float32, -s1, s1)
        W1r = jax.random.uniform(ks[4], (D_HID, D_IN), jnp.float32, -s1, s1)
        W2l = jax.random.uniform(ks[5], (D_HID, D_HID), jnp.float32, -s2, s2)
        b2 = jax.random.uniform(ks[6], (D_HID,), jnp.float32, -s2, s2)
        W2r = jax.random.uniform(ks[7], (D_HID, D_HID), jnp.float32, -s2, s2)
        return {'x': x, 'edge_index': edge_index, 'W1l': W1l, 'b1': b1, 'W1r': W1r, 'W2l': W2l, 'b2': b2, 'W2r': W2r}
    _L1_gnn_all = _L1_gnn_setup()
    _L1_gnn_in = {k: v for k, v in _L1_gnn_all.items() if k in ('W1l', 'b1', 'W1r', 'W2l', 'b2', 'W2r')}
    del _L1_gnn_all

    def _L2_gnn_setup():
        import jax, jax.numpy as jnp
        import numpy as np
        N, E = (50000, 12500)
        ND, ED = (96, 32)

        def _gelu(x):
            return jax.nn.gelu(x, approximate=False)
        key = jax.random.key(seed)
        ks = jax.random.split(key, 16)
        s = lambda fan_in: 1.0 / np.sqrt(fan_in)
        inp = {'x': jax.random.normal(ks[0], (N, ND), jnp.float32), 'edge_index': jax.random.randint(ks[1], (2, E), 0, N, jnp.int32), 'edge_attr': jax.random.normal(ks[2], (E, ED), jnp.float32), 'mW1': jax.random.uniform(ks[3], (ND + ED, ND), jnp.float32, -s(ND + ED), s(ND + ED)), 'mb1': jnp.zeros((ND,), jnp.float32), 'mW2': jax.random.uniform(ks[4], (ND, ND), jnp.float32, -s(ND), s(ND)), 'mb2': jnp.zeros((ND,), jnp.float32), 'gW1': jax.random.uniform(ks[5], (ND + ED, ND), jnp.float32, -s(ND + ED), s(ND + ED)), 'gb1': jnp.zeros((ND,), jnp.float32), 'gW2': jax.random.uniform(ks[6], (ND, 1), jnp.float32, -s(ND), s(ND)), 'gb2': jnp.zeros((1,), jnp.float32), 'uW1': jax.random.uniform(ks[7], (2 * ND, ND), jnp.float32, -s(2 * ND), s(2 * ND)), 'ub1': jnp.zeros((ND,), jnp.float32), 'uW2': jax.random.uniform(ks[8], (ND, ND), jnp.float32, -s(ND), s(ND)), 'ub2': jnp.zeros((ND,), jnp.float32), 'ln_g': jnp.ones((ND,), jnp.float32), 'ln_b': jnp.zeros((ND,), jnp.float32)}
        return inp
    _L2_gnn_all = _L2_gnn_setup()
    _L2_gnn_in = {k: v for k, v in _L2_gnn_all.items() if k in ('mW1', 'mb1', 'mW2', 'mb2', 'gW1', 'gb1', 'gW2', 'gb2', 'uW1', 'ub1', 'uW2', 'ub2', 'ln_g', 'ln_b')}
    del _L2_gnn_all

    def _L3_gnn_setup():
        import jax, jax.numpy as jnp
        import numpy as np
        K = 16
        ALPHA = 0.1
        key = jax.random.key(seed)
        k1, k2 = jax.random.split(key)
        N, E, D = (50000, 12500, 96)
        x = jax.random.normal(k1, (N, D), dtype=jnp.float32)
        edge_index = jax.random.randint(k2, (2, E), 0, N, dtype=jnp.int64)
        return {'x': x, 'edge_index': edge_index}
    _L3_gnn_all = _L3_gnn_setup()
    _L3_gnn_in = {k: v for k, v in _L3_gnn_all.items() if k in ()}
    del _L3_gnn_all
    return {'x': x, 'src': src, 'dst': dst, 'edge_attr_32': edge_attr_32, 'edge_weight': edge_weight, 'L0_gnn_W1': _L0_gnn_in['W1'], 'L0_gnn_b1': _L0_gnn_in['b1'], 'L0_gnn_W2': _L0_gnn_in['W2'], 'L0_gnn_b2': _L0_gnn_in['b2'], 'L1_gnn_W1l': _L1_gnn_in['W1l'], 'L1_gnn_b1': _L1_gnn_in['b1'], 'L1_gnn_W1r': _L1_gnn_in['W1r'], 'L1_gnn_W2l': _L1_gnn_in['W2l'], 'L1_gnn_b2': _L1_gnn_in['b2'], 'L1_gnn_W2r': _L1_gnn_in['W2r'], 'L2_gnn_mW1': _L2_gnn_in['mW1'], 'L2_gnn_mb1': _L2_gnn_in['mb1'], 'L2_gnn_mW2': _L2_gnn_in['mW2'], 'L2_gnn_mb2': _L2_gnn_in['mb2'], 'L2_gnn_gW1': _L2_gnn_in['gW1'], 'L2_gnn_gb1': _L2_gnn_in['gb1'], 'L2_gnn_gW2': _L2_gnn_in['gW2'], 'L2_gnn_gb2': _L2_gnn_in['gb2'], 'L2_gnn_uW1': _L2_gnn_in['uW1'], 'L2_gnn_ub1': _L2_gnn_in['ub1'], 'L2_gnn_uW2': _L2_gnn_in['uW2'], 'L2_gnn_ub2': _L2_gnn_in['ub2'], 'L2_gnn_ln_g': _L2_gnn_in['ln_g'], 'L2_gnn_ln_b': _L2_gnn_in['ln_b']}

def reference(x, src, dst, edge_attr_32, edge_weight, L0_gnn_W1, L0_gnn_b1, L0_gnn_W2, L0_gnn_b2, L1_gnn_W1l, L1_gnn_b1, L1_gnn_W1r, L1_gnn_W2l, L1_gnn_b2, L1_gnn_W2r, L2_gnn_mW1, L2_gnn_mb1, L2_gnn_mW2, L2_gnn_mb2, L2_gnn_gW1, L2_gnn_gb1, L2_gnn_gW2, L2_gnn_gb2, L2_gnn_uW1, L2_gnn_ub1, L2_gnn_uW2, L2_gnn_ub2, L2_gnn_ln_g, L2_gnn_ln_b):
    import jax
    import jax.numpy as jnp

    def _L0_gnn_ref(x, edge_index, edge_weight, batch, W1, b1, W2, b2):
        import jax, jax.numpy as jnp
        import numpy as np
        N = 50000
        E = 12500
        D = 96

        def gcn_conv(x, row, col, ew, W, b):
            n = x.shape[0]
            h = x @ W
            deg = jax.ops.segment_sum(ew, col, num_segments=n) + 1.0
            dinv = jnp.where(deg > 0, jax.lax.rsqrt(deg), 0.0)
            norm = dinv[row] * ew * dinv[col]
            agg = jax.ops.segment_sum(h[row] * norm[:, None], col, num_segments=n)
            agg = agg + h * (dinv * dinv)[:, None]
            return agg + b
        row, col = (edge_index[0], edge_index[1])
        h = jax.nn.relu(gcn_conv(x, row, col, edge_weight, W1, b1))
        h = jax.nn.relu(gcn_conv(h, row, col, edge_weight, W2, b2))
        return h

    def _L1_gnn_ref(x, edge_index, W1l, b1, W1r, W2l, b2, W2r):
        import jax, jax.numpy as jnp
        import numpy as np
        N_NODES = 50000
        N_EDGES = 12500
        D_IN = 96
        D_HID = 96

        def _sage_conv(x, src, dst, Wl, b, Wr, n_nodes):
            msg = x[src]
            agg = jax.ops.segment_sum(msg, dst, num_segments=n_nodes)
            cnt = jax.ops.segment_sum(jnp.ones((src.shape[0],), x.dtype), dst, num_segments=n_nodes)
            agg = agg / jnp.maximum(cnt, 1.0)[:, None]
            return agg @ Wl.T + b + x @ Wr.T
        src, dst = (edge_index[0], edge_index[1])
        n = x.shape[0]
        h = _sage_conv(x, src, dst, W1l, b1, W1r, n)
        h = jax.nn.elu(h)
        h = _sage_conv(h, src, dst, W2l, b2, W2r, n)
        return h

    def _L2_gnn_ref(x, edge_index, edge_attr, mW1, mb1, mW2, mb2, gW1, gb1, gW2, gb2, uW1, ub1, uW2, ub2, ln_g, ln_b):
        import jax, jax.numpy as jnp
        import numpy as np
        N, E = (50000, 12500)
        ND, ED = (96, 32)

        def _gelu(x):
            return jax.nn.gelu(x, approximate=False)
        src, dst = (edge_index[0], edge_index[1])
        edge_input = jnp.concatenate([x[src], edge_attr], axis=-1)
        messages = _gelu(edge_input @ mW1 + mb1) @ mW2 + mb2
        gates = jax.nn.sigmoid(_gelu(edge_input @ gW1 + gb1) @ gW2 + gb2)
        aggregated = jax.ops.segment_sum(messages * gates, dst, num_segments=x.shape[0])
        combined = jnp.concatenate([x, aggregated], axis=-1)
        update = _gelu(combined @ uW1 + ub1) @ uW2 + ub2
        h = x + update
        mu = jnp.mean(h, axis=-1, keepdims=True)
        var = jnp.mean(jnp.square(h - mu), axis=-1, keepdims=True)
        return (h - mu) * jax.lax.rsqrt(var + 1e-05) * ln_g + ln_b

    def _L3_gnn_ref(x, edge_index):
        import jax, jax.numpy as jnp
        import numpy as np
        K = 16
        ALPHA = 0.1
        N = x.shape[0]
        loop = jnp.arange(N, dtype=edge_index.dtype)
        row = jnp.concatenate([edge_index[0], loop])
        col = jnp.concatenate([edge_index[1], loop])
        deg = jax.ops.segment_sum(jnp.ones_like(col, dtype=x.dtype), col, num_segments=N)
        deg_inv_sqrt = jnp.where(deg > 0, jax.lax.rsqrt(jnp.maximum(deg, 1e-30)), 0.0)
        norm = (deg_inv_sqrt[row] * deg_inv_sqrt[col])[:, None]
        h = x
        for _ in range(K):
            h_neighbors = jax.ops.segment_sum(norm * h[row], col, num_segments=N)
            h = (1.0 - ALPHA) * h_neighbors + ALPHA * x
        return h
    edge_index = jnp.stack([src, dst])
    batch0 = jnp.zeros((50000,), jnp.int32)
    h = jnp.maximum(_layernorm(x, axis=-1), 0.0)
    x = x + _L0_gnn_ref(h, edge_index, edge_weight, batch0, L0_gnn_W1, L0_gnn_b1, L0_gnn_W2, L0_gnn_b2)
    h = jnp.maximum(_layernorm(x, axis=-1), 0.0)
    x = x + _L1_gnn_ref(h, edge_index, L1_gnn_W1l, L1_gnn_b1, L1_gnn_W1r, L1_gnn_W2l, L1_gnn_b2, L1_gnn_W2r)
    h = jnp.maximum(_layernorm(x, axis=-1), 0.0)
    x = x + _L2_gnn_ref(h, edge_index, edge_attr_32, L2_gnn_mW1, L2_gnn_mb1, L2_gnn_mW2, L2_gnn_mb2, L2_gnn_gW1, L2_gnn_gb1, L2_gnn_gW2, L2_gnn_gb2, L2_gnn_uW1, L2_gnn_ub1, L2_gnn_uW2, L2_gnn_ub2, L2_gnn_ln_g, L2_gnn_ln_b)
    h = jnp.maximum(_layernorm(x, axis=-1), 0.0)
    x = x + _L3_gnn_ref(h, edge_index)
    return x

_drawn_inputs = setup_inputs


def setup_inputs(seed=0):
    import zlib

    import numpy as np

    out = dict(_drawn_inputs(seed))
    spreads = {'L0_gnn_b1': (0.0, 0.1),
     'L0_gnn_b2': (0.0, 0.1),
     'L2_gnn_mb1': (0.0, 2.0),
     'L2_gnn_mb2': (0.0, 2.0),
     'L2_gnn_gb1': (0.0, 2.0),
     'L2_gnn_ub1': (0.0, 0.314),
     'L2_gnn_ub2': (0.0, 0.1),
     'L2_gnn_ln_g': (1.0, 0.2),
     'L2_gnn_ln_b': (0.0, 0.1)}
    factors = {'edge_attr_32': 8.0,
     'L2_gnn_mW1': 8.0,
     'L2_gnn_mW2': 8.0,
     'L2_gnn_gW1': 8.0,
     'L2_gnn_gW2': 8.0}
    for name, (base, spread) in spreads.items():
        noise = np.random.default_rng([zlib.crc32(name.encode()), seed]).standard_normal(out[name].shape)
        drawn = base * np.exp(spread * noise) if base else spread * noise
        out[name] = jnp.asarray(drawn.astype(out[name].dtype))
    for name, factor in factors.items():
        out[name] = (out[name] * factor).astype(out[name].dtype)
    return out
```

```python
import concourse.bass as bass
from concourse import mybir
from contextlib import ExitStack

F32 = mybir.dt.float32
I32 = mybir.dt.int32
ALU = mybir.AluOpType
ACT = mybir.ActivationFunctionType

P = 125
F = 96
FE = 32
NN = 50000
NE = 12500
T = NE // P
KT = 20
CH = 4
NC = KT // CH
EB = T // KT
NB = NN // P // KT
SLOTS = 20
STEPS = 16
ALPHA = 0.1
EPS = 1e-5
FAR = float(1 << 20)

WN = ["W1", "W2", "WR1", "WL1", "WR2", "WL2", "MW1", "MW2", "GW1", "UA", "UB", "UW2"]
WC = {n: i * F for i, n in enumerate(WN)}
GW2 = len(WN) * F
BC = {n: GW2 + 1 + i for i, n in enumerate(["b1", "s1", "mb", "gb", "ub"])}
WCOLS = GW2 + 6
ED = ["src", "dst", "nxt", "prv"]


def gnn_kernel(nc, x, edges, ew, dst_rows, attr, wts, lnp, ident_in, place, out):
    ctx = ExitStack()
    with ctx:
        def sb(name, shape, dt=F32):
            return ctx.enter_context(nc.sbuf_tensor(name, shape, dt))

        def sem(name):
            return ctx.enter_context(nc.semaphore(name))

        def dram(name, shape):
            return nc.dram_tensor(name, shape, F32).ap()

        V, A, PE = nc.vector, nc.scalar, nc.tensor

        EQ = sb("EQ", [P, T, P])
        XD = sb("XD", [P, T, F])
        HD = sb("HD", [P, T, F])
        M = sb("M", [P, SLOTS, F + FE])
        LX = [sb(f"LX{i}", [P, KT, F]) for i in range(2)]
        LH = [sb(f"LH{i}", [P, KT, F]) for i in range(2)]
        R = M[:].rearrange("p s f -> p (s f)")[:, 0:KT * F].rearrange("p (k f) -> p k f", k=KT)
        HT = sb("HT", [F + 1, 3, CH * P])
        UT = sb("UT", [F + 1, 3, CH * P])
        TE = sb("TE", [128, 2, CH * P])
        TR = sb("TR", [F, 2, CH * P])
        W = sb("W", [128, WCOLS])
        LNG = sb("LNG", [P, 2 * F])
        ident = sb("ident", [P, P])
        ei = sb("ei", [P, 4, T], I32)
        ef = sb("ef", [P, 4, T])
        wgt = sb("wgt", [P, T])
        plc = sb("plc", [P, 2, T])
        first, slot1 = plc[:, 0, :], plc[:, 1, :]
        rep = sb("rep", [P, T])
        carry = sb("carry", [P, T])
        dg = sb("dg", [P, T, 2])
        dw = sb("dw", [P, 2, T])
        selfc = sb("selfc", [P, 2, T])
        icnt = sb("icnt", [P, T])
        asc = sb("asc", [P, T])
        sqd = sb("sqd", [P, T])
        mrow = sb("mrow", [P, T, 2])
        mg = sb("mg", [P, T, 2])
        slotf = sb("slotf", [P, T])
        sidx = sb("sidx", [P, T], I32)
        didx = sb("didx", [P, T], I32)
        gate = sb("gate", [P, KT])
        bst = sb("bst", [P, KT, 6])
        sm = sb("sm", [P, 4, KT])
        lnv = sb("lnv", [P, 2, 2, KT])
        zer = TR[:, 0, :]

        PT = [ctx.enter_context(nc.psum_tensor(f"PT{i}", [128, 512], F32)) for i in range(2)]
        PA = [ctx.enter_context(nc.psum_tensor(f"PA{i}", [128, 512], F32)) for i in range(2)]
        PB = [ctx.enter_context(nc.psum_tensor(f"PB{i}", [128, 512], F32)) for i in range(2)]
        PS = [ctx.enter_context(nc.psum_tensor(f"PS{i}", [128, 512], F32)) for i in range(2)]

        tab = [dram(f"tab{k}", [2 * NE, F]) for k in range(7)]
        nmap = dram("nmap", [NN, 2])
        tabD = [t[0:NE, :].rearrange("(p t) f -> p t f", t=T) for t in tab]
        tabS = [t[NE:2 * NE, :].rearrange("(p t) f -> p t f", t=T) for t in tab]
        x3 = dram("x3", [NE, F]).rearrange("(p t) f -> p t f", t=T)
        xb = x.rearrange("(b p k) f -> b p k f", p=P, k=KT)
        ob = out.rearrange("(b p k) f -> b p k f", p=P, k=KT)

        s_const = sem("s_const")
        s_bc = sem("s_bc")
        s_eq = sem("s_eq")
        s_init = sem("s_init")
        s_zero = sem("s_zero")
        s_mapz = sem("s_mapz")
        s_deg = sem("s_deg")
        s_maps = sem("s_maps")
        s_mapg = sem("s_mapg")
        s_slot = sem("s_slot")
        s_xg = [sem(f"s_xg{i}") for i in range(2)]
        s_xd = sem("s_xd")
        s_xl = [sem(f"s_xl{i}") for i in range(2)]
        s_hl = [sem(f"s_hl{i}") for i in range(2)]
        s_stat = sem("s_stat")
        s_norm = sem("s_norm")
        s_tp = sem("s_tp")
        s_tev = sem("s_tev")
        s_hu = sem("s_hu")
        s_a = sem("s_a")
        s_aev = sem("s_aev")
        s_elu = sem("s_elu")
        s_uu = sem("s_uu")
        s_b = sem("s_b")
        s_bev = sem("s_bev")
        s_v = sem("s_v")
        s_fin = sem("s_fin")
        s_row = sem("s_row")
        s_rst = sem("s_rst")
        s_m0 = sem("s_m0")
        s_attr = sem("s_attr")
        s_g = [sem(f"s_g{i}") for i in range(SLOTS)]
        s_turn = sem("s_turn")
        s_sc = sem("s_sc")
        s_msg = sem("s_msg")
        s_seg = sem("s_seg")
        s_agg = sem("s_agg")
        s_hd = sem("s_hd")
        s_gate = sem("s_gate")
        s_tb = sem("s_tb")
        s_x3r = sem("s_x3r")
        s_x3 = sem("s_x3")
        s_res = sem("s_res")
        s_out = sem("s_out")
        block = ctx.enter_context(nc.Block())

        def lane_rows(view, b):
            return view[bass.ds(b, 1)].rearrange("o p k f -> (o p) k f")

        def w(name, k=F):
            return W[0:k, WC[name]:WC[name] + F]

        def bias(name):
            return W[0:F, BC[name]:BC[name] + 1]

        S_CHUNKS = EB * 3 * NC
        N_CHUNKS = NB * 3 * NC
        S_ROWS = EB * 2 * NC
        S_NORM = EB * 5 * NC
        N_NORM = NB * 5 * NC
        S_STAT, N_STAT = EB * 5, NB * 5

        class Count:

            def __init__(self):
                self.t = self.a = self.b = self.e = self.stat = self.norm = 0
                self.v = self.fin = self.row = self.xg0 = 0

        class Fixed:

            def __init__(self, reg, first):
                self.reg, self.first = reg, first

            def __call__(self, per, base):
                return base if self.reg is None else self.reg * per + base

        A_D = S_CHUNKS + N_CHUNKS
        B_L2 = S_CHUNKS + S_ROWS + N_CHUNKS + 4 * EB * NC

        def b_end(kind, nl, b0, step, lane, i):
            hid = 2 if kind == "S" else 1
            n = [0, hid * nl, 2 * hid * nl][step] * NC
            return b0 + n + (lane * NC + i + 1) * (hid if step < 2 else 1)

        def ut_free(kind, nl, b0, step, lane, i):
            if i >= 3:
                return b_end(kind, nl, b0, step, lane, i - 3)
            q = step * nl + lane - 1
            return b0 - 2 + i if q < 0 else b_end(kind, nl, b0, q // nl, q % nl, i + 2)

        PAIRS = [[0, 1], [2, 3], [4]]

        def seg(rnd, t):
            return rnd * T + t

        @block.sync
        def _(sp):
            sp.dma_start(W[:], wts).then_inc(s_const, 16)
            sp.dma_start(ident[:], ident_in).then_inc(s_const, 16)
            sp.dma_start(plc[:], place).then_inc(s_const, 16)
            sp.dma_start(ei[:], edges.rearrange("j p t -> p j t")).then_inc(s_const, 16)
            sp.dma_start(dg[:], ew).then_inc(s_const, 16)
            sp.dma_start(LNG[:], lnp.partition_broadcast(P)).then_inc(s_const, 16)
            for b in range(T // 10):
                if b >= 2:
                    sp.wait_ge(s_eq, b - 1)
                half = R[:, 0:14, :].rearrange("p k f -> p (k f)") if b % 2 == 0 else \
                    LH[1][:, 0:14, :].rearrange("p k f -> p (k f)")
                sp.dma_start(half[:, 0:10 * P].bitcast(I32),
                             dst_rows[b * 10 * P:(b + 1) * 10 * P].partition_broadcast(P)).then_inc(s_bc, 16)
                sp.wait_ge(s_bc, 16 * (b + 1))
            sp.wait_ge(s_zero, 1)
            nm = nmap.rearrange("(p k) j -> p (k j)", p=P)
            for k in range(2):
                sp.dma_start(nm[:, k * 400:(k + 1) * 400], LH[0][:, 0:5, :].rearrange("p k f -> p (k f)")[:, 0:400])\
                    .then_inc(s_mapz, 16)

            def s_store(k, b, lane):
                sp.dma_start(tabS[k][:, b * KT:(b + 1) * KT, :], LH[lane][:]).then_inc(s_hl[lane], 16)
            norm = fin = row = 0
            for pair in PAIRS:
                n0 = norm
                for step in range(3):
                    for lane, b in enumerate(pair):
                        base = n0 + (step * len(pair) + lane) * NC
                        sp.wait_ge(s_norm, base + NC)
                        s_store([0, 2, 4][step], b, lane)
                        if step < 2:
                            row += 1
                            sp.wait_ge(s_row, row)
                            sp.dma_start(tabS[[1, 3][step]][:, b * KT:(b + 1) * KT, :], R).then_inc(s_rst, 16)
                for lane, b in enumerate(pair):
                    base = n0 + (4 * len(pair) + lane) * NC
                    sp.wait_ge(s_norm, base + NC)
                    s_store(5, b, lane)
                    s_store(6, b, lane)
                norm = n0 + 5 * len(pair) * NC

            sp.wait_ge(s_fin, EB)
            with sp.Fori(0, NB // 2) as r:
                for lane in range(2):
                    sp.wait_ge(s_fin, r * 2 + (EB - 1 + lane))
                    sp.dma_start(LX[lane][:], lane_rows(xb, r * 2 + lane)).then_inc(s_xl[lane], 16)
                for lane in range(2):
                    sp.wait_ge(s_fin, r * 2 + (EB + lane + 1))
                    sp.dma_start(lane_rows(ob, r * 2 + lane), LH[lane][:]).then_inc(s_hl[lane], 16)

            for b in range(EB):
                if b == 0:
                    sp.wait_ge(s_hl[0], 16 * (5 * 3 + NB // 2))
                    sp.wait_ge(s_hl[1], 16 * (5 * 2 + NB // 2))
                    sp.wait_ge(s_rst, 16 * 2 * EB)
                else:
                    sp.wait_ge(s_seg, seg(1, b * KT))
                sp.dma_start(M[:, :, 0:F], tabS[0][:, b * KT:(b + 1) * KT, :]).then_inc(s_m0, 16)
            for k in range(1, 5):
                for b in range(EB):
                    sp.wait_ge(s_hd, (k - 1) * EB + b + 1)
                    sp.dma_start(tabD[k][:, b * KT:(b + 1) * KT, :], HD[:, b * KT:(b + 1) * KT, :])\
                        .then_inc(s_tb, 16)
            for b in range(EB):
                sp.wait_ge(s_seg, seg(5, b * KT))
                sp.dma_start(M[:, :, F:F + FE], attr[:, b * KT:(b + 1) * KT, :]).then_inc(s_attr, 16)
                sp.wait_ge(s_attr, 16 * (b + 1))
            for b in range(EB):
                sp.wait_ge(s_hd, 4 * EB + b + 1)
                sp.dma_start(tabD[5][:, b * KT:(b + 1) * KT, :], HD[:, b * KT:(b + 1) * KT, :])\
                    .then_inc(s_tb, 16)
            sp.wait_ge(s_x3r, 1)
            sp.dma_start(x3, XD[:]).then_inc(s_x3, 16)
            with sp.Fori(0, STEPS // 2) as r:
                for i in range(2):
                    for b in range(EB):
                        sp.wait_ge(s_hd, r * (2 * EB) + (5 * EB + i * EB + b + 1))
                        sp.dma_start(tabD[6 - i][:, b * KT:(b + 1) * KT, :], HD[:, b * KT:(b + 1) * KT, :])\
                            .then_inc(s_tb, 16)
            sp.wait_ge(s_seg, seg(6 + STEPS, 0))
            sp.wait_ge(s_hd, (5 + STEPS) * EB)
            sp.wait_ge(s_tb, 16 * (5 + STEPS) * EB)
            sp.dma_start(XD[:], x3).then_inc(s_x3, 16)
            sp.wait_ge(s_x3, 32)
            sp.wait_ge(s_out, 16 * T)

        @block.gpsimd
        def _(gp):
            gp.wait_ge(s_const, 96)
            for t in range(T):
                gp.indirect_dma_start(XD[:, t, :], None, x,
                                      bass.IndirectOffsetOnAxis(ei[:, 1, t:t + 1], 0)).then_inc(s_xd, 16)
            uses = [0, 0]
            for pair in PAIRS:
                for lane, b in enumerate(pair):
                    if b >= 2:
                        gp.wait_ge(s_fin, b - 1)
                    for k in range(KT):
                        t = b * KT + k
                        gp.indirect_dma_start(LX[lane][:, k, :], None, x,
                                              bass.IndirectOffsetOnAxis(ei[:, 0, t:t + 1], 0))\
                            .then_inc(s_xg[lane], 16)
                if pair[0] == 0:
                    gp.wait_ge(s_deg, 1)
                    gp.wait_ge(s_mapz, 32)
                    for t in range(T):
                        gp.indirect_dma_start(nmap, bass.IndirectOffsetOnAxis(didx[:, t:t + 1], 0),
                                              mrow[:, t, :], None, bounds_check=NN - 1, oob_is_err=False)\
                            .then_inc(s_maps, 16)
                    gp.wait_ge(s_maps, 16 * T)
                    for t in range(T):
                        gp.indirect_dma_start(mg[:, t, :], None, nmap,
                                              bass.IndirectOffsetOnAxis(ei[:, 0, t:t + 1], 0))\
                            .then_inc(s_mapg, 16)

            def gather(table, rnd, reg=None):
                for t in range(T):
                    if t % CH == 0:
                        n = seg(rnd, t + CH - 1) - SLOTS + 1
                        gp.wait_ge(s_seg, n if reg is None else reg * (2 * T) + n)
                        gp.sem_inc(s_turn, 1)
                    gp.indirect_dma_start(M[:, t % SLOTS, 0:F], None, table,
                                          bass.IndirectOffsetOnAxis(sidx[:, t:t + 1], 0))\
                        .then_inc(s_g[t % SLOTS], 16)

            gp.wait_ge(s_slot, 1)
            for k in range(1, 5):
                gp.wait_ge(s_tb, 16 * EB * k)
                gather(tab[k], 1 + k)
            with gp.Fori(0, STEPS // 2) as r:
                for i in range(2):
                    gp.wait_ge(s_tb, r * (2 * 16 * EB) + 16 * EB * (5 + i))
                    gp.sem_inc(s_turn, 1)
                    gather(tab[5 + i], 6 + i, r)
            for t in range(T):
                if t % KT == 0:
                    gp.wait_ge(s_res, t // KT + 1)
                gp.indirect_dma_start(out, bass.IndirectOffsetOnAxis(didx[:, t:t + 1], 0),
                                      HD[:, t, :], None, bounds_check=NN - 1, oob_is_err=False)\
                    .then_inc(s_out, 16)
            gp.wait_ge(s_out, 16 * T)

        def landed(g, t):
            return 16 * (g * (T // SLOTS) + t // SLOTS + 1)

        @block.scalar
        def _(act):
            c = Count()

            def norm(X, H, k0, func, slot):
                for k in range(k0 * CH, k0 * CH + CH):
                    last = A.activation(H[:, k, :], X[:, k, :], func, bias=lnv[:, slot, 1, k:k + 1],
                                        scale=lnv[:, slot, 0, k:k + 1])
                last.then_inc(s_norm, 1)

            def steps(r0, kind, lanes, batch):
                t0, a0, st0, f0 = c.t, c.a, c.stat, c.fin
                nl = len(lanes)
                for step in range(3):
                    for lane in lanes:
                        q = step * nl + lane
                        st = q
                        act.wait_ge(s_stat, r0(5 * nl, st0 + st + 1))
                        if kind == "S" and (batch[lane] >= 2 or step > 0):
                            act.wait_ge(s_hl[lane], 16 * (5 * (batch[lane] // 2) + step))
                        if kind == "N" and step == 0:
                            act.wait_ge(s_hl[lane], r0(16, 16 * 5 * (3 - lane)))
                        X, H = LX[lane], LH[lane]
                        for i in range(NC + 2):
                            if i < NC:
                                norm(X, H, i, ACT.Relu, (st0 + st) % 2)
                            if 1 <= i <= NC:
                                n = t0 + q * NC + i - 1
                                act.wait_ge(s_tp, r0(3 * nl * NC, n + 1))
                                if not (r0.first and n < 3):
                                    act.wait_ge(s_a, r0(3 * nl * NC, n - 2))
                                A.activation(HT[0:F, n % 3, :], PT[n % 2][0:F, 0:CH * P], ACT.Copy)\
                                    .then_inc(s_tev, 1)
                            if i >= 2:
                                a_evac(a0 + q * NC + i - 2, [ACT.Relu, None, ACT.Gelu][step],
                                       ["b1", "s1", "ub"][step], r0, 3 * nl * NC,
                                       c.e + lane * NC + i - 2, nl * NC,
                                       ut_free(kind, nl, c.b, step, lane, i - 2))
                for j, func in ((3, ACT.Identity), (4, ACT.Relu)):
                    for lane in lanes:
                        st = j * nl + lane
                        act.wait_ge(s_stat, r0(5 * nl, st0 + st + 1))
                        src = LH[lane] if j == 3 else LX[lane]
                        if kind == "S" and j == 3:
                            act.wait_ge(s_hl[lane], 16 * (5 * (batch[lane] // 2) + 3))
                        for i in range(NC):
                            norm(src, LH[lane], i, func, (st0 + st) % 2)

            def a_evac(n, func, bname, r0, per, e, eper, free):
                act.wait_ge(s_a, r0(per, n + 1))
                src = PA[n % 2][0:F, 0:CH * P]
                if func is None:
                    if not (r0.first and e < 2):
                        act.wait_ge(s_elu, r0(eper, e - 1))
                    A.activation(TE[0:F, e % 2, :], src, ACT.Exp, bias=bias(bname))
                    A.activation(TR[:, e % 2, :], src, ACT.Relu, bias=bias(bname)).then_inc(s_aev, 1)
                else:
                    if free is None:
                        if n - 2 > A_D:
                            act.wait_ge(s_uu, n - 2 - A_D)
                    elif not (r0.first and n < 3):
                        act.wait_ge(s_b, r0(per, free))
                    A.activation(UT[0:F, n % 3, :], src, func, bias=bias(bname)).then_inc(s_aev, 1)

            act.wait_ge(s_const, 96)
            act.wait_ge(s_mapz, 32)
            act.wait_ge(s_eq, T // 10)
            for i, pair in enumerate(PAIRS):
                steps(Fixed(None, i == 0), "S", range(len(pair)), pair)
                c.b += 3 * NC * len(pair) + 2 * NC * len(pair)
                c.t += 3 * NC * len(pair)
                c.a += 3 * NC * len(pair)
                c.e += NC * len(pair)
                c.stat += 5 * len(pair)
            with act.Fori(0, NB // 2) as r:
                steps(Fixed(r, False), "N", range(2), None)
            c.t += N_CHUNKS
            c.a += N_CHUNKS
            c.e += NB * NC
            c.stat += N_STAT

            one = Fixed(None, False)

            def d_norm(b, dst, func=ACT.Relu, src=None):
                act.wait_ge(s_stat, c.stat + 1)
                for k in range(KT):
                    t = b * KT + k
                    last = A.activation(dst[:, t, :], (src or XD)[:, t, :], func,
                                        bias=lnv[:, c.stat % 2, 1, k:k + 1], scale=lnv[:, c.stat % 2, 0, k:k + 1])
                last.then_inc(s_norm, 1)
                c.stat += 1

            def d_tev(edge=False):
                n = c.t
                act.wait_ge(s_tp, n + 1)
                if edge:
                    act.wait_ge(s_hu, n - 1 - A_D)
                    A.activation(TE[:, n % 2, :], PT[n % 2][:, 0:CH * P], ACT.Copy).then_inc(s_tev, 1)
                else:
                    if n - 2 > A_D:
                        act.wait_ge(s_hu, n - 2 - A_D)
                    A.activation(HT[0:F, n % 3, :], PT[n % 2][0:F, 0:CH * P], ACT.Copy).then_inc(s_tev, 1)
                c.t += 1

            def d_aev(func, bname):
                a_evac(c.a, func, bname, one, 0, c.e, 0, None)
                c.a += 1
                if func is None:
                    c.e += 1

            def scale(rnd_g, t, sc):
                if rnd_g is None:
                    act.wait_ge(s_m0, 16 * (t // KT + 1))
                else:
                    act.wait_ge(s_g[t % SLOTS], landed(rnd_g, t))
                A.activation(M[:, t % SLOTS, 0:F], M[:, t % SLOTS, 0:F], ACT.Copy, scale=wgt[:, t:t + 1])\
                    .then_inc(s_sc, 1)

            for b in range(EB):
                d_norm(b, HD)
            act.wait_ge(s_slot, 1)
            for b in range(EB):
                for t in range(b * KT, b * KT + KT):
                    scale(None, t, 0)
                for i in range(NC):
                    d_tev()
                    d_aev(ACT.Relu, "b1")
            for b in range(EB):
                for t in range(b * KT, b * KT + KT):
                    scale(0, t, 0)
                for i in range(NC):
                    d_tev()
                d_norm(b, HD)
            for b in range(EB):
                for i in range(NC):
                    d_tev()
                    d_tev()
                    d_aev(None, "s1")
            for b in range(EB):
                for i in range(NC):
                    d_tev()
                    d_tev()
                d_norm(b, HD)
            gates = 0
            for b in range(EB):
                for i in range(NC):
                    d_tev(True)
                    d_aev(ACT.Gelu, "mb")
                    d_aev(ACT.Gelu, "gb")
                    nb = B_L2 + (b * 3 * NC) + 2 * i + 1
                    act.wait_ge(s_b, nb + 1)
                    A.activation(gate[:, i * CH:(i + 1) * CH], PB[nb % 2][0:P, 0:CH], ACT.Tanh, scale=0.5)\
                        .then_inc(s_gate, 1)
                for i in range(NC):
                    d_tev()
                    d_tev()
                    d_aev(ACT.Gelu, "ub")
                d_norm(b, HD, ACT.Identity, HD)
                d_norm(b, HD)

        @block.tensor
        def _(pe):
            c = Count()
            pe.wait_ge(s_const, 96)
            pe.wait_ge(s_init, 1)

            def segsum(rnd, t, rhs, n, reg=None):
                s = seg(rnd, t)
                pe.wait_ge(s_msg, s + 1 if reg is None else reg * (2 * T) + (s + 1))
                PE.matmul(PS[t % 2][0:P, 0:n], EQ[:, t, :], rhs, start=True, stop=True).then_inc(s_seg, 1)

            for t in range(T):
                segsum(0, t, dg[:, t, :], 2)

            def trans(n, r0, per, rows, width=F):
                if not (r0.first and n < 2):
                    pe.wait_ge(s_tev, r0(per, n - 1))
                for k in range(CH):
                    last = PE.transpose(PT[n % 2][0:width, k * P:(k + 1) * P], rows(k), ident[:])
                last.then_inc(s_tp, 1)

            def rows_out(n, r0, per, parts, cols=F):
                if not (r0.first and n < 2):
                    pe.wait_ge(s_bev, r0(per, n - 1))
                for k in range(CH):
                    for j, (l, rh) in enumerate(parts):
                        last = PE.matmul(PB[n % 2][0:P, k * cols:(k + 1) * cols], l(k), rh,
                                         start=(j == 0), stop=(j == len(parts) - 1))
                last.then_inc(s_b, 1)
                return last

            def steps(r0, kind, lanes):
                nl = len(lanes)
                per = 3 * nl * NC
                bper = per
                b = c.b
                for step in range(3):
                    for lane in lanes:
                        q = step * nl + lane
                        st = c.norm + q * NC
                        for i in range(NC + 2):
                            if i < NC:
                                pe.wait_ge(s_norm, r0(5 * nl * NC, st + i + 1))
                                trans(c.t + q * NC + i, r0, per, lambda k: LH[lane][:, i * CH + k, :])
                            if 1 <= i <= NC:
                                n = c.t + q * NC + i - 1
                                na = c.a + q * NC + i - 1
                                pe.wait_ge(s_tev, r0(per, n + 1))
                                if not (r0.first and na < 2):
                                    pe.wait_ge(s_aev, r0(per, na - 1))
                                PE.matmul(PA[na % 2][0:F, 0:CH * P], w(["W1", "WR1", "UA"][step]),
                                          HT[0:F, n % 3, :], start=True, stop=True).then_inc(s_a, 1)
                            if i >= 2:
                                na = c.a + q * NC + i - 2
                                if step == 1:
                                    pe.wait_ge(s_elu, r0(nl * NC, c.e + lane * NC + i - 1))
                                else:
                                    pe.wait_ge(s_aev, r0(per, na + 1))
                                u = lambda k, h: UT[0:h, na % 3, k * P:(k + 1) * P]
                                if kind == "S" and step < 2:
                                    rows_out(b, r0, bper, [(lambda k: u(k, F), ident[0:F, 0:F])])
                                    b += 1
                                rows_out(b, r0, bper, [(lambda k: u(k, F + 1), w(["W2", "WR2", "UW2"][step], F + 1))])
                                b += 1
                c.b = b

            for i, pair in enumerate(PAIRS):
                nl = len(pair)
                steps(Fixed(None, i == 0), "S", range(nl))
                c.t += 3 * NC * nl
                c.a += 3 * NC * nl
                c.e += NC * nl
                c.norm += 5 * NC * nl
            with pe.Fori(0, NB // 2) as r:
                steps(Fixed(r, False), "N", range(2))
            c.b += N_CHUNKS - 6 * NC
            c.t += N_CHUNKS
            c.a += N_CHUNKS
            c.e += NB * NC
            c.norm += N_NORM

            one = Fixed(None, False)

            def d_t(rows, width=F):
                trans(c.t, one, 0, rows, width)
                c.t += 1

            def d_a(pairs_):
                n = c.a
                pe.wait_ge(s_aev, n - 1)
                for j, (wt, tn, edge) in enumerate(pairs_):
                    pe.wait_ge(s_tev, tn + 1)
                    rhs = TE[:, tn % 2, :] if edge else HT[0:F, tn % 3, :]
                    last = PE.matmul(PA[n % 2][0:F, 0:CH * P], wt, rhs, start=(j == 0), stop=(j == len(pairs_) - 1))
                last.then_inc(s_a, 1)
                c.a += 1

            def used_t(k):
                pe.wait_ge(s_a, c.a)
                pe.sem_inc(s_hu, k)

            def d_b(parts, cols=F):
                rows_out(c.b, one, 0, parts, cols)
                c.b += 1

            def ut(n, h):
                return lambda k: UT[0:h, n % 3, k * P:(k + 1) * P]

            def ht(n, h):
                return lambda k: HT[0:h, n % 3, k * P:(k + 1) * P]

            def agg_rows(b, i):
                return lambda k: LX[b % 2][:, i * CH + k, :]

            def hd_rows(b, i):
                return lambda k: HD[:, b * KT + i * CH + k, :]

            c.norm += EB
            for b in range(EB):
                for t in range(b * KT, b * KT + KT):
                    segsum(1, t, M[:, t % SLOTS, 0:F], F)
                pe.wait_ge(s_agg, b + 1)
                for i in range(NC):
                    d_t(agg_rows(b, i))
                    d_a([(w("W1"), c.t - 1, False)])
                    used_t(1)
                    pe.wait_ge(s_aev, c.a)
                    d_b([(ut(c.a - 1, F), ident[0:F, 0:F])])
                    pe.wait_ge(s_b, c.b)
                    pe.sem_inc(s_uu, 1)
            for b in range(EB):
                for t in range(b * KT, b * KT + KT):
                    segsum(2, t, M[:, t % SLOTS, 0:F], F)
                pe.wait_ge(s_agg, EB + b + 1)
                for i in range(NC):
                    d_t(agg_rows(b, i))
                    pe.wait_ge(s_tev, c.t)
                    d_b([(ht(c.t - 1, F + 1), w("W2", F + 1))])
                    pe.wait_ge(s_b, c.b)
                    pe.sem_inc(s_hu, 1)
                c.norm += 1
            for b in range(EB):
                for t in range(b * KT, b * KT + KT):
                    segsum(3, t, M[:, t % SLOTS, 0:F], F)
                pe.wait_ge(s_agg, 2 * EB + b + 1)
                pe.wait_ge(s_norm, c.norm)
                for i in range(NC):
                    d_t(hd_rows(b, i))
                    d_t(agg_rows(b, i))
                    d_a([(w("WR1"), c.t - 2, False), (w("WL1"), c.t - 1, False)])
                    used_t(2)
                    c.e += 1
                    pe.wait_ge(s_elu, c.e)
                    d_b([(ut(c.a - 1, F), ident[0:F, 0:F])])
                    pe.wait_ge(s_b, c.b)
                    pe.sem_inc(s_uu, 1)
            for b in range(EB):
                for t in range(b * KT, b * KT + KT):
                    segsum(4, t, M[:, t % SLOTS, 0:F], F)
                pe.wait_ge(s_agg, 3 * EB + b + 1)
                for i in range(NC):
                    d_t(hd_rows(b, i))
                    d_t(agg_rows(b, i))
                    pe.wait_ge(s_tev, c.t)
                    d_b([(ht(c.t - 2, F + 1), w("WR2", F + 1)), (ht(c.t - 1, F), w("WL2"))])
                    pe.wait_ge(s_b, c.b)
                    pe.sem_inc(s_hu, 2)
                c.norm += 1
            assert c.b == B_L2, (c.b, B_L2)
            for b in range(EB):
                pe.wait_ge(s_attr, 16 * (b + 1))
                for i in range(NC):
                    for k in range(CH):
                        t = b * KT + i * CH + k
                        pe.wait_ge(s_g[t % SLOTS], landed(3, t))
                    d_t(lambda k: M[:, (i * CH + k) % SLOTS, :], F + FE)
                    d_a([(w("MW1", 128), c.t - 1, True)])
                    d_a([(w("GW1", 128), c.t - 1, True)])
                    used_t(1)
                    pe.wait_ge(s_aev, c.a - 1)
                    d_b([(ut(c.a - 2, F + 1), w("MW2", F + 1))])
                    pe.wait_ge(s_aev, c.a)
                    d_b([(ut(c.a - 1, F + 1), W[0:F + 1, GW2:GW2 + 1])], 1)
                    pe.wait_ge(s_b, c.b)
                    pe.sem_inc(s_uu, 2)
                for t in range(b * KT, b * KT + KT):
                    segsum(5, t, M[:, t % SLOTS, 0:F], F)
                pe.wait_ge(s_agg, 4 * EB + b + 1)
                pe.wait_ge(s_norm, c.norm)
                for i in range(NC):
                    d_t(hd_rows(b, i))
                    d_t(agg_rows(b, i))
                    d_a([(w("UA"), c.t - 2, False), (w("UB"), c.t - 1, False)])
                    used_t(2)
                    pe.wait_ge(s_aev, c.a)
                    d_b([(ut(c.a - 1, F + 1), w("UW2", F + 1))])
                    pe.wait_ge(s_b, c.b)
                    pe.sem_inc(s_uu, 1)
            with pe.Fori(0, STEPS // 2) as r:
                for i in range(2):
                    for t in range(T):
                        segsum(6 + i, t, M[:, t % SLOTS, 0:F], F, r)


        @block.vector
        def _(dve):
            c = Count()

            def rsqrt(y, v, h):
                dve.drain()
                V.tensor_single_scalar(y.bitcast(I32), v.bitcast(I32), 1, ALU.arith_shift_right)
                dve.drain()
                V.tensor_scalar(y.bitcast(I32), y.bitcast(I32), -1.0, 1597463007.0, ALU.mult, ALU.add)
                for _ in range(3):
                    dve.drain()
                    V.scalar_tensor_tensor(out=h, in0=y, scalar=-0.5, in1=y, op0=ALU.mult, op1=ALU.mult)
                    dve.drain()
                    V.tensor_tensor(h, h, v, ALU.mult)
                    dve.drain()
                    V.scalar_tensor_tensor(out=y, in0=h, scalar=1.5, in1=y, op0=ALU.add, op1=ALU.mult)
                dve.drain()

            def stats(X, slot):
                for k in range(KT):
                    V.bn_stats(bst[:, k, :], X[:, k, :])
                s, d, v, h = (sm[:, j, :] for j in range(4))
                y = lnv[:, slot, 0, :]
                dve.drain()
                V.tensor_tensor(s, bst[:, :, 1], bst[:, :, 4], ALU.add)
                V.tensor_tensor(d, bst[:, :, 1], bst[:, :, 4], ALU.subtract)
                V.tensor_tensor(v, bst[:, :, 2], bst[:, :, 5], ALU.add)
                dve.drain()
                V.scalar_tensor_tensor(out=d, in0=d, scalar=0.25, in1=d, op0=ALU.mult, op1=ALU.mult)
                V.tensor_scalar(v, v, 1.0 / F, EPS, ALU.mult, ALU.add)
                dve.drain()
                V.tensor_tensor(v, v, d, ALU.add)
                rsqrt(y, v, h)
                V.scalar_tensor_tensor(out=lnv[:, slot, 1, :], in0=s, scalar=-0.5, in1=y, op0=ALU.mult,
                                       op1=ALU.mult).then_inc(s_stat, 1)

            def elu(e, u, r0, per, uper, free):
                dve.wait_ge(s_aev, r0(uper, u + 1))
                if free is None:
                    dve.wait_ge(s_uu, u - 2 - A_D)
                else:
                    dve.wait_ge(s_b, r0(uper, free))
                V.tensor_scalar(TE[0:F, e % 2, :], TE[0:F, e % 2, :], 1.0, -1.0, ALU.min, ALU.add)
                dve.drain()
                V.tensor_tensor(UT[0:F, u % 3, :], TE[0:F, e % 2, :], TR[:, e % 2, :], ALU.add).then_inc(s_elu, 1)

            def pb(n, cols=F):
                return PB[n % 2][0:P, 0:CH * cols].rearrange("p (k f) -> p k f", k=CH)

            def affine(X, H):
                gb = [LNG[:, j * F:(j + 1) * F].unsqueeze(1).broadcast_to([P, KT, F]) for j in range(2)]
                V.tensor_tensor(H, H, gb[0], ALU.mult)
                V.tensor_tensor(X, X, gb[1], ALU.add)
                dve.drain()
                return V.tensor_tensor(X, X, H, ALU.add)

            V.memset(HT[F:F + 1, :, :], 1.0)
            V.memset(LH[0][:, 0:5, :], 0.0).then_inc(s_zero, 1)
            V.memset(UT[F:F + 1, :, :], 1.0).then_inc(s_init, 1)
            dve.wait_ge(s_const, 96)
            V.tensor_copy(ef[:], ei[:])
            dve.drain()
            V.tensor_tensor(rep[:], ef[:, 2, :], ef[:, 1, :], ALU.not_equal)
            V.tensor_tensor(carry[:], ef[:, 3, :], ef[:, 1, :], ALU.is_equal)
            dve.drain()
            V.tensor_tensor(carry[:], carry[:], first, ALU.mult)
            for b in range(T // 10):
                half = R[:, 0:14, :].rearrange("p k f -> p (k f)") if b % 2 == 0 else \
                    LH[1][:, 0:14, :].rearrange("p k f -> p (k f)")
                dve.wait_ge(s_bc, 16 * (b + 1))
                for k in range(10):
                    t = b * 10 + k
                    last = V.tensor_scalar(EQ[:, t, :], half[:, k * P:(k + 1) * P].bitcast(I32),
                                           ef[:, 1, t:t + 1], None, ALU.is_equal)
                last.then_inc(s_eq, 1)

            wcol = slotf
            V.tensor_copy(wcol[:], dg[:, :, 1])
            dve.drain()
            V.tensor_scalar(dg[:, 0, :], dg[:, 0, :], 1.0, None, ALU.mult).then_inc(s_msg, 1)
            for t in range(T):
                dve.wait_ge(s_seg, seg(0, t) + 1)
                if t + 1 < T:
                    V.scalar_tensor_tensor(out=dg[:, t + 1, :], in0=PS[t % 2][0:P, 0:2], scalar=carry[:, t + 1:t + 2],
                                           in1=dg[:, t + 1, :], op0=ALU.mult, op1=ALU.add).then_inc(s_msg, 1)
                V.tensor_copy(dg[:, t, :], PS[t % 2][0:P, 0:2])
            dve.drain()
            V.reciprocal(icnt[:], dg[:, :, 0])
            degw, degc = sqd[:], asc[:]
            V.tensor_scalar(degw, dg[:, :, 1], 1.0, None, ALU.add)
            V.tensor_scalar(degc, dg[:, :, 0], 1.0, None, ALU.add)
            dve.drain()
            V.tensor_scalar(wgt[:], degw, 0.0, None, ALU.is_gt)
            V.tensor_scalar(degw, degw, 1e-30, None, ALU.max)
            rsqrt(dw[:, 0, :], degw, ef[:, 2, :])
            V.tensor_tensor(dw[:, 0, :], dw[:, 0, :], wgt[:], ALU.mult)
            rsqrt(dw[:, 1, :], degc, ef[:, 2, :])
            V.tensor_tensor(selfc[:, 0, :], dw[:, 0, :], rep[:], ALU.mult)
            V.tensor_tensor(sqd[:], degc, dw[:, 1, :], ALU.mult)
            V.reciprocal(ef[:, 3, :], degc)
            dve.drain()
            V.tensor_scalar(asc[:], ef[:, 3, :], 1.0 - ALPHA, None, ALU.mult)
            V.tensor_copy(mrow[:, :, 1], dw[:, 0, :])
            V.tensor_copy(mrow[:, :, 0], slot1)
            V.tensor_scalar(ef[:, 2, :], ef[:, 1, :], -FAR, None, ALU.add)
            dve.drain()
            V.tensor_tensor(ef[:, 2, :], ef[:, 2, :], rep[:], ALU.mult)
            dve.drain()
            V.tensor_scalar(didx[:], ef[:, 2, :], FAR, None, ALU.add).then_inc(s_deg, 1)

            def b_use(n, r0, per, kind, X, H, i, to=None):
                dve.wait_ge(s_b, r0(per, n + 1))
                ks = slice(i * CH, (i + 1) * CH)
                if kind == "row":
                    op = V.tensor_copy(to[:, ks, :], pb(n))
                elif kind == "relu":
                    op = V.scalar_tensor_tensor(out=X[:, ks, :], in0=pb(n), scalar=0.0, in1=X[:, ks, :],
                                                op0=ALU.max, op1=ALU.add)
                elif kind == "add":
                    op = V.tensor_tensor(X[:, ks, :], pb(n), X[:, ks, :], ALU.add)
                else:
                    op = V.tensor_tensor(H[:, ks, :], pb(n), H[:, ks, :], ALU.add)
                op.then_inc(s_bev, 1)
                return op

            def steps(r0, kind, lanes, batch, row0):
                nl = len(lanes)
                per = 3 * nl * NC
                b = c.b
                row = row0
                for lane in lanes:
                    if kind == "S":
                        dve.wait_ge(s_xg[lane], 16 * KT * (batch[lane] // 2 + 1))
                    else:
                        dve.wait_ge(s_xl[lane], r0(16, 16))
                    stats(LX[lane], (c.stat + lane) % 2)
                for step in range(3):
                    for lane in lanes:
                        q = step * nl + lane
                        X, H = LX[lane], LH[lane]
                        hidden = kind == "S" and step < 2
                        if hidden and row > 0:
                            dve.wait_ge(s_rst, 16 * row)
                        if kind == "S" and step == 2:
                            dve.wait_ge(s_hl[lane], 16 * (5 * (batch[lane] // 2) + 3))
                        for i in range(NC + 1):
                            if step == 1 and i < NC:
                                elu(c.e + lane * NC + i, c.a + q * NC + i, r0, nl * NC, per,
                                    ut_free(kind, nl, c.b, step, lane, i))
                            if i >= 1:
                                if hidden:
                                    op = b_use(b, r0, per, "row", X, H, i - 1, R)
                                    b += 1
                                b_use(b, r0, per, ["relu", "add", "hid"][step], X, H, i - 1)
                                b += 1
                        if hidden:
                            dve.drain().then_inc(s_row, 1)
                            row += 1
                        else:
                            dve.drain()
                        stats(H if step == 2 else X, (c.stat + (step + 1) * nl + lane) % 2)
                for j in (3, 4):
                    for lane in lanes:
                        X, H = LX[lane], LH[lane]
                        dve.wait_ge(s_norm, r0(5 * nl * NC, c.norm + (j * nl + lane + 1) * NC))
                        if j == 3:
                            affine(X[:], H[:])
                            dve.drain()
                            stats(X, (c.stat + 4 * nl + lane) % 2)
                        elif kind == "N":
                            V.tensor_tensor(H[:], X[:], H[:], ALU.add).then_inc(s_fin, 1)
                        else:
                            dve.sem_inc(s_fin, 1)
                c.b = b
                return row

            row = 0
            for i, pair in enumerate(PAIRS):
                nl = len(pair)
                row = steps(Fixed(None, i == 0), "S", range(nl), pair, row)
                c.a += 3 * NC * nl
                c.e += NC * nl
                c.stat += 5 * nl
                c.norm += 5 * NC * nl
                if i == 0:
                    dve.wait_ge(s_mapg, 16 * T)
                    has, own = ef[:, 3, :], ef[:, 2, :]
                    V.tensor_scalar(has, mg[:, :, 0], 1.0, None, ALU.min)
                    V.tensor_scalar(own, slot1, -1.0, -float(NE), ALU.mult, ALU.add)
                    dve.drain()
                    V.tensor_tensor(own, own, has, ALU.mult)
                    V.tensor_tensor(wgt[:], mg[:, :, 1], has, ALU.subtract)
                    dve.drain()
                    V.tensor_tensor(own, own, mg[:, :, 0], ALU.add)
                    V.scalar_tensor_tensor(out=wgt[:], in0=wgt[:], scalar=1.0, in1=wcol[:], op0=ALU.add, op1=ALU.mult)
                    dve.drain()
                    V.tensor_tensor(own, own, slot1, ALU.add)
                    dve.drain()
                    V.tensor_scalar(own, own, float(NE - 1), None, ALU.add)
                    dve.drain()
                    V.tensor_copy(sidx[:], own).then_inc(s_slot, 1)
            with dve.Fori(0, NB // 2) as r:
                steps(Fixed(r, False), "N", range(2), None, 0)
            c.b += N_CHUNKS - 6 * NC
            c.a += N_CHUNKS
            c.e += NB * NC
            c.stat += N_STAT
            c.norm += N_NORM

            one = Fixed(None, False)

            def d_stats(X, b):
                stats(X[:, b * KT:(b + 1) * KT, :], c.stat % 2)
                c.stat += 1

            def chain(rnd, t0, t1, arrive, selfcoef, outscale, dest, addend=None, reg=None, selfrow=None):
                def at(n):
                    return n if reg is None else reg * (2 * T) + n

                def own(t):
                    arrive(t)
                    if selfcoef is not None:
                        V.scalar_tensor_tensor(out=M[:, t % SLOTS, 0:F], in0=HD[:, t, :], scalar=selfcoef[:, t:t + 1],
                                               in1=M[:, t % SLOTS, 0:F], op0=ALU.mult, op1=ALU.add)

                def leave(t):
                    src = PS[t % 2][0:P, 0:F]
                    if addend is not None:
                        return V.scalar_tensor_tensor(out=dest(t), in0=src, scalar=outscale[:, t:t + 1],
                                                      in1=addend[:, t, :], op0=ALU.mult, op1=ALU.add)
                    if outscale is None:
                        return V.tensor_copy(dest(t), src)
                    return V.tensor_scalar(dest(t), src, outscale[:, t:t + 1], None, ALU.mult)

                own(t0)
                for t in range(t0, t1):
                    if t + 1 < t1:
                        own(t + 1)
                    m = M[:, t % SLOTS, 0:F]
                    if t == t0:
                        dve.drain()
                    if t == 0:
                        V.tensor_scalar(m, m, 1.0, None, ALU.mult).then_inc(s_msg, 1)
                    else:
                        dve.wait_ge(s_seg, at(seg(rnd, t)))
                        V.scalar_tensor_tensor(out=m, in0=PS[(t - 1) % 2][0:P, 0:F], scalar=carry[:, t:t + 1], in1=m,
                                               op0=ALU.mult, op1=ALU.add).then_inc(s_msg, 1)
                    if t > t0:
                        leave(t - 1)
                dve.wait_ge(s_seg, at(seg(rnd, t1 - 1) + 1))
                return leave(t1 - 1)

            def agg(b):
                return lambda t: LX[b % 2][:, t - b * KT, :]

            def elu_d():
                elu(c.e, c.a, one, 0, 0, None)
                c.e += 1

            def d_use(kind, b, i):
                op = b_use(c.b, one, 0, kind, XD[:, b * KT:(b + 1) * KT, :], HD[:, b * KT:(b + 1) * KT, :], i,
                           HD[:, b * KT:(b + 1) * KT, :])
                c.b += 1
                return op

            dve.wait_ge(s_xd, 16 * T)
            for b in range(EB):
                if b >= 2:
                    dve.wait_ge(s_norm, c.norm + b - 1)
                d_stats(XD, b)
            c.norm += EB
            dve.wait_ge(s_norm, c.norm)
            scaled = 0
            for b in range(EB):
                chain(1, b * KT, (b + 1) * KT, lambda t: dve.wait_ge(s_sc, t + 1), selfc[:, 0, :], dw[:, 0, :],
                      agg(b)).then_inc(s_agg, 1)
                for i in range(NC):
                    d_use("row", b, i)
                dve.drain().then_inc(s_hd, 1)
                c.a += NC
            for b in range(EB):
                chain(2, b * KT, (b + 1) * KT, lambda t: dve.wait_ge(s_sc, T + t + 1), selfc[:, 0, :], dw[:, 0, :],
                      agg(b)).then_inc(s_agg, 1)
                for i in range(NC):
                    d_use("relu", b, i)
                dve.drain()
                d_stats(XD, b)
                c.norm += 1
                dve.wait_ge(s_norm, c.norm)
                dve.sem_inc(s_hd, 1)
            for b in range(EB):
                chain(3, b * KT, (b + 1) * KT, lambda t: dve.wait_ge(s_g[t % SLOTS], landed(1, t)), None, icnt[:],
                      agg(b)).then_inc(s_agg, 1)
                for i in range(NC):
                    elu_d()
                    c.a += 1
                    d_use("row", b, i)
                dve.drain().then_inc(s_hd, 1)
            for b in range(EB):
                chain(4, b * KT, (b + 1) * KT, lambda t: dve.wait_ge(s_g[t % SLOTS], landed(2, t)), None, icnt[:],
                      agg(b)).then_inc(s_agg, 1)
                for i in range(NC):
                    d_use("add", b, i)
                dve.drain()
                d_stats(XD, b)
                c.norm += 1
                dve.wait_ge(s_norm, c.norm)
                dve.sem_inc(s_hd, 1)
            for b in range(EB):
                for i in range(NC):
                    gs = slice(i * CH, (i + 1) * CH)
                    dve.wait_ge(s_gate, b * NC + i + 1)
                    V.tensor_scalar(gate[:, gs], gate[:, gs], 0.5, 0.5, ALU.mult, ALU.add)
                    dve.drain()
                    for k in range(CH):
                        last = V.tensor_scalar(M[:, i * CH + k, 0:F], pb(c.b)[:, k, :],
                                               gate[:, i * CH + k:i * CH + k + 1], None, ALU.mult)
                    last.then_inc(s_bev, 2)
                    c.b += 2
                dve.drain()
                chain(5, b * KT, (b + 1) * KT, lambda t: None, None, None, agg(b)).then_inc(s_agg, 1)
                for i in range(NC):
                    d_use("hid", b, i)
                dve.drain()
                d_stats(HD, b)
                c.norm += 1
                dve.wait_ge(s_norm, c.norm)
                xs, hs = XD[:, b * KT:(b + 1) * KT, :], HD[:, b * KT:(b + 1) * KT, :]
                affine(xs, hs)
                dve.drain()
                d_stats(XD, b)
                c.norm += 1
                dve.wait_ge(s_norm, c.norm)
                V.tensor_tensor(hs, hs, dw[:, 1, b * KT:(b + 1) * KT].unsqueeze(2).broadcast_to([P, KT, F]), ALU.mult)\
                    .then_inc(s_hd, 1)
            dve.drain().then_inc(s_x3r, 1)
            dve.wait_ge(s_x3, 16)
            V.tensor_scalar(XD[:], HD[:], ALPHA, None, ALU.mult)
            with dve.Fori(0, STEPS // 2) as r:
                for i in range(2):
                    for b in range(EB):
                        chain(6 + i, b * KT, (b + 1) * KT,
                              lambda t: dve.wait_ge(s_g[t % SLOTS], r * (2 * 16 * (T // SLOTS)) + landed(4 + i, t)),
                              rep[:], asc[:], lambda t: HD[:, t, :], XD[:], r).then_inc(s_hd, 1)
            dve.wait_ge(s_x3, 32)
            for t in range(T):
                last = V.scalar_tensor_tensor(out=HD[:, t, :], in0=HD[:, t, :], scalar=sqd[:, t:t + 1], in1=XD[:, t, :],
                                              op0=ALU.mult, op1=ALU.add)
                if t % KT == KT - 1:
                    last.then_inc(s_res, 1)


def kernel(**inputs):
    import numpy as np
    import concourse.bacc as bacc
    from concourse.bass_utils import run_bass_kernel_spmd as run

    a = {k: np.asarray(v) for k, v in inputs.items()}

    def tiles(v):
        v = v.reshape((T, P) + v.shape[1:]).copy()
        v[1::2] = v[1::2, ::-1]
        return np.ascontiguousarray(np.swapaxes(v, 0, 1))

    src, dst = a["src"], a["dst"]
    no = np.full(1, -1, dst.dtype)
    nxt, prv = np.concatenate([dst[1:], no]), np.concatenate([no, dst[:-1]])
    wts = np.zeros((128, WCOLS), np.float32)

    def put(name, m, b=None):
        wts[0:m.shape[0], WC[name]:WC[name] + F] = m
        if b is not None:
            wts[F, WC[name]:WC[name] + F] = b

    put("W1", a["L0_gnn_W1"])
    put("W2", a["L0_gnn_W2"], a["L0_gnn_b2"])
    put("WR1", a["L1_gnn_W1r"].T)
    put("WL1", a["L1_gnn_W1l"].T)
    put("WR2", a["L1_gnn_W2r"].T, a["L1_gnn_b2"])
    put("WL2", a["L1_gnn_W2l"].T)
    put("MW1", a["L2_gnn_mW1"])
    put("MW2", a["L2_gnn_mW2"], a["L2_gnn_mb2"])
    put("GW1", a["L2_gnn_gW1"])
    put("UA", a["L2_gnn_uW1"][:F])
    put("UB", a["L2_gnn_uW1"][F:])
    put("UW2", a["L2_gnn_uW2"], a["L2_gnn_ub2"])
    wts[0:F, GW2], wts[F, GW2] = a["L2_gnn_gW2"][:, 0], a["L2_gnn_gb2"][0]
    for n, k in (("b1", "L0_gnn_b1"), ("s1", "L1_gnn_b1"), ("mb", "L2_gnn_mb1"), ("gb", "L2_gnn_gb1"),
                 ("ub", "L2_gnn_ub1")):
        wts[0:F, BC[n]] = a[k]
    first = np.zeros((P, T), np.float32)
    first[0, 0::2] = 1
    first[P - 1, 1::2] = 1
    place = np.stack([first, np.arange(1, NE + 1, dtype=np.float32).reshape(P, T)], 1)
    arrays = {
        "x": a["x"],
        "edges": np.stack([tiles(v) for v in (src, dst, nxt, prv)]),
        "ew": np.stack([np.ones((P, T), np.float32), tiles(a["edge_weight"])], 2),
        "dst_rows": np.ascontiguousarray(tiles(dst).T).reshape(-1),
        "attr": tiles(a["edge_attr_32"]),
        "wts": wts,
        "lnp": np.concatenate([a["L2_gnn_ln_g"], a["L2_gnn_ln_b"]]),
        "ident": np.eye(P, dtype=np.float32),
        "place": np.ascontiguousarray(place),
    }
    nc = bacc.Bacc("TRN2", target_bir_lowering=False, num_devices=1)
    args = [nc.dram_tensor(f"in_{k}", v.shape, mybir.dt.from_np(v.dtype), kind="ExternalInput").ap()
            for k, v in arrays.items()]
    args.append(nc.dram_tensor("out", (NN, F), F32, kind="ExternalOutput").ap())
    gnn_kernel(nc, *args)
    r = run(nc, [{f"in_{k}": v for k, v in arrays.items()}], core_ids=[0])
    return r.results[0]["out"]
```

```python
import concourse.bass as bass
from concourse import mybir
from contextlib import ExitStack

F32 = mybir.dt.float32
I32 = mybir.dt.int32
ALU = mybir.AluOpType
ACT = mybir.ActivationFunctionType

P = 125
F = 96
FE = 32
NN = 50000
NE = 12500
T = NE // P
KT = 20
CH = 4
NC = KT // CH
EB = T // KT
NB = NN // P // KT
SLOTS = 20
STEPS = 16
ALPHA = 0.1
EPS = 1e-5
FAR = float(1 << 20)

WN = ["W1", "W2", "WR1", "WL1", "WR2", "WL2", "MW1", "MW2", "GW1", "UA", "UB", "UW2"]
WC = {n: i * F for i, n in enumerate(WN)}
GW2 = len(WN) * F
BC = {n: GW2 + 1 + i for i, n in enumerate(["b1", "s1", "mb", "gb", "ub"])}
WCOLS = GW2 + 6
ED = ["src", "dst", "nxt", "prv"]


def gnn_kernel(nc, x, edges, ew, dst_rows, attr, wts, lnp, ident_in, place, out):
    ctx = ExitStack()
    with ctx:
        def sb(name, shape, dt=F32):
            return ctx.enter_context(nc.sbuf_tensor(name, shape, dt))

        def sem(name):
            return ctx.enter_context(nc.semaphore(name))

        def dram(name, shape):
            return nc.dram_tensor(name, shape, F32).ap()

        V, A, PE = nc.vector, nc.scalar, nc.tensor

        EQ = sb("EQ", [P, T, P])
        XD = sb("XD", [P, T, F])
        HD = sb("HD", [P, T, F])
        M = sb("M", [P, SLOTS, F + FE])
        LX = [sb(f"LX{i}", [P, KT, F]) for i in range(2)]
        LH = [sb(f"LH{i}", [P, KT, F]) for i in range(2)]
        R = M[:].rearrange("p s f -> p (s f)")[:, 0:KT * F].rearrange("p (k f) -> p k f", k=KT)
        HT = sb("HT", [F + 1, 3, CH * P])
        UT = sb("UT", [F + 1, 3, CH * P])
        TE = sb("TE", [128, 2, CH * P])
        TR = sb("TR", [F, 2, CH * P])
        W = sb("W", [128, WCOLS])
        LNG = sb("LNG", [P, 2 * F])
        ident = sb("ident", [P, P])
        ei = sb("ei", [P, 4, T], I32)
        ef = sb("ef", [P, 4, T])
        wgt = sb("wgt", [P, T])
        plc = sb("plc", [P, 2, T])
        first, slot1 = plc[:, 0, :], plc[:, 1, :]
        rep = sb("rep", [P, T])
        carry = sb("carry", [P, T])
        dg = sb("dg", [P, T, 2])
        dw = sb("dw", [P, 2, T])
        selfc = sb("selfc", [P, 2, T])
        icnt = sb("icnt", [P, T])
        asc = sb("asc", [P, T])
        sqd = sb("sqd", [P, T])
        mrow = sb("mrow", [P, T, 2])
        mg = sb("mg", [P, T, 2])
        slotf = sb("slotf", [P, T])
        sidx = sb("sidx", [P, T], I32)
        didx = sb("didx", [P, T], I32)
        gate = sb("gate", [P, KT])
        bst = sb("bst", [P, 2, KT, 6])
        sm = sb("sm", [P, 2, 4, KT])
        lnv = sb("lnv", [P, 2, 2, KT])
        SB = 25

        def spread(b):
            return HD[:].rearrange("p t f -> p (t f)")[:, b % 3 * SB * P:(b % 3 + 1) * SB * P]

        PT = [ctx.enter_context(nc.psum_tensor(f"PT{i}", [128, 512], F32)) for i in range(2)]
        PA = [ctx.enter_context(nc.psum_tensor(f"PA{i}", [128, 512], F32)) for i in range(2)]
        PB = [ctx.enter_context(nc.psum_tensor(f"PB{i}", [128, 512], F32)) for i in range(2)]
        PS = [ctx.enter_context(nc.psum_tensor(f"PS{i}", [128, 512], F32)) for i in range(2)]

        tab = [dram(f"tab{k}", [2 * NE, F]) for k in range(7)]
        nmap = dram("nmap", [NN, 2])
        tabD = [t[0:NE, :].rearrange("(p t) f -> p t f", t=T) for t in tab]
        tabS = [t[NE:2 * NE, :].rearrange("(p t) f -> p t f", t=T) for t in tab]
        x3 = dram("x3", [NE, F]).rearrange("(p t) f -> p t f", t=T)
        xb = x.rearrange("(b p k) f -> b p k f", p=P, k=KT)
        ob = out.rearrange("(b p k) f -> b p k f", p=P, k=KT)

        s_const = sem("s_const")
        s_bc = [sem(f"s_bc{b}") for b in range(T // SB)]
        s_eq = sem("s_eq")
        s_init = sem("s_init")
        s_zero = sem("s_zero")
        s_mapz = sem("s_mapz")
        s_deg = sem("s_deg")
        s_maps = sem("s_maps")
        s_mapg = sem("s_mapg")
        s_slot = sem("s_slot")
        s_xg = [sem(f"s_xg{i}") for i in range(2)]
        s_xd = sem("s_xd")
        s_xl = [sem(f"s_xl{i}") for i in range(2)]
        s_hl = [sem(f"s_hl{i}") for i in range(2)]
        s_bn = sem("s_bn")
        s_ln = sem("s_ln")
        s_xb = sem("s_xb")
        s_norm = sem("s_norm")
        s_tp = sem("s_tp")
        s_tev = sem("s_tev")
        s_a = sem("s_a")
        s_aev = sem("s_aev")
        s_eh = sem("s_eh")
        s_elu = sem("s_elu")
        s_b = sem("s_b")
        s_bev = sem("s_bev")
        s_fin = sem("s_fin")
        s_row = sem("s_row")
        s_rst = sem("s_rst")
        s_m0 = [sem(f"s_m0{i}") for i in range(NC)]
        s_attr = [sem(f"s_attr{i}") for i in range(NC)]
        s_g = [sem(f"s_g{i}") for i in range(SLOTS)]
        s_turn = sem("s_turn")
        s_sc = sem("s_sc")
        s_msg = sem("s_msg")
        s_seg = sem("s_seg")
        s_agg = sem("s_agg")
        s_hd = sem("s_hd")
        s_gate = sem("s_gate")
        s_gu = sem("s_gu")
        s_tb = sem("s_tb")
        s_x3r = sem("s_x3r")
        s_x3 = sem("s_x3")
        s_res = sem("s_res")
        s_out = sem("s_out")
        block = ctx.enter_context(nc.Block())

        def lane_rows(view, b):
            return view[bass.ds(b, 1)].rearrange("o p k f -> (o p) k f")

        def w(name, k=F):
            return W[0:k, WC[name]:WC[name] + F]

        def bias(name):
            return W[0:F, BC[name]:BC[name] + 1]

        PRE = NB // 2 - STEPS // 2
        S_CHUNKS = EB * 3 * NC
        N_CHUNKS = PRE * 2 * 3 * NC
        S_ROWS = EB * 2 * NC
        S_NORM = EB * 5 * NC
        S_STAT, N_STAT = EB * 5, PRE * 2 * 5
        NORM_D = S_NORM + PRE * 10 * NC
        NORM_N = NORM_D + 5 * EB

        LN_OPS = 18

        class Count:

            def __init__(self):
                self.t = self.a = self.b = self.e = self.stat = self.norm = 0
                self.v = self.fin = self.row = self.xg0 = 0

        class Fixed:

            def __init__(self, reg, first, pair=0):
                self.reg, self.first, self.pair = reg, first, pair

            def __call__(self, per, base):
                return base if self.reg is None else self.reg * per + base

        A_D = S_CHUNKS + N_CHUNKS
        B_D = S_CHUNKS + S_ROWS + N_CHUNKS

        LAGS = {"g1": 0, "g2": 0, "s1": 0, "s2": 0, "l2": 3}
        STAGES = list(LAGS)
        DC = T // CH

        def plan():
            t = a = A_D
            b = B_D
            no, used_t, used_a = {}, {}, {}
            for g in STAGES:
                lag = LAGS[g]
                last = 2 if g in ("g2", "s2") else 3
                for s in range(DC + lag + last + 1):
                    msg, c_t, c_a, c_b = s, s - lag - 1, s - lag - 2, s - lag - last
                    if g == "l2" and msg < DC:
                        no[g, "tm", msg] = t
                        t += 1
                    if g == "l2" and 0 <= s - 2 < DC:
                        no[g, "bm", s - 2], no[g, "bg", s - 2] = b, b + 1
                        used_a[no[g, "am", s - 2]] = b + 1
                        used_a[no[g, "ag", s - 2]] = b + 2
                        b += 2
                    if 0 <= c_b < DC:
                        no[g, "b", c_b] = b
                        if last == 3:
                            used_a[no[g, "a", c_b]] = b + 1
                        else:
                            for j in "hg":
                                if (g, "t" + j, c_b) in no:
                                    used_t[no[g, "t" + j, c_b]] = (s_b, b + 1)
                        b += 1
                    if last == 3 and 0 <= c_a < DC:
                        no[g, "a", c_a] = a
                        for j in "hg":
                            if (g, "t" + j, c_a) in no:
                                used_t[no[g, "t" + j, c_a]] = (s_a, a + 1)
                        a += 1
                    if 0 <= c_t < DC:
                        for j in ("h", "g")[g in ("g1", "g2"):]:
                            no[g, "t" + j, c_t] = t
                            t += 1
                    if g == "l2" and 0 <= s - 1 < DC:
                        no[g, "am", s - 1], no[g, "ag", s - 1] = a, a + 1
                        a += 2
            return no, used_t, used_a, t, a, b

        no, used_t, used_a, T_N, A_N, B_N = plan()

        def slots(g):
            lag, last = LAGS[g], 2 if g in ("g2", "s2") else 3
            ok = lambda c: c if 0 <= c < DC else None
            for s in range(DC + lag + last + 1):
                m = g == "l2"
                yield (ok(s - lag), ok(s - lag - 1), ok(s - lag - 2) if last == 3 else None, ok(s - lag - last),
                       ok(s) if m else None, ok(s - 1) if m else None, ok(s - 2) if m else None)

        def b_end(kind, nl, b0, step, lane, i):
            hid = 2 if kind == "S" else 1
            n = [0, hid * nl, 2 * hid * nl][step] * NC
            return b0 + n + (lane * NC + i + 1) * (hid if step < 2 else 1)

        def ut_free(kind, nl, b0, step, lane, i):
            if i >= 3:
                return b_end(kind, nl, b0, step, lane, i - 3)
            q = step * nl + lane - 1
            return b0 - 2 + i if q < 0 else b_end(kind, nl, b0, q // nl, q % nl, i + 2)

        PAIRS = [[0, 1], [2, 3], [4]]

        def seg(rnd, t):
            return rnd * T + t

        N_SLOTS = 6 * (NC + 2)
        HALF, PAUSE = 28, 3
        LEAD, END, TAIL = 6, 38, 22

        def tiles_by(k):
            k = min(k, N_SLOTS - 1)
            if k < HALF + PAUSE:
                return min(T, LEAD + (T - LEAD) * (k + 1) // HALF)
            return T + (T - END - TAIL) * (k + 1 - HALF - PAUSE) // (N_SLOTS - HALF - PAUSE)

        @block.sync
        def _(sp):
            sp.dma_start(W[:], wts).then_inc(s_const, 16)
            sp.dma_start(ident[:], ident_in).then_inc(s_const, 16)
            sp.dma_start(plc[:], place).then_inc(s_const, 16)
            sp.dma_start(ei[:], edges.rearrange("j p t -> p j t")).then_inc(s_const, 16)
            sp.dma_start(dg[:], ew).then_inc(s_const, 16)
            sp.dma_start(LNG[:], lnp.partition_broadcast(P)).then_inc(s_const, 16)
            for b in range(T // SB):
                if b >= 3:
                    sp.wait_ge(s_eq, b - 2)
                sp.dma_start(spread(b).bitcast(I32),
                             dst_rows[b * SB * P:(b + 1) * SB * P].partition_broadcast(P)).then_inc(s_bc[b], 16)
            sp.wait_ge(s_zero, 1)
            nm = nmap.rearrange("(p k) j -> p (k j)", p=P)
            for k in range(2):
                sp.dma_start(nm[:, k * 400:(k + 1) * 400], LH[0][:, 0:5, :].rearrange("p k f -> p (k f)")[:, 0:400])\
                    .then_inc(s_mapz, 16)

            def s_store(k, b, lane):
                sp.dma_start(tabS[k][:, b * KT:(b + 1) * KT, :], LH[lane][:]).then_inc(s_hl[lane], 16)
            norm = fin = row = 0
            for pair in PAIRS:
                n0 = norm
                for step in range(3):
                    for lane, b in enumerate(pair):
                        base = n0 + (step * len(pair) + lane) * NC
                        sp.wait_ge(s_norm, base + NC)
                        s_store([0, 2, 4][step], b, lane)
                        if step < 2:
                            row += 1
                            sp.wait_ge(s_row, row)
                            sp.dma_start(tabS[[1, 3][step]][:, b * KT:(b + 1) * KT, :], R).then_inc(s_rst, 16)
                for lane, b in enumerate(pair):
                    base = n0 + (4 * len(pair) + lane) * NC
                    sp.wait_ge(s_norm, base + NC)
                    s_store(5, b, lane)
                    s_store(6, b, lane)
                norm = n0 + 5 * len(pair) * NC

            def n_load(lane, b, fin):
                sp.wait_ge(s_fin, fin)
                sp.dma_start(LX[lane][:], lane_rows(xb, b)).then_inc(s_xl[lane], 16)

            def n_store(lane, b, fin):
                sp.wait_ge(s_fin, fin)
                sp.dma_start(lane_rows(ob, b), LH[lane][:]).then_inc(s_hl[lane], 16)

            sp.wait_ge(s_fin, EB)
            with sp.Fori(0, PRE) as r:
                for lane in range(2):
                    n_load(lane, r * 2 + (NB - 2 * PRE + lane), r * 2 + (EB - 1 + lane))
                for lane in range(2):
                    n_store(lane, r * 2 + (NB - 2 * PRE + lane), r * 2 + (EB + lane + 1))

            sp.wait_ge(s_hl[0], 16 * (5 * 3 + PRE))
            sp.wait_ge(s_hl[1], 16 * (5 * 2 + PRE))
            sp.wait_ge(s_rst, 16 * 2 * EB)

            def first_messages(c):
                k = c % NC * CH
                if c >= NC:
                    sp.wait_ge(s_seg, seg(1, (c - NC + 1) * CH))
                sp.dma_start(M[:, k:k + CH, 0:F], tabS[0][:, c * CH:(c + 1) * CH, :]).then_inc(s_m0[c % NC], 16)

            for c in range(2 * NC):
                first_messages(c)
            for k in range(1, 5):
                for b in range(EB):
                    if k in (1, 3):
                        sp.wait_ge(s_hd, (k // 2) * EB + b + 1)
                    else:
                        sp.wait_ge(s_norm, NORM_D + (k // 2) * EB + b + 1)
                    sp.dma_start(tabD[k][:, b * KT:(b + 1) * KT, :], HD[:, b * KT:(b + 1) * KT, :])\
                        .then_inc(s_tb, 16)
                    if k == 1 and b + 2 < EB:
                        for c in range((b + 2) * NC, (b + 3) * NC):
                            first_messages(c)
            for c in range(DC):
                k = c % NC * CH
                sp.wait_ge(s_seg, seg(5, (c - NC + 1) * CH))
                sp.dma_start(M[:, k:k + CH, F:F + FE], attr[:, c * CH:(c + 1) * CH, :]).then_inc(s_attr[c % NC], 16)
            for b in range(EB):
                sp.wait_ge(s_hd, 2 * EB + b + 1)
                sp.dma_start(tabD[5][:, b * KT:(b + 1) * KT, :], HD[:, b * KT:(b + 1) * KT, :])\
                    .then_inc(s_tb, 16)
            sp.wait_ge(s_x3r, 1)
            sp.dma_start(x3, XD[:]).then_inc(s_x3, 16)
            sp.wait_ge(s_tp, T_N)
            for lane in range(2):
                n_load(lane, lane, EB + 2 * PRE)
            with sp.Fori(0, STEPS // 2) as r:
                for i in range(2):
                    for b in range(EB):
                        if (i, b) == (1, EB - 1):
                            for lane in range(2):
                                n_store(lane, r * 2 + lane, r * 2 + (EB + 2 * PRE + lane + 1))
                                sp.dma_start(LX[lane][:], lane_rows(xb, r * 2 + (2 + lane)))\
                                    .then_inc(s_xl[lane], 16)
                        sp.wait_ge(s_hd, r * (2 * EB) + (3 * EB + i * EB + b + 1))
                        sp.dma_start(tabD[6 - i][:, b * KT:(b + 1) * KT, :], HD[:, b * KT:(b + 1) * KT, :])\
                            .then_inc(s_tb, 16)
            sp.wait_ge(s_seg, seg(6 + STEPS, 0))
            sp.wait_ge(s_hd, (3 + STEPS) * EB)
            sp.wait_ge(s_tb, 16 * (5 + STEPS) * EB)
            sp.dma_start(XD[:], x3).then_inc(s_x3, 16)
            sp.wait_ge(s_x3, 32)
            for lane in range(2):
                sp.wait_ge(s_xl[lane], 16 * (NB // 2 + 1))
                sp.wait_ge(s_hl[lane], 16 * (5 * (3 - lane) + NB // 2))
            sp.wait_ge(s_out, 16 * T)

        @block.gpsimd
        def _(gp):
            gp.wait_ge(s_const, 96)

            def source_rows(pair):
                for lane, b in enumerate(pair):
                    if b >= 2:
                        gp.wait_ge(s_fin, b - 1)
                    for k in range(KT):
                        t = b * KT + k
                        gp.indirect_dma_start(LX[lane][:, k, :], None, x,
                                              bass.IndirectOffsetOnAxis(ei[:, 0, t:t + 1], 0))\
                            .then_inc(s_xg[lane], 16)

            def source_map(t0, t1):
                for t in range(t0, t1):
                    gp.indirect_dma_start(mg[:, t, :], None, nmap,
                                          bass.IndirectOffsetOnAxis(ei[:, 0, t:t + 1], 0))\
                        .then_inc(s_mapg, 16)

            source_rows(PAIRS[0])
            for t in range(T):
                gp.indirect_dma_start(XD[:, t, :], None, x,
                                      bass.IndirectOffsetOnAxis(ei[:, 1, t:t + 1], 0)).then_inc(s_xd, 16)
            gp.wait_ge(s_deg, 1)
            gp.wait_ge(s_mapz, 32)
            for t in range(T):
                gp.indirect_dma_start(nmap, bass.IndirectOffsetOnAxis(didx[:, t:t + 1], 0),
                                      mrow[:, t, :], None, bounds_check=NN - 1, oob_is_err=False)\
                    .then_inc(s_maps, 16)
            gp.wait_ge(s_maps, 16 * T)
            source_map(0, T // 2)
            source_rows(PAIRS[1])
            source_map(T // 2, T)
            source_rows(PAIRS[2])

            def gather(table, rnd, reg=None, between=None):
                for t in range(T):
                    if t % CH == 0:
                        if between is not None:
                            between(t)
                        n = seg(rnd, t + CH - 1) - SLOTS + 1
                        gp.wait_ge(s_seg, n if reg is None else reg * (2 * T) + n)
                        gp.sem_inc(s_turn, 1)
                    gp.indirect_dma_start(M[:, t % SLOTS, 0:F], None, table,
                                          bass.IndirectOffsetOnAxis(sidx[:, t:t + 1], 0))\
                        .then_inc(s_g[t % SLOTS], 16)

            def add_ln_b(lane, r, n0):
                gp.wait_ge(s_norm, r * (10 * NC) + (n0 + (4 + lane + 1) * NC))
                nc.gpsimd.tensor_tensor(LX[lane][:], LX[lane][:],
                                        LNG[:, F:2 * F].unsqueeze(1).broadcast_to([P, KT, F]),
                                        ALU.add).then_inc(s_xb, 1)

            def finish(lane, r, n0):
                gp.wait_ge(s_norm, r * (10 * NC) + (n0 + (8 + lane + 1) * NC))
                nc.gpsimd.tensor_tensor(LH[lane][:], LX[lane][:], LH[lane][:], ALU.add).then_inc(s_fin, 1)

            with gp.Fori(0, PRE) as r:
                for lane in range(2):
                    add_ln_b(lane, r, S_NORM)
                for lane in range(2):
                    finish(lane, r, S_NORM)
            gp.wait_ge(s_slot, 1)
            for k in range(1, 5):
                gp.wait_ge(s_tb, 16 * EB * k)
                gather(tab[k], 1 + k)
            place_n = {}
            for lane in range(2):
                k = tiles_by((3 + lane) * (NC + 2) + NC - 1 + 3)
                place_n[-(-(k + 4) // CH) * CH] = lane
            with gp.Fori(0, STEPS // 2) as r:
                for i in range(2):
                    gp.wait_ge(s_tb, r * (2 * 16 * EB) + 16 * EB * (5 + i))
                    gp.sem_inc(s_turn, 1)

                    def node_sums(t):
                        if i * T + t in place_n:
                            add_ln_b(place_n[i * T + t], r, NORM_N)
                    gather(tab[5 + i], 6 + i, r, node_sums)
                for lane in range(2):
                    finish(lane, r, NORM_N)
            for t in range(T):
                if t % KT == 0:
                    gp.wait_ge(s_res, t // KT + 1)
                gp.indirect_dma_start(out, bass.IndirectOffsetOnAxis(didx[:, t:t + 1], 0),
                                      HD[:, t, :], None, bounds_check=NN - 1, oob_is_err=False)\
                    .then_inc(s_out, 16)
            gp.wait_ge(s_out, 16 * T)

        def landed(g, t):
            return 16 * (g * (T // SLOTS) + t // SLOTS + 1)

        @block.scalar
        def _(act):
            c = Count()

            def norm(X, H, k0, func, slot):
                for k in range(k0 * CH, k0 * CH + CH):
                    last = A.activation(H[:, k, :], X[:, k, :], func, bias=lnv[:, slot, 1, k:k + 1],
                                        scale=lnv[:, slot, 0, k:k + 1])
                last.then_inc(s_norm, 1)

            def steps(r0, kind, lanes, batch):
                t0, a0, st0, f0 = c.t, c.a, c.stat, c.fin
                nl = len(lanes)
                for step in range(3):
                    for lane in lanes:
                        q = step * nl + lane
                        X, H = LX[lane], LH[lane]
                        if step < 2:
                            act.wait_ge(s_ln, r0(LN_OPS * 5 * nl, LN_OPS * (st0 + q + 1)))
                            if kind == "S" and (batch[lane] >= 2 or step > 0):
                                act.wait_ge(s_hl[lane], 16 * (5 * (batch[lane] // 2) + step))
                            if kind == "N" and step == 0:
                                act.wait_ge(s_hl[lane], r0(16, 16 * (5 * (3 - lane) + r0.pair)))
                        for i in range(NC + 2):
                            if i < NC and step < 2:
                                norm(X, H, i, ACT.Relu, (st0 + q) % 2)
                            if 1 <= i <= NC:
                                n = t0 + q * NC + i - 1
                                act.wait_ge(s_tp, r0(3 * nl * NC, n + 1))
                                if not (r0.first and n < 3):
                                    act.wait_ge(s_a, r0(3 * nl * NC, a0 + q * NC + i - 3))
                                A.activation(HT[0:F, n % 3, :], PT[n % 2][0:F, 0:CH * P],
                                             ACT.Relu if step == 2 else ACT.Copy).then_inc(s_tev, 1)
                            if i >= 2:
                                a_evac(a0 + q * NC + i - 2, [ACT.Relu, None, ACT.Gelu][step],
                                       ["b1", "s1", "ub"][step], r0, 3 * nl * NC,
                                       c.e + lane * NC + i - 2, nl * NC,
                                       ut_free(kind, nl, c.b, step, lane, i - 2))
                for j, func in ((3, ACT.Identity), (4, ACT.Relu)):
                    for lane in lanes:
                        st = j * nl + lane
                        act.wait_ge(s_ln, r0(LN_OPS * 5 * nl, LN_OPS * (st0 + st + 1)))
                        src = LH[lane] if j == 3 else LX[lane]
                        for i in range(NC):
                            norm(src, LH[lane], i, func, (st0 + st) % 2)

            def a_evac(n, func, bname, r0, per, e, eper, free):
                act.wait_ge(s_a, r0(per, n + 1))
                src = PA[n % 2][0:F, 0:CH * P]
                if func is None:
                    if not (r0.first and e < 2):
                        act.wait_ge(s_elu, r0(eper, e - 1))
                    A.activation(TE[0:F, e % 2, :], src, ACT.Exp, bias=bias(bname))
                    A.activation(TR[:, e % 2, :], src, ACT.Relu, bias=bias(bname)).then_inc(s_aev, 1)
                else:
                    if free is None:
                        if n - 3 >= A_D:
                            act.wait_ge(s_b, used_a[n - 3])
                    elif not (r0.first and n < 3):
                        act.wait_ge(s_b, r0(per, free))
                    A.activation(UT[0:F, n % 3, :], src, func, bias=bias(bname)).then_inc(s_aev, 1)

            act.wait_ge(s_const, 96)
            act.wait_ge(s_mapz, 32)
            act.wait_ge(s_eq, T // SB)
            for i, pair in enumerate(PAIRS):
                steps(Fixed(None, i == 0), "S", range(len(pair)), pair)
                c.b += 3 * NC * len(pair) + 2 * NC * len(pair)
                c.t += 3 * NC * len(pair)
                c.a += 3 * NC * len(pair)
                c.e += NC * len(pair)
                c.stat += 5 * len(pair)
            with act.Fori(0, PRE) as r:
                steps(Fixed(r, False), "N", range(2), None)
            c.t += N_CHUNKS
            c.a += N_CHUNKS
            c.e += PRE * 2 * NC
            c.stat += N_STAT

            one = Fixed(None, False)

            def d_norm(b, func=ACT.Relu, X=XD):
                n = c.stat - S_STAT - N_STAT
                act.wait_ge(s_ln, LN_OPS * (c.stat + 1))
                for k in range(KT):
                    t = b * KT + k
                    last = A.activation(HD[:, t, :], X[:, t, :], func, bias=lnv[:, c.stat % 2, 1, k:k + 1],
                                        scale=lnv[:, c.stat % 2, 0, k:k + 1])
                last.then_inc(s_norm, 1)
                c.stat += 1

            def d_tev(g, kind, ch):
                n = no[g, kind, ch]
                act.wait_ge(s_tp, n + 1)
                if kind == "tm":
                    if ch >= 2:
                        act.wait_ge(s_a, no[g, "ag", ch - 2] + 1)
                    A.activation(TE[:, ch % 2, :], PT[n % 2][:, 0:CH * P], ACT.Copy).then_inc(s_tev, 1)
                else:
                    if n - 3 in used_t:
                        act.wait_ge(*used_t[n - 3])
                    A.activation(HT[0:F, n % 3, :], PT[n % 2][0:F, 0:CH * P], ACT.Copy).then_inc(s_tev, 1)

            def d_aev(n, func, bname):
                a_evac(n, func, bname, one, 0, c.e, 0, None)
                if func is None:
                    c.e += 1

            def scale(g, ch):
                if g == "g1":
                    act.wait_ge(s_m0[ch % NC], 16 * (ch // NC + 1))
                for t in range(ch * CH, ch * CH + CH):
                    if g == "g2":
                        act.wait_ge(s_g[t % SLOTS], landed(0, t))
                    A.activation(M[:, t % SLOTS, 0:F], M[:, t % SLOTS, 0:F], ACT.Copy, scale=wgt[:, t:t + 1])\
                        .then_inc(s_sc, 1)

            for b in range(EB):
                d_norm(b)
            act.wait_ge(s_slot, 1)
            for g in STAGES:
                if g in ("g1", "g2"):
                    scale(g, 0)
                for seg_c, t_c, a_c, b_c, tm, am, bm in slots(g):
                    if g in ("g1", "g2") and seg_c is not None and seg_c + 1 < DC:
                        scale(g, seg_c + 1)
                    if tm is not None:
                        d_tev(g, "tm", tm)
                    if bm is not None:
                        n, k = no[g, "bg", bm], bm % NC * CH
                        act.wait_ge(s_b, n + 1)
                        if bm >= NC:
                            act.wait_ge(s_gu, bm - NC + 1)
                        A.activation(gate[:, k:k + CH], PB[n % 2][0:P, 0:CH], ACT.Tanh, scale=0.5)\
                            .then_inc(s_gate, 1)
                    if a_c is not None:
                        d_aev(no[g, "a", a_c], {"g1": ACT.Relu, "s1": None, "l2": ACT.Gelu}[g],
                              {"g1": "b1", "s1": "s1", "l2": "ub"}[g])
                    if t_c is not None:
                        if g not in ("g1", "g2"):
                            d_tev(g, "th", t_c)
                        d_tev(g, "tg", t_c)
                    if am is not None:
                        d_aev(no[g, "am", am], ACT.Gelu, "mb")
                        d_aev(no[g, "ag", am], ACT.Gelu, "gb")
                    if b_c is not None and b_c % NC == NC - 1:
                        b = b_c // NC
                        if g in ("g2", "s2"):
                            d_norm(b)
                        elif g == "l2":
                            if b >= 1:
                                d_norm(b - 1)
                            d_norm(b, ACT.Identity, HD)
            d_norm(EB - 1)
            c.t, c.a, c.b = T_N, A_N, B_N
            with act.Fori(0, STEPS // 2) as r:
                steps(Fixed(r, False, PRE), "N", range(2), None)

        @block.tensor
        def _(pe):
            c = Count()
            pe.wait_ge(s_const, 96)
            pe.wait_ge(s_init, 1)

            def segsum(rnd, t, rhs, n, reg=None):
                s = seg(rnd, t)
                pe.wait_ge(s_msg, s + 1 if reg is None else reg * (2 * T) + (s + 1))
                PE.matmul(PS[t % 2][0:P, 0:n], EQ[:, t, :], rhs, start=True, stop=True).then_inc(s_seg, 1)

            for t in range(T):
                segsum(0, t, dg[:, t, :], 2)

            def trans(n, r0, per, rows, width=F):
                if not (r0.first and n < 2):
                    pe.wait_ge(s_tev, r0(per, n - 1))
                for k in range(CH):
                    last = PE.transpose(PT[n % 2][0:width, k * P:(k + 1) * P], rows(k), ident[:])
                last.then_inc(s_tp, 1)

            def rows_out(n, r0, per, parts, cols=F):
                if not (r0.first and n < 2):
                    pe.wait_ge(s_bev, r0(per, n - 1))
                for k in range(CH):
                    for j, (l, rh) in enumerate(parts):
                        last = PE.matmul(PB[n % 2][0:P, k * cols:(k + 1) * cols], l(k), rh,
                                         start=(j == 0), stop=(j == len(parts) - 1))
                last.then_inc(s_b, 1)
                return last

            def steps(r0, kind, lanes, sums=None):
                nl = len(lanes)
                per = 3 * nl * NC
                b = c.b

                def between(k, part):
                    if sums is not None:
                        n = tiles_by(k - 1)
                        sums(n + ((tiles_by(k) - n) * part + 2) // 4)

                between(-1, 4)
                for step in range(3):
                    for lane in lanes:
                        q = step * nl + lane
                        st = c.norm + q * NC
                        for i in range(NC + 2):
                            k_ = q * (NC + 2) + i
                            if i < NC:
                                pe.wait_ge(s_norm, r0(5 * nl * NC, st + i + 1))
                                trans(c.t + q * NC + i, r0, per, lambda k: LH[lane][:, i * CH + k, :])
                            between(k_, 1)
                            if 1 <= i <= NC:
                                n = c.t + q * NC + i - 1
                                na = c.a + q * NC + i - 1
                                pe.wait_ge(s_tev, r0(per, n + 1))
                                if not (r0.first and na < 2):
                                    pe.wait_ge(s_aev, r0(per, na - 1))
                                halves = [(0, CH * P)] if sums is None else \
                                    [(0, CH * P // 2), (CH * P // 2, CH * P)]
                                for h, (c0, c1) in enumerate(halves):
                                    if h == 1:
                                        between(k_, 2)
                                    last = PE.matmul(PA[na % 2][0:F, c0:c1], w(["W1", "WR1", "UA"][step]),
                                                     HT[0:F, n % 3, c0:c1], start=True, stop=True)
                                last.then_inc(s_a, 1)
                            between(k_, 3)
                            if i >= 2:
                                na = c.a + q * NC + i - 2
                                if step == 1:
                                    pe.wait_ge(s_elu, r0(nl * NC, c.e + lane * NC + i - 1))
                                else:
                                    pe.wait_ge(s_aev, r0(per, na + 1))
                                u = lambda k, h: UT[0:h, na % 3, k * P:(k + 1) * P]
                                if kind == "S" and step < 2:
                                    rows_out(b, r0, per, [(lambda k: u(k, F), ident[0:F, 0:F])])
                                    b += 1
                                rows_out(b, r0, per, [(lambda k: u(k, F + 1), w(["W2", "WR2", "UW2"][step], F + 1))])
                                b += 1
                            between(k_, 4)
                c.b = b

            for i, pair in enumerate(PAIRS):
                nl = len(pair)
                steps(Fixed(None, i == 0), "S", range(nl))
                c.t += 3 * NC * nl
                c.a += 3 * NC * nl
                c.e += NC * nl
                c.norm += 5 * NC * nl
            with pe.Fori(0, PRE) as r:
                steps(Fixed(r, False), "N", range(2))
            c.b += N_CHUNKS - 6 * NC
            c.e += PRE * 2 * NC

            one = Fixed(None, False)

            def d_t(g, kind, ch):
                b, i = ch // NC, ch % NC
                if kind == "tm":
                    pe.wait_ge(s_attr[i], 16 * (b + 1))
                    for t in range(ch * CH, ch * CH + CH):
                        pe.wait_ge(s_g[t % SLOTS], landed(3, t))
                    trans(no[g, kind, ch], one, 0, lambda k: M[:, (i * CH + k) % SLOTS, :], F + FE)
                elif kind == "th":
                    trans(no[g, kind, ch], one, 0, lambda k: HD[:, ch * CH + k, :])
                else:
                    pe.wait_ge(s_agg, STAGES.index(g) * DC + ch + 1)
                    trans(no[g, kind, ch], one, 0, lambda k: LX[b % 2][:, i * CH + k, :])

            def d_a(n, parts):
                pe.wait_ge(s_aev, n - 1)
                for j, (wt, rhs, tn) in enumerate(parts):
                    pe.wait_ge(s_tev, tn + 1)
                    last = PE.matmul(PA[n % 2][0:F, 0:CH * P], wt, rhs, start=(j == 0), stop=(j == len(parts) - 1))
                last.then_inc(s_a, 1)

            def ring(buf, n, h):
                return lambda k: buf[0:h, n % 3, k * P:(k + 1) * P]

            for g in STAGES:
                if g in ("s1", "l2"):
                    pe.wait_ge(s_norm, NORM_D + (2 if g == "s1" else 3) * EB)
                for seg_c, t_c, a_c, b_c, tm, am, bm in slots(g):
                    if seg_c is not None:
                        for t in range(seg_c * CH, seg_c * CH + CH):
                            segsum(1 + STAGES.index(g), t, M[:, t % SLOTS, 0:F], F)
                    if tm is not None:
                        d_t(g, "tm", tm)
                    if bm is not None:
                        for x_, y_, rhs, cols in (("am", "bm", w("MW2", F + 1), F),
                                                  ("ag", "bg", W[0:F + 1, GW2:GW2 + 1], 1)):
                            an = no[g, x_, bm]
                            pe.wait_ge(s_aev, an + 1)
                            rows_out(no[g, y_, bm], one, 0, [(ring(UT, an, F + 1), rhs)], cols)
                    if b_c is not None:
                        if g in ("g1", "s1", "l2"):
                            an = no[g, "a", b_c]
                            if g == "s1":
                                pe.wait_ge(s_elu, c.e + b_c + 1)
                            else:
                                pe.wait_ge(s_aev, an + 1)
                            parts = [(ring(UT, an, F + 1), w("UW2", F + 1))] if g == "l2" else \
                                [(ring(UT, an, F), ident[0:F, 0:F])]
                        else:
                            pe.wait_ge(s_tev, no[g, "tg", b_c] + 1)
                            parts = [(ring(HT, no[g, "tg", b_c], F + 1), w("W2", F + 1))] if g == "g2" else \
                                [(ring(HT, no[g, "th", b_c], F + 1), w("WR2", F + 1)),
                                 (ring(HT, no[g, "tg", b_c], F), w("WL2"))]
                        rows_out(no[g, "b", b_c], one, 0, parts)
                    if a_c is not None:
                        parts = []
                        for x_, wn in {"g1": [("tg", "W1")], "s1": [("th", "WR1"), ("tg", "WL1")],
                                       "l2": [("th", "UA"), ("tg", "UB")]}[g]:
                            tn = no[g, x_, a_c]
                            parts.append((w(wn), HT[0:F, tn % 3, :], tn))
                        d_a(no[g, "a", a_c], parts)
                    if t_c is not None:
                        if g not in ("g1", "g2"):
                            d_t(g, "th", t_c)
                        d_t(g, "tg", t_c)
                    if am is not None:
                        for x_, wn in (("am", "MW1"), ("ag", "GW1")):
                            d_a(no[g, x_, am], [(w(wn, 128), TE[:, am % 2, :], no[g, "tm", am])])
            c.t, c.a, c.b, c.norm = T_N, A_N, B_N, NORM_N
            c.e += DC
            with pe.Fori(0, STEPS // 2) as r:
                summed = 0

                def sums(n):
                    nonlocal summed
                    for u in range(summed, n):
                        segsum(6 + u // T, u % T, M[:, u % SLOTS, 0:F], F, r)
                    summed = max(n, summed)

                steps(Fixed(r, False), "N", range(2), sums)
                sums(2 * T)

        @block.vector
        def _(dve):
            c = Count()

            def rsqrt(y, v, h):
                dve.drain()
                V.tensor_single_scalar(y.bitcast(I32), v.bitcast(I32), 1, ALU.arith_shift_right)
                dve.drain()
                V.tensor_scalar(y.bitcast(I32), y.bitcast(I32), -1.0, 1597463007.0, ALU.mult, ALU.add)
                for _ in range(3):
                    dve.drain()
                    V.scalar_tensor_tensor(out=h, in0=y, scalar=-0.5, in1=y, op0=ALU.mult, op1=ALU.mult)
                    dve.drain()
                    V.tensor_tensor(h, h, v, ALU.mult)
                    dve.drain()
                    V.scalar_tensor_tensor(out=y, in0=h, scalar=1.5, in1=y, op0=ALU.add, op1=ALU.mult)
                dve.drain()

            def ln_op(j, lane, n, r0, per):
                s_, d, v, h = (sm[:, lane, m, :] for m in range(4))
                y = lnv[:, n % 2, 0, :]
                bs = bst[:, lane, :, :]
                if j == 0:
                    dve.wait_ge(s_bn, r0(per * NC, (n + 1) * NC))
                if n or j:
                    dve.wait_ge(s_ln, r0(per * LN_OPS, n * LN_OPS + j))
                if j == 0:
                    op = V.tensor_tensor(s_, bs[:, :, 1], bs[:, :, 4], ALU.add)
                elif j == 1:
                    op = V.tensor_tensor(d, bs[:, :, 1], bs[:, :, 4], ALU.subtract)
                elif j == 2:
                    op = V.tensor_tensor(v, bs[:, :, 2], bs[:, :, 5], ALU.add)
                elif j == 3:
                    op = V.scalar_tensor_tensor(out=d, in0=d, scalar=0.25, in1=d, op0=ALU.mult, op1=ALU.mult)
                elif j == 4:
                    op = V.tensor_scalar(v, v, 1.0 / F, EPS, ALU.mult, ALU.add)
                elif j == 5:
                    op = V.tensor_tensor(v, v, d, ALU.add)
                elif j == 6:
                    op = V.tensor_single_scalar(y.bitcast(I32), v.bitcast(I32), 1, ALU.arith_shift_right)
                elif j == 7:
                    op = V.tensor_scalar(y.bitcast(I32), y.bitcast(I32), -1.0, 1597463007.0, ALU.mult, ALU.add)
                elif j == LN_OPS - 1:
                    op = V.scalar_tensor_tensor(out=lnv[:, n % 2, 1, :], in0=s_, scalar=-0.5, in1=y, op0=ALU.mult,
                                                op1=ALU.mult)
                elif j % 3 == 2:
                    op = V.scalar_tensor_tensor(out=h, in0=y, scalar=-0.5, in1=y, op0=ALU.mult, op1=ALU.mult)
                elif j % 3 == 0:
                    op = V.tensor_tensor(h, h, v, ALU.mult)
                else:
                    op = V.scalar_tensor_tensor(out=y, in0=h, scalar=1.5, in1=y, op0=ALU.add, op1=ALU.mult)
                op.then_inc(s_ln, 1)

            def bn_chunk(X, lane, i, r0, per, other=None, first=0, count=0, beat=None):
                for k in range(CH):
                    last = V.bn_stats(bst[:, lane, i * CH + k, :], X[:, i * CH + k, :])
                    if k == CH - 1:
                        last.then_inc(s_bn, 1)
                    if other is not None:
                        for j in range(first + count * k // CH, first + count * (k + 1) // CH):
                            ln_op(j, *other, r0, per)
                    if beat is not None:
                        beat(k + 2)

            def elu(e, u, r0, eper, uper, free):
                dve.wait_ge(s_aev, r0(uper, u + 1))
                if free is None:
                    if u - 3 >= A_D:
                        dve.wait_ge(s_b, used_a[u - 3])
                else:
                    dve.wait_ge(s_b, r0(uper, free))
                V.tensor_scalar(TE[0:F, e % 2, :], TE[0:F, e % 2, :], 1.0, -1.0, ALU.min, ALU.add)\
                    .then_inc(s_eh, 1)
                dve.wait_ge(s_eh, r0(eper, e + 1))
                V.tensor_tensor(UT[0:F, u % 3, :], TE[0:F, e % 2, :], TR[:, e % 2, :], ALU.add).then_inc(s_elu, 1)

            def pb(n, cols=F):
                return PB[n % 2][0:P, 0:CH * cols].rearrange("p (k f) -> p k f", k=CH)

            def affine(X, H, shift, beat=None):
                gb = [LNG[:, j * F:(j + 1) * F].unsqueeze(1).broadcast_to([P, KT, F]) for j in range(2)]
                step = KT if beat is None else CH
                for k in range(0, KT, step):
                    V.tensor_tensor(H[:, k:k + step, :], H[:, k:k + step, :], gb[0][:, k:k + step, :], ALU.mult)
                    if beat is not None:
                        beat(1)
                if shift:
                    V.tensor_tensor(X, X, gb[1], ALU.add)
                dve.drain()
                for k in range(0, KT, step):
                    V.tensor_tensor(X[:, k:k + step, :], X[:, k:k + step, :], H[:, k:k + step, :], ALU.add)
                    if beat is not None:
                        beat(1)
                dve.drain()

            V.memset(HT[F:F + 1, :, :], 1.0)
            V.memset(LH[0][:, 0:5, :], 0.0).then_inc(s_zero, 1)
            V.memset(UT[F:F + 1, :, :], 1.0).then_inc(s_init, 1)
            dve.wait_ge(s_const, 96)
            V.tensor_copy(ef[:], ei[:])
            dve.drain()
            V.tensor_tensor(rep[:], ef[:, 2, :], ef[:, 1, :], ALU.not_equal)
            V.tensor_tensor(carry[:], ef[:, 3, :], ef[:, 1, :], ALU.is_equal)
            dve.drain()
            V.tensor_tensor(carry[:], carry[:], first, ALU.mult)
            for b in range(T // SB):
                dve.wait_ge(s_bc[b], 16)
                for k in range(SB):
                    t = b * SB + k
                    last = V.tensor_scalar(EQ[:, t, :], spread(b)[:, k * P:(k + 1) * P].bitcast(I32),
                                           ef[:, 1, t:t + 1], None, ALU.is_equal)
                last.then_inc(s_eq, 1)

            wcol = slotf
            V.tensor_copy(wcol[:], dg[:, :, 1])
            dve.drain()
            V.tensor_scalar(dg[:, 0, :], dg[:, 0, :], 1.0, None, ALU.mult).then_inc(s_msg, 1)
            for t in range(T):
                dve.wait_ge(s_seg, seg(0, t) + 1)
                if t + 1 < T:
                    V.scalar_tensor_tensor(out=dg[:, t + 1, :], in0=PS[t % 2][0:P, 0:2], scalar=carry[:, t + 1:t + 2],
                                           in1=dg[:, t + 1, :], op0=ALU.mult, op1=ALU.add).then_inc(s_msg, 1)
                V.tensor_copy(dg[:, t, :], PS[t % 2][0:P, 0:2])
            dve.drain()
            V.reciprocal(icnt[:], dg[:, :, 0])
            degw, degc = sqd[:], asc[:]
            V.tensor_scalar(degw, dg[:, :, 1], 1.0, None, ALU.add)
            V.tensor_scalar(degc, dg[:, :, 0], 1.0, None, ALU.add)
            dve.drain()
            V.tensor_scalar(wgt[:], degw, 0.0, None, ALU.is_gt)
            V.tensor_scalar(degw, degw, 1e-30, None, ALU.max)
            rsqrt(dw[:, 0, :], degw, ef[:, 2, :])
            V.tensor_tensor(dw[:, 0, :], dw[:, 0, :], wgt[:], ALU.mult)
            rsqrt(dw[:, 1, :], degc, ef[:, 2, :])
            V.tensor_tensor(selfc[:, 0, :], dw[:, 0, :], rep[:], ALU.mult)
            V.tensor_tensor(sqd[:], degc, dw[:, 1, :], ALU.mult)
            V.reciprocal(ef[:, 3, :], degc)
            dve.drain()
            V.tensor_scalar(asc[:], ef[:, 3, :], 1.0 - ALPHA, None, ALU.mult)
            V.tensor_copy(mrow[:, :, 1], dw[:, 0, :])
            V.tensor_copy(mrow[:, :, 0], slot1)
            V.tensor_scalar(ef[:, 2, :], ef[:, 1, :], -FAR, None, ALU.add)
            dve.drain()
            V.tensor_tensor(ef[:, 2, :], ef[:, 2, :], rep[:], ALU.mult)
            dve.drain()
            V.tensor_scalar(didx[:], ef[:, 2, :], FAR, None, ALU.add).then_inc(s_deg, 1)

            def b_use(n, r0, per, kind, X, H, i, to=None):
                dve.wait_ge(s_b, r0(per, n + 1))
                ks = slice(i * CH, (i + 1) * CH)
                if kind == "row":
                    op = V.tensor_copy(to[:, ks, :], pb(n))
                elif kind == "relu":
                    op = V.scalar_tensor_tensor(out=X[:, ks, :], in0=pb(n), scalar=0.0, in1=X[:, ks, :],
                                                op0=ALU.max, op1=ALU.add)
                elif kind == "add":
                    op = V.tensor_tensor(X[:, ks, :], pb(n), X[:, ks, :], ALU.add)
                else:
                    op = V.scalar_tensor_tensor(out=H[:, ks, :], in0=H[:, ks, :], scalar=0.0, in1=pb(n),
                                                op0=ALU.max, op1=ALU.add)
                op.then_inc(s_bev, 1)
                return op

            def steps(r0, kind, lanes, batch, row0, sums=None):
                nl = len(lanes)
                per = 3 * nl * NC
                lnper = 5 * nl
                b = c.b
                row = row0

                def ln_rest(st, lane, j0=0, n0=0, n1=0):
                    for j in range(j0, LN_OPS):
                        ln_op(j, lane, c.stat + st, r0, lnper)
                        if sums is not None:
                            sums(n0 + (n1 - n0) * (j + 1) // LN_OPS)

                def norm3(lane, beat=None):
                    X, H, slot = LX[lane], LH[lane], (c.stat + 2 * nl + lane) % 2
                    if kind == "S":
                        dve.wait_ge(s_hl[lane], 16 * (5 * (batch[lane] // 2) + 2))
                    dve.wait_ge(s_ln, r0(lnper * LN_OPS, LN_OPS * (c.stat + 2 * nl + lane + 1)))
                    for k in range(KT):
                        op = V.tensor_scalar(H[:, k, :], X[:, k, :], lnv[:, slot, 0, k:k + 1],
                                             lnv[:, slot, 1, k:k + 1], ALU.mult, ALU.add)
                        if kind == "N" and k % CH == CH - 1:
                            op.then_inc(s_norm, 1)
                        if beat is not None and k % 4 == 3:
                            beat(2 + k // 5)
                    if kind == "S":
                        dve.drain()
                        V.tensor_scalar(H[:], H[:], 0.0, None, ALU.max).then_inc(s_norm, NC)

                for lane in lanes:
                    if kind == "S":
                        dve.wait_ge(s_xg[lane], 16 * KT * (batch[lane] // 2 + 1))
                    else:
                        dve.wait_ge(s_xl[lane], r0(16, 16 * (r0.pair + 1)))
                    for i in range(NC):
                        other = (0, c.stat) if lane == 1 else None
                        bn_chunk(LX[lane], lane, i, r0, lnper, other, 4 * i if i < 4 else 16, 4 if i < 4 else 2)
                        if sums is not None and lane == 1:
                            sums(LEAD * (i + 1) // NC)
                    if nl == 1:
                        ln_rest(0, 0)
                for step in range(3):
                    for lane in lanes:
                        q = step * nl + lane
                        X, H = LX[lane], LH[lane]
                        hidden = kind == "S" and step < 2
                        st = q + nl - 1
                        if hidden and row > 0:
                            dve.wait_ge(s_rst, 16 * row)
                        if kind == "S" and step == 2:
                            dve.wait_ge(s_hl[lane], 16 * (5 * (batch[lane] // 2) + 3))
                        for i in range(NC + 1):
                            k_ = q * (NC + 2) + i
                            n0, n1 = tiles_by(k_ + 1), tiles_by(k_ + 2 + (i == NC))

                            def beat(part):
                                sums(n0 + (n1 - n0) * part // 6)

                            if step == 1 and i < NC:
                                elu(c.e + lane * NC + i, c.a + q * NC + i, r0, nl * NC, per,
                                    ut_free(kind, nl, c.b, step, lane, i))
                            if i == 0 and nl == 2 and step == 0 and lane == 0:
                                ln_rest(1, 1, 0, LEAD, n0)
                            if i >= 1:
                                if hidden:
                                    b_use(b, r0, per, "row", X, H, i - 1, R)
                                    b += 1
                                b_use(b, r0, per, ["relu", "add", "hid"][step], X, H, i - 1)
                                b += 1
                                if sums is not None:
                                    beat(1)
                                dve.wait_ge(s_bev, r0(per, b))
                                other, j0, cnt = None, 0, 0
                                if nl == 2 and not (step == 0 and lane == 0) and i <= 3:
                                    other, j0, cnt = (1 - lane, c.stat + st), 6 * (i - 1), 6
                                bn_chunk(H if step == 2 else X, lane, i - 1, r0, lnper, other, j0, cnt,
                                         None if sums is None or (i == 4 and st // nl == 2) else beat)
                                if i == 4 and nl == 2 and st // nl == 2:
                                    norm3(1 - lane, None if sums is None else beat)
                            if sums is not None:
                                beat(6)
                        if hidden:
                            dve.drain().then_inc(s_row, 1)
                            row += 1
                        if nl == 1:
                            ln_rest(q + 1, 0)
                            if step == 1:
                                norm3(0)
                end = 0

                def end_beat(n):
                    nonlocal end
                    end += n
                    if sums is not None:
                        sums(2 * T - TAIL - END + min(end, END))

                if nl == 2:
                    ln_rest(7, 1, 0, 2 * T - TAIL - END, 2 * T - TAIL - END + 4)
                    end = 4
                for lane in lanes:
                    X, H = LX[lane], LH[lane]
                    dve.wait_ge(s_norm, r0(5 * nl * NC, c.norm + (3 * nl + lane + 1) * NC))
                    if kind == "N":
                        dve.wait_ge(s_xb, r0(2, 2 * r0.pair + lane + 1))
                    affine(X[:], H[:], kind == "S", None if sums is None else end_beat)
                    for i in range(NC):
                        other = (0, c.stat + 4 * nl) if lane == 1 else None
                        bn_chunk(X, lane, i, r0, lnper, other, 4 * i if i < 4 else 16, 4 if i < 4 else 2)
                        end_beat(1 + lane)
                    if lane == nl - 1:
                        ln_rest(4 * nl + lane, lane, 0, 2 * T - TAIL - 4, 2 * T - TAIL)
                if kind == "S":
                    for lane in lanes:
                        dve.wait_ge(s_norm, c.norm + (4 * nl + lane + 1) * NC)
                        dve.sem_inc(s_fin, 1)
                c.b = b
                return row

            row = 0
            for i, pair in enumerate(PAIRS):
                nl = len(pair)
                row = steps(Fixed(None, i == 0), "S", range(nl), pair, row)
                c.a += 3 * NC * nl
                c.e += NC * nl
                c.stat += 5 * nl
                c.norm += 5 * NC * nl
                if i == 1:
                    dve.wait_ge(s_mapg, 16 * T)
                    has, own = ef[:, 3, :], ef[:, 2, :]
                    V.tensor_scalar(has, mg[:, :, 0], 1.0, None, ALU.min)
                    V.tensor_scalar(own, slot1, -1.0, -float(NE), ALU.mult, ALU.add)
                    dve.drain()
                    V.tensor_tensor(own, own, has, ALU.mult)
                    V.tensor_tensor(wgt[:], mg[:, :, 1], has, ALU.subtract)
                    dve.drain()
                    V.tensor_tensor(own, own, mg[:, :, 0], ALU.add)
                    V.scalar_tensor_tensor(out=wgt[:], in0=wgt[:], scalar=1.0, in1=wcol[:], op0=ALU.add, op1=ALU.mult)
                    dve.drain()
                    V.tensor_tensor(own, own, slot1, ALU.add)
                    dve.drain()
                    V.tensor_scalar(own, own, float(NE - 1), None, ALU.add)
                    dve.drain()
                    V.tensor_copy(sidx[:], own).then_inc(s_slot, 1)
            with dve.Fori(0, PRE) as r:
                steps(Fixed(r, False), "N", range(2), None, 0)
            c.b += N_CHUNKS - 6 * NC
            c.a += N_CHUNKS
            c.e += PRE * 2 * NC
            c.stat += N_STAT

            one = Fixed(None, False)

            LN_D = S_STAT + N_STAT
            assert c.stat == LN_D

            def d_ln(X, b):
                n = c.stat
                if n - 2 >= LN_D:
                    dve.wait_ge(s_norm, NORM_D + n - 2 - LN_D + 1)
                for i in range(NC):
                    bn_chunk(X[:, b * KT:(b + 1) * KT, :], n % 2, i, one, 0)
                for j in range(LN_OPS):
                    ln_op(j, n % 2, n, one, 0)
                c.stat += 1

            def chain(rnd, t0, t1, arrive, selfcoef, outscale, dest, addend=None, reg=None, selfrow=None):
                def at(n):
                    return n if reg is None else reg * (2 * T) + n

                def own(t):
                    arrive(t)
                    if selfcoef is not None:
                        V.scalar_tensor_tensor(out=M[:, t % SLOTS, 0:F], in0=HD[:, t, :], scalar=selfcoef[:, t:t + 1],
                                               in1=M[:, t % SLOTS, 0:F], op0=ALU.mult, op1=ALU.add)

                def leave(t):
                    src = PS[t % 2][0:P, 0:F]
                    if addend is not None:
                        return V.scalar_tensor_tensor(out=dest(t), in0=src, scalar=outscale[:, t:t + 1],
                                                      in1=addend[:, t, :], op0=ALU.mult, op1=ALU.add)
                    if outscale is None:
                        return V.tensor_copy(dest(t), src)
                    return V.tensor_scalar(dest(t), src, outscale[:, t:t + 1], None, ALU.mult)

                own(t0)
                for t in range(t0, t1):
                    if t + 1 < t1:
                        own(t + 1)
                    m = M[:, t % SLOTS, 0:F]
                    if t == t0:
                        dve.drain()
                    if t == 0:
                        V.tensor_scalar(m, m, 1.0, None, ALU.mult).then_inc(s_msg, 1)
                    else:
                        dve.wait_ge(s_seg, at(seg(rnd, t)))
                        V.scalar_tensor_tensor(out=m, in0=PS[(t - 1) % 2][0:P, 0:F], scalar=carry[:, t:t + 1], in1=m,
                                               op0=ALU.mult, op1=ALU.add).then_inc(s_msg, 1)
                    if t > t0:
                        leave(t - 1)
                dve.wait_ge(s_seg, at(seg(rnd, t1 - 1) + 1))
                return leave(t1 - 1)

            def agg(b):
                return lambda t: LX[b % 2][:, t - b * KT, :]

            dve.wait_ge(s_xd, 16 * T)
            dve.wait_ge(s_norm, NORM_D)
            for b in range(EB):
                d_ln(XD, b)
            dve.wait_ge(s_norm, NORM_D + EB)
            CONV = {
                "g1": (lambda t: dve.wait_ge(s_sc, t + 1), selfc[:, 0, :], dw[:, 0, :]),
                "g2": (lambda t: dve.wait_ge(s_sc, T + t + 1), selfc[:, 0, :], dw[:, 0, :]),
                "s1": (lambda t: dve.wait_ge(s_g[t % SLOTS], landed(1, t)), None, icnt[:]),
                "s2": (lambda t: dve.wait_ge(s_g[t % SLOTS], landed(2, t)), None, icnt[:]),
                "l2": (lambda t: None, None, None),
            }
            for g in STAGES:
                for seg_c, t_c, a_c, b_c, tm, am, bm in slots(g):
                    if seg_c is not None:
                        chain(1 + STAGES.index(g), seg_c * CH, seg_c * CH + CH, *CONV[g], agg(seg_c // NC))\
                            .then_inc(s_agg, 1)
                    if g == "s1" and a_c is not None:
                        elu(c.e + a_c, no[g, "a", a_c], one, 0, 0, None)
                    if bm is not None:
                        k0, n = bm % NC * CH, no[g, "bm", bm]
                        dve.wait_ge(s_gate, bm + 1)
                        V.tensor_scalar(gate[:, k0:k0 + CH], gate[:, k0:k0 + CH], 0.5, 0.5, ALU.mult, ALU.add)
                        dve.drain()
                        for k in range(CH):
                            last = V.tensor_scalar(M[:, k0 + k, 0:F], pb(n)[:, k, :], gate[:, k0 + k:k0 + k + 1],
                                                   None, ALU.mult)
                        last.then_inc(s_bev, 2)
                        dve.drain().then_inc(s_gu, 1)
                    if b_c is not None:
                        b, i = b_c // NC, b_c % NC
                        rows = slice(b * KT, (b + 1) * KT)
                        b_use(no[g, "b", b_c], one, 0, {"g1": "row", "g2": "relu", "s1": "row", "s2": "add",
                                                        "l2": "hid"}[g], XD[:, rows, :], HD[:, rows, :], i,
                              HD[:, rows, :])
                        if i == NC - 1:
                            if g in ("g1", "s1"):
                                dve.drain().then_inc(s_hd, 1)
                            elif g in ("g2", "s2"):
                                dve.drain()
                                d_ln(XD, b)
                            else:
                                if b >= 1:
                                    dve.wait_ge(s_norm, NORM_D + 3 * EB + 2 * (b - 1) + 1)
                                    prev = slice((b - 1) * KT, b * KT)
                                    affine(XD[:, prev, :], HD[:, prev, :], True)
                                    d_ln(XD, b - 1)
                                else:
                                    dve.drain()
                                d_ln(HD, b)
            dve.wait_ge(s_norm, NORM_D + 5 * EB - 1)
            prev = slice((EB - 1) * KT, EB * KT)
            affine(XD[:, prev, :], HD[:, prev, :], True)
            d_ln(XD, EB - 1)
            dve.wait_ge(s_norm, NORM_D + 5 * EB)
            for b in range(EB):
                hs = HD[:, b * KT:(b + 1) * KT, :]
                V.tensor_tensor(hs, hs, dw[:, 1, b * KT:(b + 1) * KT].unsqueeze(2).broadcast_to([P, KT, F]), ALU.mult)\
                    .then_inc(s_hd, 1)
            dve.drain().then_inc(s_x3r, 1)
            dve.wait_ge(s_x3, 16)
            V.tensor_scalar(XD[:], HD[:], ALPHA, None, ALU.mult)
            dve.drain()
            c.a, c.b, c.norm = A_N, B_N, NORM_N
            c.e += DC
            with dve.Fori(0, STEPS // 2) as r:
                summed = 0

                def appnp_tile(i, t):
                    def own(t):
                        dve.wait_ge(s_g[t % SLOTS], r * (2 * 16 * (T // SLOTS)) + landed(4 + i, t))
                        V.scalar_tensor_tensor(out=M[:, t % SLOTS, 0:F], in0=HD[:, t, :], scalar=rep[:, t:t + 1],
                                               in1=M[:, t % SLOTS, 0:F], op0=ALU.mult, op1=ALU.add)

                    def leave(t):
                        op = V.scalar_tensor_tensor(out=HD[:, t, :], in0=PS[t % 2][0:P, 0:F], scalar=asc[:, t:t + 1],
                                                    in1=XD[:, t, :], op0=ALU.mult, op1=ALU.add)
                        if t % KT == KT - 1:
                            op.then_inc(s_hd, 1)

                    m = M[:, t % SLOTS, 0:F]
                    if t == 0:
                        own(0)
                    if t + 1 < T:
                        own(t + 1)
                    if t == 0:
                        dve.drain()
                        V.tensor_scalar(m, m, 1.0, None, ALU.mult).then_inc(s_msg, 1)
                    else:
                        dve.wait_ge(s_seg, r * (2 * T) + seg(6 + i, t))
                        V.scalar_tensor_tensor(out=m, in0=PS[(t - 1) % 2][0:P, 0:F], scalar=carry[:, t:t + 1], in1=m,
                                               op0=ALU.mult, op1=ALU.add).then_inc(s_msg, 1)
                        leave(t - 1)
                    if t == T - 1:
                        dve.wait_ge(s_seg, r * (2 * T) + (seg(6 + i, t) + 1))
                        leave(t)

                def sums(n):
                    nonlocal summed
                    for u in range(summed, n):
                        appnp_tile(u // T, u % T)
                    summed = max(n, summed)

                steps(Fixed(r, False, PRE), "N", range(2), None, 0, sums)
                sums(2 * T)
            dve.wait_ge(s_x3, 32)
            for t in range(T):
                last = V.scalar_tensor_tensor(out=HD[:, t, :], in0=HD[:, t, :], scalar=sqd[:, t:t + 1], in1=XD[:, t, :],
                                              op0=ALU.mult, op1=ALU.add)
                if t % KT == KT - 1:
                    last.then_inc(s_res, 1)


def kernel(**inputs):
    import numpy as np
    import concourse.bacc as bacc
    from concourse.bass_utils import run_bass_kernel_spmd as run

    a = {k: np.asarray(v) for k, v in inputs.items()}

    def tiles(v):
        v = v.reshape((T, P) + v.shape[1:]).copy()
        v[1::2] = v[1::2, ::-1]
        return np.ascontiguousarray(np.swapaxes(v, 0, 1))

    src, dst = a["src"], a["dst"]
    no = np.full(1, -1, dst.dtype)
    nxt, prv = np.concatenate([dst[1:], no]), np.concatenate([no, dst[:-1]])
    wts = np.zeros((128, WCOLS), np.float32)

    def put(name, m, b=None):
        wts[0:m.shape[0], WC[name]:WC[name] + F] = m
        if b is not None:
            wts[F, WC[name]:WC[name] + F] = b

    put("W1", a["L0_gnn_W1"])
    put("W2", a["L0_gnn_W2"], a["L0_gnn_b2"])
    put("WR1", a["L1_gnn_W1r"].T)
    put("WL1", a["L1_gnn_W1l"].T)
    put("WR2", a["L1_gnn_W2r"].T, a["L1_gnn_b2"])
    put("WL2", a["L1_gnn_W2l"].T)
    put("MW1", a["L2_gnn_mW1"])
    put("MW2", a["L2_gnn_mW2"], a["L2_gnn_mb2"])
    put("GW1", a["L2_gnn_gW1"])
    put("UA", a["L2_gnn_uW1"][:F])
    put("UB", a["L2_gnn_uW1"][F:])
    put("UW2", a["L2_gnn_uW2"], a["L2_gnn_ub2"])
    wts[0:F, GW2], wts[F, GW2] = a["L2_gnn_gW2"][:, 0], a["L2_gnn_gb2"][0]
    for n, k in (("b1", "L0_gnn_b1"), ("s1", "L1_gnn_b1"), ("mb", "L2_gnn_mb1"), ("gb", "L2_gnn_gb1"),
                 ("ub", "L2_gnn_ub1")):
        wts[0:F, BC[n]] = a[k]
    first = np.zeros((P, T), np.float32)
    first[0, 0::2] = 1
    first[P - 1, 1::2] = 1
    place = np.stack([first, np.arange(1, NE + 1, dtype=np.float32).reshape(P, T)], 1)
    arrays = {
        "x": a["x"],
        "edges": np.stack([tiles(v) for v in (src, dst, nxt, prv)]),
        "ew": np.stack([np.ones((P, T), np.float32), tiles(a["edge_weight"])], 2),
        "dst_rows": np.ascontiguousarray(tiles(dst).T).reshape(-1),
        "attr": tiles(a["edge_attr_32"]),
        "wts": wts,
        "lnp": np.concatenate([a["L2_gnn_ln_g"], a["L2_gnn_ln_b"]]),
        "ident": np.eye(P, dtype=np.float32),
        "place": np.ascontiguousarray(place),
    }
    nc = bacc.Bacc("TRN2", target_bir_lowering=False, num_devices=1)
    args = [nc.dram_tensor(f"in_{k}", v.shape, mybir.dt.from_np(v.dtype), kind="ExternalInput").ap()
            for k, v in arrays.items()]
    args.append(nc.dram_tensor("out", (NN, F), F32, kind="ExternalOutput").ap())
    gnn_kernel(nc, *args)
    r = run(nc, [{f"in_{k}": v for k, v in arrays.items()}], core_ids=[0])
    return r.results[0]["out"]
```

```python
import concourse.bass as bass
from concourse import mybir
from contextlib import ExitStack

F32 = mybir.dt.float32
I32 = mybir.dt.int32
ALU = mybir.AluOpType
ACT = mybir.ActivationFunctionType

P = 125
F = 96
FE = 32
NN = 50000
NE = 12500
T = NE // P
KT = 20
CH = 4
NC = KT // CH
EB = T // KT
NB = NN // P // KT
SLOTS = 20
STEPS = 16
ALPHA = 0.1
EPS = 1e-5
FAR = float(1 << 20)

WN = ["W1", "W2", "WR1", "WL1", "WR2", "WL2", "MW1", "MW2", "GW1", "UA", "UB", "UW2"]
WC = {n: i * F for i, n in enumerate(WN)}
GW2 = len(WN) * F
BC = {n: GW2 + 1 + i for i, n in enumerate(["b1", "s1", "mb", "gb", "ub"])}
WCOLS = GW2 + 6
ED = ["src", "dst", "nxt", "prv"]


def gnn_kernel(nc, x, edges, ew, dst_rows, attr, wts, lnp, ident_in, place, out):
    ctx = ExitStack()
    with ctx:
        def sb(name, shape, dt=F32):
            return ctx.enter_context(nc.sbuf_tensor(name, shape, dt))

        def sem(name):
            return ctx.enter_context(nc.semaphore(name))

        def dram(name, shape):
            return nc.dram_tensor(name, shape, F32).ap()

        V, A, PE = nc.vector, nc.scalar, nc.tensor

        EQ = sb("EQ", [P, T, P])
        XD = sb("XD", [P, T, F])
        HD = sb("HD", [P, T, F])
        M = sb("M", [P, SLOTS, F + FE])
        LX = [sb(f"LX{i}", [P, KT, F]) for i in range(2)]
        LH = [sb(f"LH{i}", [P, KT, F]) for i in range(2)]
        R = M[:].rearrange("p s f -> p (s f)")[:, 0:KT * F].rearrange("p (k f) -> p k f", k=KT)
        HT = sb("HT", [F + 1, 3, CH * P])
        UT = sb("UT", [F + 1, 3, CH * P])
        TE = sb("TE", [128, 2, CH * P])
        TR = sb("TR", [F, 2, CH * P])
        W = sb("W", [128, WCOLS])
        LNG = sb("LNG", [P, 2 * F])
        ident = sb("ident", [P, P])
        ei = sb("ei", [P, 4, T], I32)
        ef = sb("ef", [P, 4, T])
        wgt = sb("wgt", [P, T])
        plc = sb("plc", [P, 2, T])
        first, slot1 = plc[:, 0, :], plc[:, 1, :]
        rep = sb("rep", [P, T])
        carry = sb("carry", [P, T])
        dg = sb("dg", [P, T, 2])
        dw = sb("dw", [P, 2, T])
        selfc = sb("selfc", [P, 2, T])
        icnt = sb("icnt", [P, T])
        asc = sb("asc", [P, T])
        sqd = sb("sqd", [P, T])
        mrow = sb("mrow", [P, T, 2])
        mg = sb("mg", [P, T, 2])
        slotf = sb("slotf", [P, T])
        sidx = sb("sidx", [P, T], I32)
        didx = sb("didx", [P, T], I32)
        gate = sb("gate", [P, KT])
        bst = sb("bst", [P, 2, KT, 6])
        sm = sb("sm", [P, 2, 4, KT])
        lnv = sb("lnv", [P, 2, 2, KT])
        SB = 25

        def spread(b):
            return HD[:].rearrange("p t f -> p (t f)")[:, b % 3 * SB * P:(b % 3 + 1) * SB * P]

        PT = [ctx.enter_context(nc.psum_tensor(f"PT{i}", [128, 512], F32)) for i in range(2)]
        PA = [ctx.enter_context(nc.psum_tensor(f"PA{i}", [128, 512], F32)) for i in range(2)]
        PB = [ctx.enter_context(nc.psum_tensor(f"PB{i}", [128, 512], F32)) for i in range(2)]
        PS = [ctx.enter_context(nc.psum_tensor(f"PS{i}", [128, 512], F32)) for i in range(2)]

        tab = [dram(f"tab{k}", [2 * NE, F]) for k in range(7)]
        nmap = dram("nmap", [NN, 2])
        tabD = [t[0:NE, :].rearrange("(p t) f -> p t f", t=T) for t in tab]
        tabS = [t[NE:2 * NE, :].rearrange("(p t) f -> p t f", t=T) for t in tab]
        x3 = dram("x3", [NE, F]).rearrange("(p t) f -> p t f", t=T)
        xb = x.rearrange("(b p k) f -> b p k f", p=P, k=KT)
        ob = out.rearrange("(b p k) f -> b p k f", p=P, k=KT)

        s_const = sem("s_const")
        s_bc = [sem(f"s_bc{b}") for b in range(T // SB)]
        s_eq = sem("s_eq")
        s_init = sem("s_init")
        s_zero = sem("s_zero")
        s_mapz = sem("s_mapz")
        s_deg = sem("s_deg")
        s_maps = sem("s_maps")
        s_mapg = sem("s_mapg")
        s_slot = sem("s_slot")
        s_xg = [sem(f"s_xg{i}") for i in range(2)]
        s_xc = [sem(f"s_xc{i}") for i in range(2)]
        s_xs = [sem(f"s_xs{b}") for b in range(EB)]
        s_xd = sem("s_xd")
        s_xl = [sem(f"s_xl{i}") for i in range(2)]
        s_hl = [sem(f"s_hl{i}") for i in range(2)]
        s_bn = sem("s_bn")
        s_ln = sem("s_ln")
        s_xb = sem("s_xb")
        s_norm = sem("s_norm")
        s_tp = sem("s_tp")
        s_tev = sem("s_tev")
        s_a = sem("s_a")
        s_aev = sem("s_aev")
        s_eh = sem("s_eh")
        s_elu = sem("s_elu")
        s_b = sem("s_b")
        s_bev = sem("s_bev")
        s_fin = sem("s_fin")
        s_row = sem("s_row")
        s_rst = sem("s_rst")
        s_m0 = [sem(f"s_m0{i}") for i in range(NC)]
        s_attr = [sem(f"s_attr{i}") for i in range(NC)]
        s_g = [sem(f"s_g{i}") for i in range(SLOTS)]
        s_turn = sem("s_turn")
        s_sc = sem("s_sc")
        s_msg = sem("s_msg")
        s_seg = sem("s_seg")
        s_left = sem("s_left")
        s_agg = sem("s_agg")
        s_hd = sem("s_hd")
        s_gate = sem("s_gate")
        s_gu = sem("s_gu")
        s_tb = sem("s_tb")
        s_x3r = sem("s_x3r")
        s_x3 = sem("s_x3")
        s_x3l = [sem(f"s_x3l{b}") for b in range(EB)]
        s_res = sem("s_res")
        s_out = sem("s_out")
        block = ctx.enter_context(nc.Block())

        def lane_rows(view, b):
            return view[bass.ds(b, 1)].rearrange("o p k f -> (o p) k f")

        def w(name, k=F):
            return W[0:k, WC[name]:WC[name] + F]

        def bias(name):
            return W[0:F, BC[name]:BC[name] + 1]

        PRE = NB // 2 - STEPS // 2
        S_CHUNKS = EB * 3 * NC
        N_CHUNKS = PRE * 2 * 3 * NC
        S_ROWS = EB * 2 * NC
        S_NORM = EB * 5 * NC
        S_STAT, N_STAT = EB * 5, PRE * 2 * 5
        NORM_D = S_NORM + PRE * 10 * NC
        NORM_N = NORM_D + 5 * EB

        LN_OPS = 18

        class Count:

            def __init__(self):
                self.t = self.a = self.b = self.e = self.stat = self.norm = 0

        class Fixed:

            def __init__(self, reg, first, pair=0):
                self.reg, self.first, self.pair = reg, first, pair

            def __call__(self, per, base):
                return base if self.reg is None else self.reg * per + base

        A_D = S_CHUNKS + N_CHUNKS
        B_D = S_CHUNKS + S_ROWS + N_CHUNKS

        LAGS = {"g1": 0, "g2": 0, "s1": 0, "s2": 0, "l2": 3}
        STAGES = list(LAGS)
        DC = T // CH

        def plan():
            t = a = A_D
            b = B_D
            no, used_t, used_a = {}, {}, {}
            for g in STAGES:
                lag = LAGS[g]
                last = 2 if g in ("g2", "s2") else 3
                for s in range(DC + lag + last + 1):
                    msg, c_t, c_a, c_b = s, s - lag - 1, s - lag - 2, s - lag - last
                    if g == "l2" and 0 <= s - 2 < DC:
                        no[g, "bm", s - 2] = b
                        used_a[no[g, "am", s - 2]] = used_a[no[g, "ag", s - 2]] = b + 1
                        b += 1
                    if 0 <= c_b < DC:
                        no[g, "b", c_b] = b
                        if last == 3:
                            used_a[no[g, "a", c_b]] = b + 1
                        else:
                            for j in "hg":
                                if (g, "t" + j, c_b) in no:
                                    used_t[no[g, "t" + j, c_b]] = (s_b, b + 1)
                        b += 1
                    if last == 3 and 0 <= c_a < DC:
                        no[g, "a", c_a] = a
                        for j in "hg":
                            if (g, "t" + j, c_a) in no:
                                used_t[no[g, "t" + j, c_a]] = (s_a, a + 1)
                        a += 1
                    if 0 <= c_t < DC:
                        for j in ("h", "g")[g in ("g1", "g2"):]:
                            no[g, "t" + j, c_t] = t
                            t += 1
                    if g == "l2" and 0 <= s - 1 < DC:
                        no[g, "am", s - 1], no[g, "ag", s - 1] = a, a + 1
                        a += 2
                    if g == "l2" and msg < DC:
                        no[g, "tm", msg] = t
                        t += 1
            return no, used_t, used_a, t, a, b

        no, used_t, used_a, T_N, A_N, B_N = plan()

        def slots(g):
            lag, last = LAGS[g], 2 if g in ("g2", "s2") else 3
            ok = lambda c: c if 0 <= c < DC else None
            for s in range(DC + lag + last + 1):
                m = g == "l2"
                yield (ok(s - lag), ok(s - lag - 1), ok(s - lag - 2) if last == 3 else None, ok(s - lag - last),
                       ok(s) if m else None, ok(s - 1) if m else None, ok(s - 2) if m else None)

        NO_SLOT = (None,) * 7
        GATE = CH * F

        def slots_after(g):
            before = NO_SLOT
            for now in slots(g):
                yield now, before
                before = now
            yield NO_SLOT, before

        def b_end(kind, nl, b0, step, lane, i):
            hid = 2 if kind == "S" else 1
            n = [0, hid * nl, 2 * hid * nl][step] * NC
            return b0 + n + (lane * NC + i + 1) * (hid if step < 2 else 1)

        def ut_free(kind, nl, b0, step, lane, i):
            if i >= 3:
                return b_end(kind, nl, b0, step, lane, i - 3)
            q = step * nl + lane - 1
            return b0 - 2 + i if q < 0 else b_end(kind, nl, b0, q // nl, q % nl, i + 2)

        PAIRS = [[0, 1], [2, 3], [4]]

        def seg(rnd, t):
            return rnd * T + t

        N_SLOTS = 6 * (NC + 2)
        HALF, PAUSE = 28, 3
        LEAD, END, TAIL = 6, 44, 18

        def tiles_by(k):
            k = min(k, N_SLOTS - 1)
            if k < HALF + PAUSE:
                return min(T, LEAD + (T - LEAD) * (k + 1) // HALF)
            return T + (T - END - TAIL) * (k + 1 - HALF - PAUSE) // (N_SLOTS - HALF - PAUSE)

        @block.sync
        def _(sp):
            sp.dma_start(W[:], wts).then_inc(s_const, 16)
            sp.dma_start(ident[:], ident_in).then_inc(s_const, 16)
            sp.dma_start(plc[:], place).then_inc(s_const, 16)
            sp.dma_start(ei[:], edges.rearrange("j p t -> p j t")).then_inc(s_const, 16)
            sp.dma_start(dg[:], ew).then_inc(s_const, 16)
            sp.dma_start(LNG[:], lnp.partition_broadcast(P)).then_inc(s_const, 16)
            for b in range(T // SB):
                if b >= 3:
                    sp.wait_ge(s_eq, b - 2)
                sp.dma_start(spread(b).bitcast(I32),
                             dst_rows[b * SB * P:(b + 1) * SB * P].partition_broadcast(P)).then_inc(s_bc[b], 16)
            sp.wait_ge(s_zero, 1)
            nm = nmap.rearrange("(p k) j -> p (k j)", p=P)
            for k in range(2):
                sp.dma_start(nm[:, k * 400:(k + 1) * 400], LH[0][:, 0:5, :].rearrange("p k f -> p (k f)")[:, 0:400])\
                    .then_inc(s_mapz, 16)

            def s_store(k, b, lane):
                sp.dma_start(tabS[k][:, b * KT:(b + 1) * KT, :], LH[lane][:]).then_inc(s_hl[lane], 16)
            norm = row = 0
            for pair in PAIRS:
                n0 = norm
                for step in range(3):
                    for lane, b in enumerate(pair):
                        base = n0 + (step * len(pair) + lane) * NC
                        sp.wait_ge(s_norm, base + NC)
                        s_store([0, 2, 4][step], b, lane)
                        if step < 2:
                            row += 1
                            sp.wait_ge(s_row, row)
                            sp.dma_start(tabS[[1, 3][step]][:, b * KT:(b + 1) * KT, :], R).then_inc(s_rst, 16)
                for lane, b in enumerate(pair):
                    if b + 2 < EB:
                        sp.wait_ge(s_fin, b + 1)
                        sp.wait_ge(s_xs[b + 2], 16 * KT)
                        sp.dma_start(LX[lane][:], HD[:, (b + 2) * KT:(b + 3) * KT, :]).then_inc(s_xc[lane], 16)
                for lane, b in enumerate(pair):
                    base = n0 + (4 * len(pair) + lane) * NC
                    sp.wait_ge(s_norm, base + NC)
                    s_store(5, b, lane)
                    s_store(6, b, lane)
                norm = n0 + 5 * len(pair) * NC

            def n_load(lane, b, fin):
                sp.wait_ge(s_fin, fin)
                sp.dma_start(LX[lane][:], xb[b]).then_inc(s_xl[lane], 16)

            def n_store(lane, b, fin):
                sp.wait_ge(s_fin, fin)
                rows = ob[b] if isinstance(b, int) else lane_rows(ob, b)
                sp.dma_start(rows, LH[lane][:]).then_inc(s_hl[lane], 16)

            for lane in range(2):
                n_load(lane, NB - 2 * PRE + lane, EB - 1 + lane)
            for r in range(PRE):
                for lane in range(2):
                    n_store(lane, NB - 2 * PRE + 2 * r + lane, EB + 2 * r + lane + 1)
                    if r + 1 < PRE:
                        n_load(lane, NB - 2 * PRE + 2 * r + 2 + lane, EB + 2 * r + lane + 1)

            sp.wait_ge(s_hl[0], 16 * (5 * 3 + PRE))
            sp.wait_ge(s_hl[1], 16 * (5 * 2 + PRE))
            sp.wait_ge(s_rst, 16 * 2 * EB)

            def first_messages(c):
                k = c % NC * CH
                if c >= NC:
                    sp.wait_ge(s_seg, seg(1, (c - NC + 1) * CH))
                sp.dma_start(M[:, k:k + CH, 0:F], tabS[0][:, c * CH:(c + 1) * CH, :]).then_inc(s_m0[c % NC], 16)

            for c in range(2 * NC):
                first_messages(c)
            for k in range(1, 5):
                for b in range(EB):
                    if k in (1, 3):
                        sp.wait_ge(s_hd, (k // 2) * EB + b + 1)
                    else:
                        sp.wait_ge(s_norm, NORM_D + (k // 2) * EB + b + 1)
                    sp.dma_start(tabD[k][:, b * KT:(b + 1) * KT, :], HD[:, b * KT:(b + 1) * KT, :])\
                        .then_inc(s_tb, 16)
                    if k == 1 and b + 2 < EB:
                        for c in range((b + 2) * NC, (b + 3) * NC):
                            first_messages(c)
            for c in range(DC):
                k = c % NC * CH
                sp.wait_ge(s_seg, seg(5, (c - NC + 1) * CH))
                sp.dma_start(M[:, k:k + CH, F:F + FE], attr[:, c * CH:(c + 1) * CH, :]).then_inc(s_attr[c % NC], 16)
            for b in range(EB):
                sp.wait_ge(s_x3r, b + 1)
                sp.dma_start(x3[:, b * KT:(b + 1) * KT, :], XD[:, b * KT:(b + 1) * KT, :]).then_inc(s_x3, 16)
            for b in range(EB):
                sp.wait_ge(s_hd, 2 * EB + b + 1)
                sp.dma_start(tabD[5][:, b * KT:(b + 1) * KT, :], HD[:, b * KT:(b + 1) * KT, :])\
                    .then_inc(s_tb, 16)
            sp.wait_ge(s_tp, T_N)
            for lane in range(2):
                n_load(lane, lane, EB + 2 * PRE)
            with sp.Fori(0, STEPS // 2) as r:
                for i in range(2):
                    for b in range(EB):
                        if (i, b) == (1, EB - 1):
                            for lane in range(2):
                                n_store(lane, r * 2 + lane, r * 2 + (EB + 2 * PRE + lane + 1))
                                sp.dma_start(LX[lane][:], lane_rows(xb, r * 2 + (2 + lane)))\
                                    .then_inc(s_xl[lane], 16)
                        sp.wait_ge(s_left, r * (2 * T) + (i * T + (b + 1) * KT))
                        sp.dma_start(tabD[6 - i][:, b * KT:(b + 1) * KT, :], HD[:, b * KT:(b + 1) * KT, :])\
                            .then_inc(s_tb, 16)
            sp.wait_ge(s_seg, seg(6 + STEPS, 0))
            sp.wait_ge(s_left, STEPS * T)
            sp.wait_ge(s_tb, 16 * (5 + STEPS) * EB)
            for b in range(EB):
                sp.dma_start(XD[:, b * KT:(b + 1) * KT, :], x3[:, b * KT:(b + 1) * KT, :]).then_inc(s_x3l[b], 16)
            for b in range(EB):
                sp.wait_ge(s_x3l[b], 16)
            for lane in range(2):
                sp.wait_ge(s_xl[lane], 16 * (NB // 2 + 1))
                sp.wait_ge(s_hl[lane], 16 * (5 * (3 - lane) + NB // 2))
            sp.wait_ge(s_out, 16 * T)

        @block.gpsimd
        def _(gp):
            gp.wait_ge(s_const, 96)

            def source_rows(b, rows, done):
                for k in range(KT):
                    t = b * KT + k
                    gp.indirect_dma_start(rows[:, k, :], None, x,
                                          bass.IndirectOffsetOnAxis(ei[:, 0, t:t + 1], 0)).then_inc(done, 16)

            for lane in range(2):
                source_rows(lane, LX[lane], s_xg[lane])
            gp.wait_ge(s_eq, T // SB)
            for b in range(2, EB):
                source_rows(b, HD[:, b * KT:(b + 1) * KT, :], s_xs[b])
            for t in range(T):
                gp.indirect_dma_start(XD[:, t, :], None, x,
                                      bass.IndirectOffsetOnAxis(ei[:, 1, t:t + 1], 0)).then_inc(s_xd, 16)
            gp.wait_ge(s_deg, 1)
            gp.wait_ge(s_mapz, 32)
            for t in range(T):
                gp.indirect_dma_start(nmap, bass.IndirectOffsetOnAxis(didx[:, t:t + 1], 0),
                                      mrow[:, t, :], None, bounds_check=NN - 1, oob_is_err=False)\
                    .then_inc(s_maps, 16)
            gp.wait_ge(s_maps, 16 * T)
            for t in range(T):
                gp.indirect_dma_start(mg[:, t, :], None, nmap,
                                      bass.IndirectOffsetOnAxis(ei[:, 0, t:t + 1], 0)).then_inc(s_mapg, 16)

            def gather(table, rnd, reg=None, between=None):
                for t in range(T):
                    if t % CH == 0:
                        if between is not None:
                            between(t)
                        n = seg(rnd, t + CH - 1) - SLOTS + 1
                        gp.wait_ge(s_seg, n if reg is None else reg * (2 * T) + n)
                        gp.sem_inc(s_turn, 1)
                    gp.indirect_dma_start(M[:, t % SLOTS, 0:F], None, table,
                                          bass.IndirectOffsetOnAxis(sidx[:, t:t + 1], 0))\
                        .then_inc(s_g[t % SLOTS], 16)

            def add_ln_b(lane, r, n0):
                gp.wait_ge(s_norm, r * (10 * NC) + (n0 + (4 + lane + 1) * NC))
                nc.gpsimd.tensor_tensor(LX[lane][:], LX[lane][:],
                                        LNG[:, F:2 * F].unsqueeze(1).broadcast_to([P, KT, F]),
                                        ALU.add).then_inc(s_xb, 1)

            def finish(lane, r, n0):
                gp.wait_ge(s_norm, r * (10 * NC) + (n0 + (8 + lane + 1) * NC))
                nc.gpsimd.tensor_tensor(LH[lane][:], LX[lane][:], LH[lane][:], ALU.add).then_inc(s_fin, 1)

            with gp.Fori(0, PRE) as r:
                for lane in range(2):
                    add_ln_b(lane, r, S_NORM)
                for lane in range(2):
                    finish(lane, r, S_NORM)
            gp.wait_ge(s_slot, 1)
            for k in range(1, 5):
                gp.wait_ge(s_tb, 16 * EB * k)
                gather(tab[k], 1 + k)
            place_n = {}
            for lane in range(2):
                k = tiles_by((3 + lane) * (NC + 2) + NC - 1 + 3)
                place_n[-(-(k + 4) // CH) * CH] = lane
            with gp.Fori(0, STEPS // 2) as r:
                for i in range(2):
                    gp.wait_ge(s_tb, r * (2 * 16 * EB) + 16 * EB * (5 + i))
                    gp.sem_inc(s_turn, 1)

                    def node_sums(t):
                        if i * T + t in place_n:
                            add_ln_b(place_n[i * T + t], r, NORM_N)
                    gather(tab[5 + i], 6 + i, r, node_sums)
                for lane in range(2):
                    finish(lane, r, NORM_N)
            for t in range(T):
                if t % KT == 0:
                    gp.wait_ge(s_res, t // KT + 1)
                gp.indirect_dma_start(out, bass.IndirectOffsetOnAxis(didx[:, t:t + 1], 0),
                                      HD[:, t, :], None, bounds_check=NN - 1, oob_is_err=False)\
                    .then_inc(s_out, 16)
            gp.wait_ge(s_out, 16 * T)

        def landed(g, t):
            return 16 * (g * (T // SLOTS) + t // SLOTS + 1)

        @block.scalar
        def _(act):
            c = Count()

            def norm(X, H, k0, func, slot):
                for k in range(k0 * CH, k0 * CH + CH):
                    last = A.activation(H[:, k, :], X[:, k, :], func, bias=lnv[:, slot, 1, k:k + 1],
                                        scale=lnv[:, slot, 0, k:k + 1])
                last.then_inc(s_norm, 1)

            def steps(r0, kind, lanes, batch):
                t0, a0, st0 = c.t, c.a, c.stat
                nl = len(lanes)
                for step in range(3):
                    for lane in lanes:
                        q = step * nl + lane
                        X, H = LX[lane], LH[lane]
                        if step < 2:
                            act.wait_ge(s_ln, r0(LN_OPS * 5 * nl, LN_OPS * (st0 + q + 1)))
                            if kind == "S" and (batch[lane] >= 2 or step > 0):
                                act.wait_ge(s_hl[lane], 16 * (5 * (batch[lane] // 2) + step))
                            if kind == "N" and step == 0:
                                act.wait_ge(s_hl[lane], r0(16, 16 * (5 * (3 - lane) + r0.pair)))
                        for i in range(NC + 2):
                            if i < NC and step < 2:
                                norm(X, H, i, ACT.Relu, (st0 + q) % 2)
                            if 1 <= i <= NC:
                                n = t0 + q * NC + i - 1
                                act.wait_ge(s_tp, r0(3 * nl * NC, n + 1))
                                if not (r0.first and n < 3):
                                    act.wait_ge(s_a, r0(3 * nl * NC, a0 + q * NC + i - 3))
                                A.activation(HT[0:F, n % 3, :], PT[n % 2][0:F, 0:CH * P],
                                             ACT.Relu if step == 2 else ACT.Copy).then_inc(s_tev, 1)
                            if i >= 2:
                                a_evac(a0 + q * NC + i - 2, [ACT.Relu, None, ACT.Gelu][step],
                                       ["b1", "s1", "ub"][step], r0, 3 * nl * NC,
                                       c.e + lane * NC + i - 2, nl * NC,
                                       ut_free(kind, nl, c.b, step, lane, i - 2))
                for j, func in ((3, ACT.Identity), (4, ACT.Relu)):
                    for lane in lanes:
                        st = j * nl + lane
                        act.wait_ge(s_ln, r0(LN_OPS * 5 * nl, LN_OPS * (st0 + st + 1)))
                        src = LH[lane] if j == 3 else LX[lane]
                        for i in range(NC):
                            norm(src, LH[lane], i, func, (st0 + st) % 2)

            def a_evac(n, func, bname, r0, per, e, eper, free):
                act.wait_ge(s_a, r0(per, n + 1))
                src = PA[n % 2][0:F, 0:CH * P]
                if func is None:
                    if not (r0.first and e < 2):
                        act.wait_ge(s_elu, r0(eper, e - 1))
                    A.activation(TE[0:F, e % 2, :], src, ACT.Exp, bias=bias(bname))
                    A.activation(TR[:, e % 2, :], src, ACT.Relu, bias=bias(bname)).then_inc(s_aev, 1)
                else:
                    if free is None:
                        if n - 3 >= A_D:
                            act.wait_ge(s_b, used_a[n - 3])
                    elif not (r0.first and n < 3):
                        act.wait_ge(s_b, r0(per, free))
                    A.activation(UT[0:F, n % 3, :], src, func, bias=bias(bname)).then_inc(s_aev, 1)

            act.wait_ge(s_const, 96)
            act.wait_ge(s_mapz, 32)
            act.wait_ge(s_eq, T // SB)
            for i, pair in enumerate(PAIRS):
                steps(Fixed(None, i == 0), "S", range(len(pair)), pair)
                c.b += 3 * NC * len(pair) + 2 * NC * len(pair)
                c.t += 3 * NC * len(pair)
                c.a += 3 * NC * len(pair)
                c.e += NC * len(pair)
                c.stat += 5 * len(pair)
            with act.Fori(0, PRE) as r:
                steps(Fixed(r, False), "N", range(2), None)
            c.t += N_CHUNKS
            c.a += N_CHUNKS
            c.e += PRE * 2 * NC
            c.stat += N_STAT

            one = Fixed(None, False)

            def d_norm(b, func=ACT.Relu, X=XD):
                n = c.stat - S_STAT - N_STAT
                act.wait_ge(s_ln, LN_OPS * (c.stat + 1))
                for k in range(KT):
                    t = b * KT + k
                    last = A.activation(HD[:, t, :], X[:, t, :], func, bias=lnv[:, c.stat % 2, 1, k:k + 1],
                                        scale=lnv[:, c.stat % 2, 0, k:k + 1])
                last.then_inc(s_norm, 1)
                c.stat += 1

            def d_norm_chunk(b, i):
                act.wait_ge(s_ln, LN_OPS * (c.stat + 1))
                for k in range(i * CH, i * CH + CH):
                    t = b * KT + k
                    last = A.activation(HD[:, t, :], XD[:, t, :], ACT.Relu, bias=lnv[:, c.stat % 2, 1, k:k + 1],
                                        scale=lnv[:, c.stat % 2, 0, k:k + 1])
                if i == NC - 1:
                    last.then_inc(s_norm, 1)
                    c.stat += 1

            def d_tev(g, kind, ch):
                n = no[g, kind, ch]
                act.wait_ge(s_tp, n + 1)
                if kind == "tm":
                    if ch >= 2:
                        act.wait_ge(s_a, no[g, "ag", ch - 2] + 1)
                    A.activation(TE[:, ch % 2, :], PT[n % 2][:, 0:CH * P], ACT.Copy).then_inc(s_tev, 1)
                else:
                    if n - 3 in used_t:
                        act.wait_ge(*used_t[n - 3])
                    A.activation(HT[0:F, n % 3, :], PT[n % 2][0:F, 0:CH * P], ACT.Copy).then_inc(s_tev, 1)

            def d_aev(n, func, bname):
                a_evac(n, func, bname, one, 0, c.e, 0, None)
                if func is None:
                    c.e += 1

            def scale(g, ch):
                if g == "g1":
                    act.wait_ge(s_m0[ch % NC], 16 * (ch // NC + 1))
                for t in range(ch * CH, ch * CH + CH):
                    if g == "g2":
                        act.wait_ge(s_g[t % SLOTS], landed(0, t))
                    A.activation(M[:, t % SLOTS, 0:F], M[:, t % SLOTS, 0:F], ACT.Copy, scale=wgt[:, t:t + 1])\
                        .then_inc(s_sc, 1)

            for b in range(EB):
                d_norm(b)
            act.wait_ge(s_slot, 1)
            for g in STAGES:
                if g in ("g1", "g2"):
                    scale(g, 0)
                for (seg_c, t_c, a_c, b_c, tm, am, bm), (_, _, _, b_before, _, _, _) in slots_after(g):
                    if g in ("g1", "g2") and seg_c is not None and seg_c + 1 < DC:
                        scale(g, seg_c + 1)
                    if bm is not None:
                        n, k = no[g, "bm", bm], bm % NC * CH
                        act.wait_ge(s_b, n + 1)
                        if bm >= NC:
                            act.wait_ge(s_gu, bm - NC + 1)
                        A.activation(gate[:, k:k + CH], PB[n % 2][0:P, GATE:GATE + CH], ACT.Tanh, scale=0.5)\
                            .then_inc(s_gate, 1)
                    if a_c is not None:
                        d_aev(no[g, "a", a_c], {"g1": ACT.Relu, "s1": None, "l2": ACT.Gelu}[g],
                              {"g1": "b1", "s1": "s1", "l2": "ub"}[g])
                    if t_c is not None:
                        if g not in ("g1", "g2"):
                            d_tev(g, "th", t_c)
                        d_tev(g, "tg", t_c)
                    if am is not None:
                        d_aev(no[g, "am", am], ACT.Gelu, "mb")
                        d_aev(no[g, "ag", am], ACT.Gelu, "gb")
                    if tm is not None:
                        d_tev(g, "tm", tm)
                    if b_before is not None and b_before % NC == NC - 1:
                        b = b_before // NC
                        if g == "l2":
                            if b >= 1:
                                d_norm(b - 1)
                            d_norm(b, ACT.Identity, HD)
                    if b_before is not None and g in ("g2", "s2"):
                        b, i = b_before // NC, b_before % NC
                        if i == NC - 1 and b >= 1:
                            d_norm_chunk(b - 1, 0)
                        elif i < NC - 1 and b >= 2:
                            d_norm_chunk(b - 2, i + 1)
                if g in ("g2", "s2"):
                    for i in range(1, NC):
                        d_norm_chunk(EB - 2, i)
                    for i in range(NC):
                        d_norm_chunk(EB - 1, i)
            d_norm(EB - 1)
            c.t, c.a, c.b = T_N, A_N, B_N
            with act.Fori(0, STEPS // 2) as r:
                steps(Fixed(r, False, PRE), "N", range(2), None)

        @block.tensor
        def _(pe):
            c = Count()
            pe.wait_ge(s_const, 96)
            pe.wait_ge(s_init, 1)

            def segsum(rnd, t, rhs, n, reg=None):
                s = seg(rnd, t)
                pe.wait_ge(s_msg, s + 1 if reg is None else reg * (2 * T) + (s + 1))
                PE.matmul(PS[t % 2][0:P, 0:n], EQ[:, t, :], rhs, start=True, stop=True).then_inc(s_seg, 1)

            def trans(n, r0, per, rows, width=F):
                if not (r0.first and n < 2):
                    pe.wait_ge(s_tev, r0(per, n - 1))
                for k in range(CH):
                    last = PE.transpose(PT[n % 2][0:width, k * P:(k + 1) * P], rows(k), ident[:])
                last.then_inc(s_tp, 1)

            def rows_out(n, r0, per, parts, cols=F):
                if not (r0.first and n < 2):
                    pe.wait_ge(s_bev, r0(per, n - 1))
                for k in range(CH):
                    for j, (l, rh) in enumerate(parts):
                        last = PE.matmul(PB[n % 2][0:P, k * cols:(k + 1) * cols], l(k), rh,
                                         start=(j == 0), stop=(j == len(parts) - 1))
                last.then_inc(s_b, 1)
                return last

            def steps(r0, kind, lanes, sums=None):
                nl = len(lanes)
                per = 3 * nl * NC
                b = c.b

                def between(k, part):
                    if sums is not None:
                        n = tiles_by(k - 1)
                        sums(n + ((tiles_by(k) - n) * part + 2) // 4)

                between(-1, 4)
                for step in range(3):
                    for lane in lanes:
                        q = step * nl + lane
                        st = c.norm + q * NC
                        for i in range(NC + 2):
                            k_ = q * (NC + 2) + i
                            if i < NC:
                                pe.wait_ge(s_norm, r0(5 * nl * NC, st + i + 1))
                                trans(c.t + q * NC + i, r0, per, lambda k: LH[lane][:, i * CH + k, :])
                            between(k_, 1)
                            if 1 <= i <= NC:
                                n = c.t + q * NC + i - 1
                                na = c.a + q * NC + i - 1
                                pe.wait_ge(s_tev, r0(per, n + 1))
                                if not (r0.first and na < 2):
                                    pe.wait_ge(s_aev, r0(per, na - 1))
                                halves = [(0, CH * P)] if sums is None else \
                                    [(0, CH * P // 2), (CH * P // 2, CH * P)]
                                for h, (c0, c1) in enumerate(halves):
                                    if h == 1:
                                        between(k_, 2)
                                    last = PE.matmul(PA[na % 2][0:F, c0:c1], w(["W1", "WR1", "UA"][step]),
                                                     HT[0:F, n % 3, c0:c1], start=True, stop=True)
                                last.then_inc(s_a, 1)
                            between(k_, 3)
                            if i >= 2:
                                na = c.a + q * NC + i - 2
                                if step == 1:
                                    pe.wait_ge(s_elu, r0(nl * NC, c.e + lane * NC + i - 1))
                                else:
                                    pe.wait_ge(s_aev, r0(per, na + 1))
                                u = lambda k, h: UT[0:h, na % 3, k * P:(k + 1) * P]
                                if kind == "S" and step < 2:
                                    rows_out(b, r0, per, [(lambda k: u(k, F), ident[0:F, 0:F])])
                                    b += 1
                                rows_out(b, r0, per, [(lambda k: u(k, F + 1), w(["W2", "WR2", "UW2"][step], F + 1))])
                                b += 1
                            between(k_, 4)
                c.b = b

            for t in range(T):
                segsum(0, t, dg[:, t, :], 2)
            for i, pair in enumerate(PAIRS):
                nl = len(pair)
                steps(Fixed(None, i == 0), "S", range(nl))
                c.t += 3 * NC * nl
                c.a += 3 * NC * nl
                c.e += NC * nl
                c.norm += 5 * NC * nl
            with pe.Fori(0, PRE) as r:
                steps(Fixed(r, False), "N", range(2))
            c.b += N_CHUNKS - 6 * NC
            c.e += PRE * 2 * NC

            one = Fixed(None, False)

            def d_t(g, kind, ch):
                b, i = ch // NC, ch % NC
                if kind == "tm":
                    pe.wait_ge(s_attr[i], 16 * (b + 1))
                    for t in range(ch * CH, ch * CH + CH):
                        pe.wait_ge(s_g[t % SLOTS], landed(3, t))
                    trans(no[g, kind, ch], one, 0, lambda k: M[:, (i * CH + k) % SLOTS, :], F + FE)
                elif kind == "th":
                    trans(no[g, kind, ch], one, 0, lambda k: HD[:, ch * CH + k, :])
                else:
                    pe.wait_ge(s_agg, STAGES.index(g) * DC + ch + 1)
                    trans(no[g, kind, ch], one, 0, lambda k: LX[b % 2][:, i * CH + k, :])

            def d_a(n, parts):
                pe.wait_ge(s_aev, n - 1)
                for j, (wt, rhs, tn) in enumerate(parts):
                    pe.wait_ge(s_tev, tn + 1)
                    last = PE.matmul(PA[n % 2][0:F, 0:CH * P], wt, rhs, start=(j == 0), stop=(j == len(parts) - 1))
                last.then_inc(s_a, 1)

            def ring(buf, n, h):
                return lambda k: buf[0:h, n % 3, k * P:(k + 1) * P]

            for g in STAGES:
                if g in ("s1", "l2"):
                    pe.wait_ge(s_norm, NORM_D + (2 if g == "s1" else 3) * EB)
                for seg_c, t_c, a_c, b_c, tm, am, bm in slots(g):
                    def seg_tile(k):
                        if seg_c is not None:
                            t = seg_c * CH + k
                            segsum(1 + STAGES.index(g), t, M[:, t % SLOTS, 0:F], F)

                    def b_chunk():
                        if g in ("g1", "s1", "l2"):
                            an = no[g, "a", b_c]
                            if g == "s1":
                                pe.wait_ge(s_elu, c.e + b_c + 1)
                            else:
                                pe.wait_ge(s_aev, an + 1)
                            parts = [(ring(UT, an, F + 1), w("UW2", F + 1))] if g == "l2" else \
                                [(ring(UT, an, F), ident[0:F, 0:F])]
                        else:
                            pe.wait_ge(s_tev, no[g, "tg", b_c] + 1)
                            parts = [(ring(HT, no[g, "tg", b_c], F + 1), w("W2", F + 1))] if g == "g2" else \
                                [(ring(HT, no[g, "th", b_c], F + 1), w("WR2", F + 1)),
                                 (ring(HT, no[g, "tg", b_c], F), w("WL2"))]
                        rows_out(no[g, "b", b_c], one, 0, parts)

                    seg_tile(0)
                    if bm is not None:
                        pe.wait_ge(s_aev, no[g, "ag", bm] + 1)
                        n = no[g, "bm", bm]
                        pe.wait_ge(s_bev, n - 1)
                        for x_, rhs, c0, cols in (("am", w("MW2", F + 1), 0, F),
                                                  ("ag", W[0:F + 1, GW2:GW2 + 1], GATE, 1)):
                            for k in range(CH):
                                last = PE.matmul(PB[n % 2][0:P, c0 + k * cols:c0 + (k + 1) * cols],
                                                 ring(UT, no[g, x_, bm], F + 1)(k), rhs, start=True, stop=True)
                        last.then_inc(s_b, 1)
                    if b_c is not None and g != "s1":
                        b_chunk()
                    seg_tile(1)
                    if a_c is not None:
                        parts = []
                        for x_, wn in {"g1": [("tg", "W1")], "s1": [("th", "WR1"), ("tg", "WL1")],
                                       "l2": [("th", "UA"), ("tg", "UB")]}[g]:
                            tn = no[g, x_, a_c]
                            parts.append((w(wn), HT[0:F, tn % 3, :], tn))
                        d_a(no[g, "a", a_c], parts)
                    seg_tile(2)
                    if t_c is not None:
                        if g not in ("g1", "g2"):
                            d_t(g, "th", t_c)
                        d_t(g, "tg", t_c)
                    seg_tile(3)
                    if am is not None:
                        for x_, wn in (("am", "MW1"), ("ag", "GW1")):
                            d_a(no[g, x_, am], [(w(wn, 128), TE[:, am % 2, :], no[g, "tm", am])])
                    if tm is not None:
                        d_t(g, "tm", tm)
                    if b_c is not None and g == "s1":
                        b_chunk()
            c.t, c.a, c.b, c.norm = T_N, A_N, B_N, NORM_N
            c.e += DC
            with pe.Fori(0, STEPS // 2) as r:
                summed = 0

                def sums(n):
                    nonlocal summed
                    for u in range(summed, n):
                        t = u % T
                        own = lambda: PE.matmul(PS[t % 2][0:P, 0:F], EQ[:, t, :], HD[:, t, :], start=True, stop=False)
                        if u >= 2:
                            pe.wait_ge(s_left, r * (2 * T) + (u - 1))
                            own()
                        pe.wait_ge(s_msg, r * (2 * T) + (seg(6, u) + 1))
                        if u < 2:
                            own()
                        PE.matmul(PS[t % 2][0:P, 0:F], EQ[:, t, :], M[:, t % SLOTS, 0:F], start=False, stop=True)\
                            .then_inc(s_seg, 1)
                    summed = max(n, summed)

                steps(Fixed(r, False), "N", range(2), sums)
                sums(2 * T)

        @block.vector
        def _(dve):
            c = Count()

            def rsqrt(y, v, h):
                dve.drain()
                V.tensor_single_scalar(y.bitcast(I32), v.bitcast(I32), 1, ALU.arith_shift_right)
                dve.drain()
                V.tensor_scalar(y.bitcast(I32), y.bitcast(I32), -1.0, 1597463007.0, ALU.mult, ALU.add)
                for _ in range(3):
                    dve.drain()
                    V.scalar_tensor_tensor(out=h, in0=y, scalar=-0.5, in1=y, op0=ALU.mult, op1=ALU.mult)
                    dve.drain()
                    V.tensor_tensor(h, h, v, ALU.mult)
                    dve.drain()
                    V.scalar_tensor_tensor(out=y, in0=h, scalar=1.5, in1=y, op0=ALU.add, op1=ALU.mult)
                dve.drain()

            def ln_op(j, lane, n, r0, per):
                s_, d, v, h = (sm[:, lane, m, :] for m in range(4))
                y = lnv[:, n % 2, 0, :]
                bs = bst[:, lane, :, :]
                if j == 0:
                    dve.wait_ge(s_bn, r0(per * NC, (n + 1) * NC))
                if n or j:
                    dve.wait_ge(s_ln, r0(per * LN_OPS, n * LN_OPS + j))
                if j == 0:
                    op = V.tensor_tensor(s_, bs[:, :, 1], bs[:, :, 4], ALU.add)
                elif j == 1:
                    op = V.tensor_tensor(d, bs[:, :, 1], bs[:, :, 4], ALU.subtract)
                elif j == 2:
                    op = V.tensor_tensor(v, bs[:, :, 2], bs[:, :, 5], ALU.add)
                elif j == 3:
                    op = V.scalar_tensor_tensor(out=d, in0=d, scalar=0.25, in1=d, op0=ALU.mult, op1=ALU.mult)
                elif j == 4:
                    op = V.tensor_scalar(v, v, 1.0 / F, EPS, ALU.mult, ALU.add)
                elif j == 5:
                    op = V.tensor_tensor(v, v, d, ALU.add)
                elif j == 6:
                    op = V.tensor_single_scalar(y.bitcast(I32), v.bitcast(I32), 1, ALU.arith_shift_right)
                elif j == 7:
                    op = V.tensor_scalar(y.bitcast(I32), y.bitcast(I32), -1.0, 1597463007.0, ALU.mult, ALU.add)
                elif j == LN_OPS - 1:
                    op = V.scalar_tensor_tensor(out=lnv[:, n % 2, 1, :], in0=s_, scalar=-0.5, in1=y, op0=ALU.mult,
                                                op1=ALU.mult)
                elif j % 3 == 2:
                    op = V.scalar_tensor_tensor(out=h, in0=y, scalar=-0.5, in1=y, op0=ALU.mult, op1=ALU.mult)
                elif j % 3 == 0:
                    op = V.tensor_tensor(h, h, v, ALU.mult)
                else:
                    op = V.scalar_tensor_tensor(out=y, in0=h, scalar=1.5, in1=y, op0=ALU.add, op1=ALU.mult)
                op.then_inc(s_ln, 1)

            def bn_chunk(X, lane, i, r0, per, other=None, first=0, count=0, beat=None):
                for k in range(CH):
                    last = V.bn_stats(bst[:, lane, i * CH + k, :], X[:, i * CH + k, :])
                    if k == CH - 1:
                        last.then_inc(s_bn, 1)
                    if other is not None:
                        for j in range(first + count * k // CH, first + count * (k + 1) // CH):
                            ln_op(j, *other, r0, per)
                    if beat is not None:
                        beat(k + 2)

            def elu(e, u, r0, eper, uper, free):
                dve.wait_ge(s_aev, r0(uper, u + 1))
                if free is None:
                    if u - 3 >= A_D:
                        dve.wait_ge(s_b, used_a[u - 3])
                else:
                    dve.wait_ge(s_b, r0(uper, free))
                V.tensor_scalar(TE[0:F, e % 2, :], TE[0:F, e % 2, :], 1.0, -1.0, ALU.min, ALU.add)\
                    .then_inc(s_eh, 1)
                dve.wait_ge(s_eh, r0(eper, e + 1))
                V.tensor_tensor(UT[0:F, u % 3, :], TE[0:F, e % 2, :], TR[:, e % 2, :], ALU.add).then_inc(s_elu, 1)

            def pb(n, cols=F):
                return PB[n % 2][0:P, 0:CH * cols].rearrange("p (k f) -> p k f", k=CH)

            def affine(X, H, shift, beat=None):
                gb = [LNG[:, j * F:(j + 1) * F].unsqueeze(1).broadcast_to([P, KT, F]) for j in range(2)]
                step = KT if beat is None else CH
                for k in range(0, KT, step):
                    V.tensor_tensor(H[:, k:k + step, :], H[:, k:k + step, :], gb[0][:, k:k + step, :], ALU.mult)
                    if beat is not None:
                        beat(1)
                if shift:
                    V.tensor_tensor(X, X, gb[1], ALU.add)
                dve.drain()
                for k in range(0, KT, step):
                    V.tensor_tensor(X[:, k:k + step, :], X[:, k:k + step, :], H[:, k:k + step, :], ALU.add)
                    if beat is not None:
                        beat(1)
                dve.drain()

            V.memset(HT[F:F + 1, :, :], 1.0)
            V.memset(LH[0][:, 0:5, :], 0.0).then_inc(s_zero, 1)
            V.memset(UT[F:F + 1, :, :], 1.0).then_inc(s_init, 1)
            dve.wait_ge(s_const, 96)
            V.tensor_copy(ef[:], ei[:])
            dve.drain()
            V.tensor_tensor(rep[:], ef[:, 2, :], ef[:, 1, :], ALU.not_equal)
            V.tensor_tensor(carry[:], ef[:, 3, :], ef[:, 1, :], ALU.is_equal)
            dve.drain()
            V.tensor_tensor(carry[:], carry[:], first, ALU.mult)
            for b in range(T // SB):
                dve.wait_ge(s_bc[b], 16)
                for k in range(SB):
                    t = b * SB + k
                    last = V.tensor_scalar(EQ[:, t, :], spread(b)[:, k * P:(k + 1) * P].bitcast(I32),
                                           ef[:, 1, t:t + 1], None, ALU.is_equal)
                last.then_inc(s_eq, 1)

            wcol = slotf
            V.tensor_copy(wcol[:], dg[:, :, 1])
            dve.drain()
            for t in range(T):
                if t == 0:
                    V.tensor_scalar(dg[:, 0, :], dg[:, 0, :], 1.0, None, ALU.mult).then_inc(s_msg, 1)
                else:
                    dve.wait_ge(s_seg, seg(0, t))
                    V.scalar_tensor_tensor(out=dg[:, t, :], in0=PS[(t - 1) % 2][0:P, 0:2], scalar=carry[:, t:t + 1],
                                           in1=dg[:, t, :], op0=ALU.mult, op1=ALU.add).then_inc(s_msg, 1)
                    V.tensor_copy(dg[:, t - 1, :], PS[(t - 1) % 2][0:P, 0:2])
            dve.wait_ge(s_seg, seg(0, T))
            V.tensor_copy(dg[:, T - 1, :], PS[(T - 1) % 2][0:P, 0:2])
            dve.drain()
            V.reciprocal(icnt[:], dg[:, :, 0])
            degw, degc = sqd[:], asc[:]
            V.tensor_scalar(degw, dg[:, :, 1], 1.0, None, ALU.add)
            V.tensor_scalar(degc, dg[:, :, 0], 1.0, None, ALU.add)
            dve.drain()
            V.tensor_scalar(wgt[:], degw, 0.0, None, ALU.is_gt)
            V.tensor_scalar(degw, degw, 1e-30, None, ALU.max)
            rsqrt(dw[:, 0, :], degw, ef[:, 2, :])
            V.tensor_tensor(dw[:, 0, :], dw[:, 0, :], wgt[:], ALU.mult)
            rsqrt(dw[:, 1, :], degc, ef[:, 2, :])
            V.tensor_tensor(selfc[:, 0, :], dw[:, 0, :], rep[:], ALU.mult)
            V.tensor_tensor(sqd[:], degc, dw[:, 1, :], ALU.mult)
            V.reciprocal(ef[:, 3, :], degc)
            dve.drain()
            V.scalar_tensor_tensor(out=asc[:], in0=ef[:, 3, :], scalar=1.0 - ALPHA, in1=rep[:], op0=ALU.mult,
                                   op1=ALU.mult)
            V.tensor_tensor(selfc[:, 1, :], dw[:, 1, :], rep[:], ALU.mult)
            V.tensor_copy(mrow[:, :, 1], dw[:, 0, :])
            V.tensor_copy(mrow[:, :, 0], slot1)
            V.tensor_scalar(ef[:, 2, :], ef[:, 1, :], -FAR, None, ALU.add)
            dve.drain()
            V.tensor_tensor(ef[:, 2, :], ef[:, 2, :], rep[:], ALU.mult)
            dve.drain()
            V.tensor_scalar(didx[:], ef[:, 2, :], FAR, None, ALU.add).then_inc(s_deg, 1)

            def b_use(n, r0, per, kind, X, H, i, to=None):
                dve.wait_ge(s_b, r0(per, n + 1))
                ks = slice(i * CH, (i + 1) * CH)
                if kind == "row":
                    op = V.tensor_copy(to[:, ks, :], pb(n))
                elif kind == "relu":
                    op = V.scalar_tensor_tensor(out=X[:, ks, :], in0=pb(n), scalar=0.0, in1=X[:, ks, :],
                                                op0=ALU.max, op1=ALU.add)
                elif kind == "add":
                    op = V.tensor_tensor(X[:, ks, :], pb(n), X[:, ks, :], ALU.add)
                else:
                    op = V.scalar_tensor_tensor(out=H[:, ks, :], in0=H[:, ks, :], scalar=0.0, in1=pb(n),
                                                op0=ALU.max, op1=ALU.add)
                op.then_inc(s_bev, 1)
                return op

            def steps(r0, kind, lanes, batch, row0, sums=None):
                nl = len(lanes)
                per = 3 * nl * NC
                lnper = 5 * nl
                b = c.b
                row = row0

                def ln_rest(st, lane, j0=0, n0=0, n1=0):
                    for j in range(j0, LN_OPS):
                        ln_op(j, lane, c.stat + st, r0, lnper)
                        if sums is not None:
                            sums(n0 + (n1 - n0) * (j + 1) // LN_OPS)

                def norm3(lane, beat=None):
                    X, H, slot = LX[lane], LH[lane], (c.stat + 2 * nl + lane) % 2
                    if kind == "S":
                        dve.wait_ge(s_hl[lane], 16 * (5 * (batch[lane] // 2) + 2))
                    dve.wait_ge(s_ln, r0(lnper * LN_OPS, LN_OPS * (c.stat + 2 * nl + lane + 1)))
                    for k in range(KT):
                        op = V.tensor_scalar(H[:, k, :], X[:, k, :], lnv[:, slot, 0, k:k + 1],
                                             lnv[:, slot, 1, k:k + 1], ALU.mult, ALU.add)
                        if kind == "N" and k % CH == CH - 1:
                            op.then_inc(s_norm, 1)
                        if beat is not None and k % 4 == 3:
                            beat(2 + k // 5)
                    if kind == "S":
                        dve.drain()
                        V.tensor_scalar(H[:], H[:], 0.0, None, ALU.max).then_inc(s_norm, NC)

                for lane in lanes:
                    if kind == "S":
                        if batch[lane] < 2:
                            dve.wait_ge(s_xg[lane], 16 * KT)
                        else:
                            dve.wait_ge(s_xc[lane], 16 * (batch[lane] // 2))
                    else:
                        dve.wait_ge(s_xl[lane], r0(16, 16 * (r0.pair + 1)))
                    for i in range(NC):
                        other = (0, c.stat) if lane == 1 else None
                        bn_chunk(LX[lane], lane, i, r0, lnper, other, 4 * i if i < 4 else 16, 4 if i < 4 else 2)
                        if sums is not None and lane == 1:
                            sums(LEAD * (i + 1) // NC)
                    if nl == 1:
                        ln_rest(0, 0)
                for step in range(3):
                    for lane in lanes:
                        q = step * nl + lane
                        X, H = LX[lane], LH[lane]
                        hidden = kind == "S" and step < 2
                        st = q + nl - 1
                        if hidden and row > 0:
                            dve.wait_ge(s_rst, 16 * row)
                        if kind == "S" and step == 2:
                            dve.wait_ge(s_hl[lane], 16 * (5 * (batch[lane] // 2) + 3))
                        for i in range(NC + 1):
                            k_ = q * (NC + 2) + i
                            n0, n1 = tiles_by(k_ + 1), tiles_by(k_ + 2 + (i == NC))

                            def beat(part):
                                sums(n0 + (n1 - n0) * part // 6)

                            if step == 1 and i < NC:
                                elu(c.e + lane * NC + i, c.a + q * NC + i, r0, nl * NC, per,
                                    ut_free(kind, nl, c.b, step, lane, i))
                            if i == 0 and nl == 2 and step == 0 and lane == 0:
                                ln_rest(1, 1, 0, LEAD, n0)
                            if i >= 1:
                                if hidden:
                                    b_use(b, r0, per, "row", X, H, i - 1, R)
                                    b += 1
                                b_use(b, r0, per, ["relu", "add", "hid"][step], X, H, i - 1)
                                b += 1
                                if sums is not None:
                                    beat(1)
                                dve.wait_ge(s_bev, r0(per, b))
                                other, j0, cnt = None, 0, 0
                                if nl == 2 and not (step == 0 and lane == 0) and i <= 3:
                                    other, j0, cnt = (1 - lane, c.stat + st), 6 * (i - 1), 6
                                bn_chunk(H if step == 2 else X, lane, i - 1, r0, lnper, other, j0, cnt,
                                         None if sums is None or (i == 4 and st // nl == 2) else beat)
                                if i == 4 and nl == 2 and st // nl == 2:
                                    norm3(1 - lane, None if sums is None else beat)
                            if sums is not None:
                                beat(6)
                        if hidden:
                            dve.drain().then_inc(s_row, 1)
                            row += 1
                        if nl == 1:
                            ln_rest(q + 1, 0)
                            if step == 1:
                                norm3(0)
                end = 0

                def end_beat(n):
                    nonlocal end
                    end += n
                    if sums is not None:
                        sums(2 * T - TAIL - END + min(end, END))

                if nl == 2:
                    ln_rest(7, 1, 0, 2 * T - TAIL - END, 2 * T - TAIL - END + 4)
                    end = 4
                for lane in lanes:
                    X, H = LX[lane], LH[lane]
                    dve.wait_ge(s_norm, r0(5 * nl * NC, c.norm + (3 * nl + lane + 1) * NC))
                    if kind == "N":
                        dve.wait_ge(s_xb, r0(2, 2 * r0.pair + lane + 1))
                    affine(X[:], H[:], kind == "S", None if sums is None else end_beat)
                    for i in range(NC):
                        other = (0, c.stat + 4 * nl) if lane == 1 else None
                        bn_chunk(X, lane, i, r0, lnper, other, 4 * i if i < 4 else 16, 4 if i < 4 else 2)
                        end_beat(1 + lane)
                    if lane == nl - 1:
                        ln_rest(4 * nl + lane, lane, 0, 2 * T - TAIL - 4, 2 * T - TAIL)
                if kind == "S":
                    for lane in lanes:
                        dve.wait_ge(s_norm, c.norm + (4 * nl + lane + 1) * NC)
                        dve.sem_inc(s_fin, 1)
                c.b = b
                return row

            row = 0
            for i, pair in enumerate(PAIRS):
                nl = len(pair)
                row = steps(Fixed(None, i == 0), "S", range(nl), pair, row)
                c.a += 3 * NC * nl
                c.e += NC * nl
                c.stat += 5 * nl
                c.norm += 5 * NC * nl
                if i == len(PAIRS) - 1:
                    dve.wait_ge(s_mapg, 16 * T)
                    has, own = ef[:, 3, :], ef[:, 2, :]
                    V.tensor_scalar(has, mg[:, :, 0], 1.0, None, ALU.min)
                    V.tensor_scalar(own, slot1, -1.0, -float(NE), ALU.mult, ALU.add)
                    dve.drain()
                    V.tensor_tensor(own, own, has, ALU.mult)
                    V.tensor_tensor(wgt[:], mg[:, :, 1], has, ALU.subtract)
                    dve.drain()
                    V.tensor_tensor(own, own, mg[:, :, 0], ALU.add)
                    V.scalar_tensor_tensor(out=wgt[:], in0=wgt[:], scalar=1.0, in1=wcol[:], op0=ALU.add, op1=ALU.mult)
                    dve.drain()
                    V.tensor_tensor(own, own, slot1, ALU.add)
                    dve.drain()
                    V.tensor_scalar(own, own, float(NE - 1), None, ALU.add)
                    dve.drain()
                    V.tensor_copy(sidx[:], own).then_inc(s_slot, 1)
            with dve.Fori(0, PRE) as r:
                steps(Fixed(r, False), "N", range(2), None, 0)
            c.b += N_CHUNKS - 6 * NC
            c.a += N_CHUNKS
            c.e += PRE * 2 * NC
            c.stat += N_STAT

            one = Fixed(None, False)

            LN_D = S_STAT + N_STAT
            assert c.stat == LN_D

            def d_ln(X, b):
                n = c.stat
                if n - 2 >= LN_D:
                    dve.wait_ge(s_norm, NORM_D + n - 2 - LN_D + 1)
                for i in range(NC):
                    bn_chunk(X[:, b * KT:(b + 1) * KT, :], n % 2, i, one, 0)
                for j in range(LN_OPS):
                    ln_op(j, n % 2, n, one, 0)
                c.stat += 1

            def conv_tile(g, t):
                arrive, selfcoef, outscale = CONV[g]
                rnd = 1 + STAGES.index(g)

                def own(t):
                    arrive(t)
                    if selfcoef is not None:
                        V.scalar_tensor_tensor(out=M[:, t % SLOTS, 0:F], in0=HD[:, t, :], scalar=selfcoef[:, t:t + 1],
                                               in1=M[:, t % SLOTS, 0:F], op0=ALU.mult, op1=ALU.add)

                def leave(t):
                    src, dest = PS[t % 2][0:P, 0:F], LX[t // KT % 2][:, t % KT, :]
                    if outscale is None:
                        op = V.tensor_copy(dest, src)
                    else:
                        op = V.tensor_scalar(dest, src, outscale[:, t:t + 1], None, ALU.mult)
                    if t % CH == CH - 1:
                        op.then_inc(s_agg, 1)

                m = M[:, t % SLOTS, 0:F]
                if t == 0:
                    own(0)
                if t + 1 < T:
                    own(t + 1)
                if t == 0:
                    dve.drain()
                    V.tensor_scalar(m, m, 1.0, None, ALU.mult).then_inc(s_msg, 1)
                else:
                    dve.wait_ge(s_seg, seg(rnd, t))
                    V.scalar_tensor_tensor(out=m, in0=PS[(t - 1) % 2][0:P, 0:F], scalar=carry[:, t:t + 1], in1=m,
                                           op0=ALU.mult, op1=ALU.add).then_inc(s_msg, 1)
                    leave(t - 1)
                if t == T - 1:
                    dve.wait_ge(s_seg, seg(rnd, t) + 1)
                    leave(t)

            dve.wait_ge(s_xd, 16 * T)
            dve.wait_ge(s_norm, NORM_D)
            for b in range(EB):
                d_ln(XD, b)
            dve.wait_ge(s_norm, NORM_D + EB)
            CONV = {
                "g1": (lambda t: dve.wait_ge(s_sc, t + 1), selfc[:, 0, :], dw[:, 0, :]),
                "g2": (lambda t: dve.wait_ge(s_sc, T + t + 1), selfc[:, 0, :], dw[:, 0, :]),
                "s1": (lambda t: dve.wait_ge(s_g[t % SLOTS], landed(1, t)), None, icnt[:]),
                "s2": (lambda t: dve.wait_ge(s_g[t % SLOTS], landed(2, t)), None, icnt[:]),
                "l2": (lambda t: None, None, None),
            }
            for g in STAGES:
                for (seg_c, *_), (_, _, a_c, b_c, _, _, bm) in slots_after(g):
                    def seg_tile(k):
                        if seg_c is not None:
                            conv_tile(g, seg_c * CH + k)

                    def ln_part(part):
                        if b_c is None or g not in ("g2", "s2") or b_c < NC or b_c % NC == NC - 1:
                            return
                        first = 2 * (b_c % NC) + part
                        if first == 0:
                            dve.wait_ge(s_norm, NORM_D + c.stat - 2 - LN_D + 1)
                        for j in range(LN_OPS * first // 8, LN_OPS * (first + 1) // 8):
                            ln_op(j, c.stat % 2, c.stat, one, 0)
                        if first == 7:
                            c.stat += 1

                    if bm is not None:
                        k0, n = bm % NC * CH, no[g, "bm", bm]
                        dve.wait_ge(s_gate, bm + 1)
                        V.tensor_scalar(gate[:, k0:k0 + CH], gate[:, k0:k0 + CH], 0.5, 0.5, ALU.mult, ALU.add)
                        dve.drain()
                        for k in range(CH):
                            last = V.tensor_scalar(M[:, k0 + k, 0:F], pb(n)[:, k, :], gate[:, k0 + k:k0 + k + 1],
                                                   None, ALU.mult)
                        last.then_inc(s_bev, 1)
                        dve.drain().then_inc(s_gu, 1)
                    seg_tile(0)
                    if b_c is not None:
                        b, i = b_c // NC, b_c % NC
                        rows = slice(b * KT, (b + 1) * KT)
                        b_use(no[g, "b", b_c], one, 0, {"g1": "row", "g2": "relu", "s1": "row", "s2": "add",
                                                        "l2": "hid"}[g], XD[:, rows, :], HD[:, rows, :], i,
                              HD[:, rows, :])
                        if i == NC - 1 and g in ("g1", "s1"):
                            dve.drain().then_inc(s_hd, 1)
                    ln_part(0)
                    seg_tile(1)
                    if b_c is not None and g in ("g2", "s2"):
                        dve.wait_ge(s_bev, no[g, "b", b_c] + 1)
                        n = c.stat + (i < NC - 1 and b >= 1)
                        bn_chunk(XD[:, rows, :], n % 2, i, one, 0)
                    if g == "s1" and a_c is not None:
                        elu(c.e + a_c, no[g, "a", a_c], one, 0, 0, None)
                    seg_tile(2)
                    ln_part(1)
                    if b_c is not None and i == NC - 1:
                        if g == "l2":
                            if b >= 1:
                                dve.wait_ge(s_norm, NORM_D + 3 * EB + 2 * (b - 1) + 1)
                                prev = slice((b - 1) * KT, b * KT)
                                affine(XD[:, prev, :], HD[:, prev, :], True)
                                dve.sem_inc(s_x3r, 1)
                                d_ln(XD, b - 1)
                            else:
                                dve.drain()
                            d_ln(HD, b)
                    seg_tile(3)
                if g in ("g2", "s2"):
                    dve.wait_ge(s_norm, NORM_D + c.stat - 2 - LN_D + 1)
                    for j in range(LN_OPS):
                        ln_op(j, c.stat % 2, c.stat, one, 0)
                    c.stat += 1
            dve.wait_ge(s_norm, NORM_D + 5 * EB - 1)
            prev = slice((EB - 1) * KT, EB * KT)
            affine(XD[:, prev, :], HD[:, prev, :], True)
            dve.sem_inc(s_x3r, 1)
            d_ln(XD, EB - 1)
            dve.wait_ge(s_norm, NORM_D + 5 * EB)
            for b in range(EB):
                hs = HD[:, b * KT:(b + 1) * KT, :]
                V.tensor_tensor(hs, hs, selfc[:, 1, b * KT:(b + 1) * KT].unsqueeze(2).broadcast_to([P, KT, F]), ALU.mult)\
                    .then_inc(s_hd, 1)
            dve.drain()
            dve.wait_ge(s_x3, 16 * EB)
            V.tensor_scalar(XD[:], HD[:], ALPHA, None, ALU.mult)
            dve.drain()
            c.a, c.b, c.norm = A_N, B_N, NORM_N
            c.e += DC
            with dve.Fori(0, STEPS // 2) as r:
                summed = 0

                def appnp_tile(i, t):
                    def leave(t):
                        V.scalar_tensor_tensor(out=HD[:, t, :], in0=PS[t % 2][0:P, 0:F], scalar=asc[:, t:t + 1],
                                               in1=XD[:, t, :], op0=ALU.mult, op1=ALU.add).then_inc(s_left, 1)

                    m = M[:, t % SLOTS, 0:F]
                    dve.wait_ge(s_g[t % SLOTS], r * (2 * 16 * (T // SLOTS)) + landed(4 + i, t))
                    if t == 0:
                        V.tensor_scalar(m, m, 1.0, None, ALU.mult).then_inc(s_msg, 1)
                    else:
                        dve.wait_ge(s_seg, r * (2 * T) + seg(6 + i, t))
                        V.scalar_tensor_tensor(out=m, in0=PS[(t - 1) % 2][0:P, 0:F], scalar=carry[:, t:t + 1], in1=m,
                                               op0=ALU.mult, op1=ALU.add).then_inc(s_msg, 1)
                        leave(t - 1)
                    if t == T - 1:
                        dve.wait_ge(s_seg, r * (2 * T) + (seg(6 + i, t) + 1))
                        leave(t)

                def sums(n):
                    nonlocal summed
                    for u in range(summed, n):
                        appnp_tile(u // T, u % T)
                    summed = max(n, summed)

                steps(Fixed(r, False, PRE), "N", range(2), None, 0, sums)
                sums(2 * T)
            for t in range(T):
                if t % KT == 0:
                    dve.wait_ge(s_x3l[t // KT], 16)
                last = V.scalar_tensor_tensor(out=HD[:, t, :], in0=HD[:, t, :], scalar=sqd[:, t:t + 1], in1=XD[:, t, :],
                                              op0=ALU.mult, op1=ALU.add)
                if t % KT == KT - 1:
                    last.then_inc(s_res, 1)


def kernel(**inputs):
    import numpy as np
    import concourse.bacc as bacc
    from concourse.bass_utils import run_bass_kernel_spmd as run

    a = {k: np.asarray(v) for k, v in inputs.items()}

    def tiles(v):
        v = v.reshape((T, P) + v.shape[1:]).copy()
        v[1::2] = v[1::2, ::-1]
        return np.ascontiguousarray(np.swapaxes(v, 0, 1))

    src, dst = a["src"], a["dst"]
    no = np.full(1, -1, dst.dtype)
    nxt, prv = np.concatenate([dst[1:], no]), np.concatenate([no, dst[:-1]])
    wts = np.zeros((128, WCOLS), np.float32)

    def put(name, m, b=None):
        wts[0:m.shape[0], WC[name]:WC[name] + F] = m
        if b is not None:
            wts[F, WC[name]:WC[name] + F] = b

    put("W1", a["L0_gnn_W1"])
    put("W2", a["L0_gnn_W2"], a["L0_gnn_b2"])
    put("WR1", a["L1_gnn_W1r"].T)
    put("WL1", a["L1_gnn_W1l"].T)
    put("WR2", a["L1_gnn_W2r"].T, a["L1_gnn_b2"])
    put("WL2", a["L1_gnn_W2l"].T)
    put("MW1", a["L2_gnn_mW1"])
    put("MW2", a["L2_gnn_mW2"], a["L2_gnn_mb2"])
    put("GW1", a["L2_gnn_gW1"])
    put("UA", a["L2_gnn_uW1"][:F])
    put("UB", a["L2_gnn_uW1"][F:])
    put("UW2", a["L2_gnn_uW2"], a["L2_gnn_ub2"])
    wts[0:F, GW2], wts[F, GW2] = a["L2_gnn_gW2"][:, 0], a["L2_gnn_gb2"][0]
    for n, k in (("b1", "L0_gnn_b1"), ("s1", "L1_gnn_b1"), ("mb", "L2_gnn_mb1"), ("gb", "L2_gnn_gb1"),
                 ("ub", "L2_gnn_ub1")):
        wts[0:F, BC[n]] = a[k]
    first = np.zeros((P, T), np.float32)
    first[0, 0::2] = 1
    first[P - 1, 1::2] = 1
    place = np.stack([first, np.arange(1, NE + 1, dtype=np.float32).reshape(P, T)], 1)
    arrays = {
        "x": a["x"],
        "edges": np.stack([tiles(v) for v in (src, dst, nxt, prv)]),
        "ew": np.stack([np.ones((P, T), np.float32), tiles(a["edge_weight"])], 2),
        "dst_rows": np.ascontiguousarray(tiles(dst).T).reshape(-1),
        "attr": tiles(a["edge_attr_32"]),
        "wts": wts,
        "lnp": np.concatenate([a["L2_gnn_ln_g"], a["L2_gnn_ln_b"]]),
        "ident": np.eye(P, dtype=np.float32),
        "place": np.ascontiguousarray(place),
    }
    nc = bacc.Bacc("TRN2", target_bir_lowering=False, num_devices=1)
    args = [nc.dram_tensor(f"in_{k}", v.shape, mybir.dt.from_np(v.dtype), kind="ExternalInput").ap()
            for k, v in arrays.items()]
    args.append(nc.dram_tensor("out", (NN, F), F32, kind="ExternalOutput").ap())
    gnn_kernel(nc, *args)
    r = run(nc, [{f"in_{k}": v for k, v in arrays.items()}], core_ids=[0])
    return r.results[0]["out"]
```
